# Optimizing a Trainium2 kernel written in Bass

```python
import numpy as np
import jax
import jax.numpy as jnp

def _softmax(x, axis=-1):
    return jax.nn.softmax(x, axis=axis)

def _gelu(x):
    return jax.nn.gelu(x, approximate=True)

def _silu(x):
    return jax.nn.silu(x)

def _sigmoid(x):
    return jax.nn.sigmoid(x)

def _layernorm(x, axis=-1, eps=1e-05):
    m = jnp.mean(x, axis=axis, keepdims=True)
    v = jnp.var(x, axis=axis, keepdims=True)
    return (x - m) / jnp.sqrt(v + eps)

def _scatter_add(tgt, idx, src, axis=0):
    return tgt.at[idx].add(src)

def _segment_sum(src, seg, n):
    return jax.ops.segment_sum(src, seg, n)
kernel_name = 'mk_decoder_postln_d2_seqx_r8_eaca1f'

def setup_inputs(seed: int=0):
    np.random.seed(seed)
    _w = jnp.asarray

    def _rec_inputs():
        import jax
        import jax.numpy as jnp
        _rk = jax.random.key(seed)
        x = -0.0002928 + 1 * jax.random.normal(jax.random.fold_in(_rk, 1), (32, 56, 256), jnp.float32)
        _lenS = 56 - jax.random.randint(jax.random.fold_in(_rk, 7), (32,), 0, max(1, 56 // 4) + 1, jnp.int32)
        _lenS2 = 1500 - jax.random.randint(jax.random.fold_in(_rk, 8), (32,), 0, max(1, 1500 // 4) + 1, jnp.int32)
        _ctx_512P = jax.random.normal(jax.random.fold_in(_rk, 11), (32, 16, 64), jnp.float32)
        _ctx_512c = jax.random.dirichlet(jax.random.fold_in(_rk, 511), 0.3 * jnp.ones((16,), jnp.float32), (32, 1500))
        _ctx_512t = jnp.einsum('bsk,bkd->bsd', _ctx_512c, _ctx_512P)
        _ctx_512t = _ctx_512t * jax.lax.rsqrt(jnp.mean(jnp.square(_ctx_512t)) + 1e-12) * 0.953939
        ctx_512 = 0.000227908 + 0.99994 * (_ctx_512t + 0.3 * jax.random.normal(jax.random.fold_in(_rk, 611), (32, 1500, 64), jnp.float32))
        return (x, ctx_512)
    x, ctx_512 = _rec_inputs()

    def _L0_attn_setup():
        import jax, jax.numpy as jnp
        import numpy as np
        D_STATE = 16
        DT_RANK = 6
        EPS = 1e-05

        def layer_norm(x, w, b):
            mu = jnp.mean(x, axis=-1, keepdims=True)
            var = jnp.mean((x - mu) ** 2, axis=-1, keepdims=True)
            return (x - mu) * jax.lax.rsqrt(var + EPS) * w + b

        def selective_scan(u, delta, A, Bp, Cp, Dp):
            delta_A = jnp.exp(jnp.einsum('bld,dn->bldn', delta, A))
            delta_B_u = jnp.einsum('bld,bln,bld->bldn', delta, Bp, u)
            Bsz, L, D = u.shape

            def step(x, inp):
                dA_t, dBu_t, C_t = inp
                x = dA_t * x + dBu_t
                y = jnp.einsum('bdn,bn->bd', x, C_t)
                return (x, y)
            x0 = jnp.zeros((Bsz, D, D_STATE), dtype=u.dtype)
            xs = (jnp.swapaxes(delta_A, 0, 1), jnp.swapaxes(delta_B_u, 0, 1), jnp.swapaxes(Cp, 0, 1))
            _, ys = jax.lax.scan(step, x0, xs)
            y = jnp.swapaxes(ys, 0, 1)
            return y + u * Dp

        def ssm(x, x_proj_W, dt_proj_W, dt_proj_b, A_log, D_param):
            A = -jnp.exp(A_log.astype(jnp.float32))
            dbc = x @ x_proj_W.T
            delta_r = dbc[..., :DT_RANK]
            Bp = dbc[..., DT_RANK:DT_RANK + D_STATE]
            Cp = dbc[..., DT_RANK + D_STATE:]
            delta = jax.nn.softplus(delta_r @ dt_proj_W.T + dt_proj_b) * 0.001
            return selective_scan(x, delta, A, Bp, Cp, D_param.astype(jnp.float32))
        key = jax.random.key(seed)
        ks = jax.random.split(key, 10)
        B, L, C, Din = (16, 256, 256, 96)
        A = jnp.tile(jnp.arange(1, D_STATE + 1, dtype=jnp.float32)[None, :], (Din, 1))
        return {'feat_patch': jax.random.normal(ks[0], (B, L, C), dtype=jnp.float32), 'ln_w': jnp.ones((C,), jnp.float32), 'ln_b': jnp.zeros((C,), jnp.float32), 'in_proj_W': jax.random.normal(ks[1], (Din, C), jnp.float32) * (1.0 / np.sqrt(C)), 'conv_w': jax.random.normal(ks[2], (Din, 1, 3), jnp.float32) * 0.3, 'conv_b': jnp.zeros((Din,), jnp.float32), 'x_proj_W': jax.random.normal(ks[3], (DT_RANK + 2 * D_STATE, Din), jnp.float32) * (1.0 / np.sqrt(Din)), 'dt_proj_W': jax.random.normal(ks[4], (Din, DT_RANK), jnp.float32) * (1.0 / np.sqrt(DT_RANK)), 'dt_proj_b': jnp.zeros((Din,), jnp.float32), 'A_log': jnp.log(A), 'D_param': jnp.ones((Din,), jnp.float32), 'out_proj_W': jax.random.normal(ks[5], (C, Din), jnp.float32) * (1.0 / np.sqrt(Din))}
    _L0_attn_all = _L0_attn_setup()
    _L0_attn_in = {k: v for k, v in _L0_attn_all.items() if k in ('ln_w', 'ln_b', 'in_proj_W', 'conv_w', 'conv_b', 'x_proj_W', 'dt_proj_W', 'dt_proj_b', 'A_log', 'D_param', 'out_proj_W')}
    del _L0_attn_all

    def _L0_xattn_setup():
        import jax, jax.numpy as jnp
        import numpy as np
        B, S, L = (2, 128, 128)
        DIM_Q, H, K, D_C, D_CQ, R = (256, 16, 128, 64, 192, 64)

        def _rope_tables(length, dim):
            inv = 1.0 / 10000.0 ** (jnp.arange(0, dim, 2, dtype=jnp.float32) / dim)
            f = jnp.arange(length, dtype=jnp.float32)[:, None] * inv[None, :]
            sin = jnp.repeat(jnp.sin(f), 2, axis=-1)
            cos = jnp.repeat(jnp.cos(f), 2, axis=-1)
            return (sin, cos)

        def _rotate_half(x):
            half = x.shape[-1] // 2
            return jnp.concatenate([-x[..., half:], x[..., :half]], axis=-1)

        def _apply_rope(x, sin, cos):
            return x * cos + _rotate_half(x) * sin
        key = jax.random.key(seed)
        ks = jax.random.split(key, 8)
        return {'hidden_q': jax.random.normal(ks[0], (B, S, DIM_Q), jnp.float32), 'kv_c': jax.random.normal(ks[1], (B, L, D_C), jnp.float32), 'Wq': jax.random.normal(ks[2], (H * K, DIM_Q), jnp.float32) / np.sqrt(DIM_Q).astype(np.float32), 'w_kc_q': jax.random.normal(ks[3], (H, K, D_CQ), jnp.float32) / np.sqrt(K).astype(np.float32), 'w_kc_kv': jax.random.normal(ks[4], (H, K, D_C), jnp.float32) / np.sqrt(K).astype(np.float32), 'W_qr': jax.random.normal(ks[5], (H, D_CQ, R), jnp.float32) / np.float32(np.sqrt(D_CQ) * np.sqrt(R)), 'W_kr': jax.random.normal(ks[6], (H, D_C, R), jnp.float32) / np.sqrt(D_C).astype(np.float32), 'Wo': jax.random.normal(ks[7], (DIM_Q, H * K), jnp.float32) / np.sqrt(H * K).astype(np.float32)}
    _L0_xattn_all = _L0_xattn_setup()
    _L0_xattn_in = {k: v for k, v in _L0_xattn_all.items() if k in ('Wq', 'w_kc_q', 'w_kc_kv', 'W_qr', 'W_kr', 'Wo')}
    del _L0_xattn_all

    def _L0_ffn_setup():
        import jax, jax.numpy as jnp
        import numpy as np
        HIDDEN = 256
        INTER = 704
        B, S = (2, 256)

        def _ternary(key, shape):
            return jax.random.randint(key, shape, -1, 2).astype(jnp.float32)
        key = jax.random.key(seed)
        ks = jax.random.split(key, 7)
        x = jax.random.normal(ks[0], (B, S, HIDDEN), dtype=jnp.float32)
        gate_w = _ternary(ks[1], (INTER, HIDDEN))
        up_w = _ternary(ks[2], (INTER, HIDDEN))
        down_w = _ternary(ks[3], (HIDDEN, INTER))
        gate_s = jax.random.uniform(ks[4], (INTER,), minval=0.01, maxval=0.1, dtype=jnp.float32)
        up_s = jax.random.uniform(ks[5], (INTER,), minval=0.01, maxval=0.1, dtype=jnp.float32)
        down_s = jax.random.uniform(ks[6], (HIDDEN,), minval=0.01, maxval=0.1, dtype=jnp.float32)
        return {'x': x, 'gate_w': gate_w, 'up_w': up_w, 'down_w': down_w, 'gate_s': gate_s, 'up_s': up_s, 'down_s': down_s}
    _L0_ffn_all = _L0_ffn_setup()
    _L0_ffn_in = {k: v for k, v in _L0_ffn_all.items() if k in ('gate_w', 'up_w', 'down_w', 'gate_s', 'up_s', 'down_s')}
    del _L0_ffn_all

    def _L1_attn_setup():
        import jax, jax.numpy as jnp
        import numpy as np
        H = 16

        def _split_heads(x, h):
            B, T, D = x.shape
            return x.reshape(B, T, h, D // h).transpose(0, 2, 1, 3)
        key = jax.random.key(seed)
        ks = jax.random.split(key, 7)
        B, T, D = (2, 256, 256)
        s = 0.02
        return {'x': jax.random.normal(ks[0], (B, T, D), dtype=jnp.float32), 'Wq1': jax.random.normal(ks[1], (D, D), dtype=jnp.float32) * s, 'Wq2': jax.random.normal(ks[2], (D, D), dtype=jnp.float32) * s, 'Wk': jax.random.normal(ks[3], (D, D), dtype=jnp.float32) * s, 'Wv': jax.random.normal(ks[4], (D, D), dtype=jnp.float32) * s, 'Wlam': jax.random.normal(ks[5], (D, H), dtype=jnp.float32) * s, 'Wo': jax.random.normal(ks[6], (D, D), dtype=jnp.float32) * s}
    _L1_attn_all = _L1_attn_setup()
    _L1_attn_in = {k: v for k, v in _L1_attn_all.items() if k in ('Wq1', 'Wq2', 'Wk', 'Wv', 'Wlam', 'Wo')}
    del _L1_attn_all

    def _L1_xattn_setup():
        import jax, jax.numpy as jnp
        import numpy as np
        B, S, H, NH, L = (2, 256, 256, 16, 64)
        HD = H // NH
        key = jax.random.key(seed)
        k1, k2, k3, k4, k5 = jax.random.split(key, 5)
        scale = 0.02
        return {'q': jax.random.normal(k1, (B, S, H), dtype=jnp.float32), 'latent_kv': jax.random.normal(k2, (B, S, L), dtype=jnp.float32), 'Wq': jax.random.normal(k3, (H, H), dtype=jnp.float32) * scale, 'Wkv_expand': jax.random.normal(k4, (2 * H, L), dtype=jnp.float32) * scale, 'Wout': jax.random.normal(k5, (H, H), dtype=jnp.float32) * scale}
    _L1_xattn_all = _L1_xattn_setup()
    _L1_xattn_in = {k: v for k, v in _L1_xattn_all.items() if k in ('Wq', 'Wkv_expand', 'Wout')}
    del _L1_xattn_all

    def _L1_ffn_setup():
        import jax, jax.numpy as jnp
        import numpy as np
        B, S, H = (2, 256, 256)
        E, G, TKG, K = (32, 8, 4, 8)
        I, SI = (128, 256)
        ROUTED_SCALE = 2.5

        def _moe_forward(hidden_states, router_w, router_bias, w_gate, w_up, w_down, sw_gate, sw_up, sw_down):
            x = hidden_states.reshape(-1, H)
            T = x.shape[0]
            logits = x.astype(jnp.float32) @ router_w.astype(jnp.float32)
            scores = jax.nn.sigmoid(logits)
            scores_grouped = (scores + router_bias).reshape(T, G, E // G)
            top2, _ = jax.lax.top_k(scores_grouped, 2)
            group_scores = top2.sum(-1)
            _, top_groups = jax.lax.top_k(group_scores, TKG)
            mask = jnp.ones((T, G), bool).at[jnp.arange(T)[:, None], top_groups].set(False)
            masked = jnp.where(mask[:, :, None], 0.0, scores_grouped).reshape(T, E)
            _, top_k_index = jax.lax.top_k(masked, K)
            tkw = jnp.take_along_axis(scores, top_k_index, axis=-1)
            tkw = tkw / tkw.sum(-1, keepdims=True)
            tkw = (tkw * ROUTED_SCALE).astype(hidden_states.dtype)
            flat_idx = top_k_index.reshape(-1)
            sort_idx = jnp.argsort(flat_idx)
            xs = jnp.repeat(x, K, axis=0)[sort_idx]
            group_sizes = jnp.bincount(flat_idx, length=E).astype(jnp.int32)
            gate = jax.lax.ragged_dot(xs, w_gate, group_sizes)
            up = jax.lax.ragged_dot(xs, w_up, group_sizes)
            down = jax.lax.ragged_dot(jax.nn.silu(gate) * up, w_down, group_sizes)
            unsort = jnp.argsort(sort_idx)
            routed = (down[unsort].reshape(T, K, H) * tkw[..., None]).sum(axis=1)
            shared = jax.nn.silu(x @ sw_gate) * (x @ sw_up) @ sw_down
            return (routed + shared).reshape(hidden_states.shape)
        key = jax.random.key(seed)
        ks = jax.random.split(key, 9)

        def w(k, shape, fan_in):
            return jax.random.normal(k, shape, jnp.float32) / np.float32(np.sqrt(fan_in))
        return dict(hidden_states=jax.random.normal(ks[0], (B, S, H), jnp.float32), router_w=w(ks[1], (H, E), H), router_bias=jnp.zeros((E,), jnp.float32), w_gate=w(ks[2], (E, H, I), H), w_up=w(ks[3], (E, H, I), H), w_down=w(ks[4], (E, I, H), I), sw_gate=w(ks[5], (H, SI), H), sw_up=w(ks[6], (H, SI), H), sw_down=w(ks[7], (SI, H), SI))
    _L1_ffn_all = _L1_ffn_setup()
    _L1_ffn_in = {k: v for k, v in _L1_ffn_all.items() if k in ('router_w', 'router_bias', 'w_gate', 'w_up', 'w_down', 'sw_gate', 'sw_up', 'sw_down')}
    del _L1_ffn_all
    return {'x': x, 'ctx_512': ctx_512, 'L0_attn_ln_w': _L0_attn_in['ln_w'], 'L0_attn_ln_b': _L0_attn_in['ln_b'], 'L0_attn_in_proj_W': _L0_attn_in['in_proj_W'], 'L0_attn_conv_w': _L0_attn_in['conv_w'], 'L0_attn_conv_b': _L0_attn_in['conv_b'], 'L0_attn_x_proj_W': _L0_attn_in['x_proj_W'], 'L0_attn_dt_proj_W': _L0_attn_in['dt_proj_W'], 'L0_attn_dt_proj_b': _L0_attn_in['dt_proj_b'], 'L0_attn_A_log': _L0_attn_in['A_log'], 'L0_attn_D_param': _L0_attn_in['D_param'], 'L0_attn_out_proj_W': _L0_attn_in['out_proj_W'], 'L0_xattn_Wq': _L0_xattn_in['Wq'], 'L0_xattn_w_kc_q': _L0_xattn_in['w_kc_q'], 'L0_xattn_w_kc_kv': _L0_xattn_in['w_kc_kv'], 'L0_xattn_W_qr': _L0_xattn_in['W_qr'], 'L0_xattn_W_kr': _L0_xattn_in['W_kr'], 'L0_xattn_Wo': _L0_xattn_in['Wo'], 'L0_ffn_gate_w': _L0_ffn_in['gate_w'], 'L0_ffn_up_w': _L0_ffn_in['up_w'], 'L0_ffn_down_w': _L0_ffn_in['down_w'], 'L0_ffn_gate_s': _L0_ffn_in['gate_s'], 'L0_ffn_up_s': _L0_ffn_in['up_s'], 'L0_ffn_down_s': _L0_ffn_in['down_s'], 'L1_attn_Wq1': _L1_attn_in['Wq1'], 'L1_attn_Wq2': _L1_attn_in['Wq2'], 'L1_attn_Wk': _L1_attn_in['Wk'], 'L1_attn_Wv': _L1_attn_in['Wv'], 'L1_attn_Wlam': _L1_attn_in['Wlam'], 'L1_attn_Wo': _L1_attn_in['Wo'], 'L1_xattn_Wq': _L1_xattn_in['Wq'], 'L1_xattn_Wkv_expand': _L1_xattn_in['Wkv_expand'], 'L1_xattn_Wout': _L1_xattn_in['Wout'], 'L1_ffn_router_w': _L1_ffn_in['router_w'], 'L1_ffn_router_bias': _L1_ffn_in['router_bias'], 'L1_ffn_w_gate': _L1_ffn_in['w_gate'], 'L1_ffn_w_up': _L1_ffn_in['w_up'], 'L1_ffn_w_down': _L1_ffn_in['w_down'], 'L1_ffn_sw_gate': _L1_ffn_in['sw_gate'], 'L1_ffn_sw_up': _L1_ffn_in['sw_up'], 'L1_ffn_sw_down': _L1_ffn_in['sw_down']}

def reference(x, ctx_512, L0_attn_ln_w, L0_attn_ln_b, L0_attn_in_proj_W, L0_attn_conv_w, L0_attn_conv_b, L0_attn_x_proj_W, L0_attn_dt_proj_W, L0_attn_dt_proj_b, L0_attn_A_log, L0_attn_D_param, L0_attn_out_proj_W, L0_xattn_Wq, L0_xattn_w_kc_q, L0_xattn_w_kc_kv, L0_xattn_W_qr, L0_xattn_W_kr, L0_xattn_Wo, L0_ffn_gate_w, L0_ffn_up_w, L0_ffn_down_w, L0_ffn_gate_s, L0_ffn_up_s, L0_ffn_down_s, L1_attn_Wq1, L1_attn_Wq2, L1_attn_Wk, L1_attn_Wv, L1_attn_Wlam, L1_attn_Wo, L1_xattn_Wq, L1_xattn_Wkv_expand, L1_xattn_Wout, L1_ffn_router_w, L1_ffn_router_bias, L1_ffn_w_gate, L1_ffn_w_up, L1_ffn_w_down, L1_ffn_sw_gate, L1_ffn_sw_up, L1_ffn_sw_down):
    import jax
    import jax.numpy as jnp

    def _L0_attn_ref(feat_patch, ln_w, ln_b, in_proj_W, conv_w, conv_b, x_proj_W, dt_proj_W, dt_proj_b, A_log, D_param, out_proj_W):
        import jax, jax.numpy as jnp
        import numpy as np
        D_STATE = 16
        DT_RANK = 6
        EPS = 1e-05

        def layer_norm(x, w, b):
            mu = jnp.mean(x, axis=-1, keepdims=True)
            var = jnp.mean((x - mu) ** 2, axis=-1, keepdims=True)
            return (x - mu) * jax.lax.rsqrt(var + EPS) * w + b

        def selective_scan(u, delta, A, Bp, Cp, Dp):
            delta_A = jnp.exp(jnp.einsum('bld,dn->bldn', delta, A))
            delta_B_u = jnp.einsum('bld,bln,bld->bldn', delta, Bp, u)
            Bsz, L, D = u.shape

            def step(x, inp):
                dA_t, dBu_t, C_t = inp
                x = dA_t * x + dBu_t
                y = jnp.einsum('bdn,bn->bd', x, C_t)
                return (x, y)
            x0 = jnp.zeros((Bsz, D, D_STATE), dtype=u.dtype)
            xs = (jnp.swapaxes(delta_A, 0, 1), jnp.swapaxes(delta_B_u, 0, 1), jnp.swapaxes(Cp, 0, 1))
            _, ys = jax.lax.scan(step, x0, xs)
            y = jnp.swapaxes(ys, 0, 1)
            return y + u * Dp

        def ssm(x, x_proj_W, dt_proj_W, dt_proj_b, A_log, D_param):
            A = -jnp.exp(A_log.astype(jnp.float32))
            dbc = x @ x_proj_W.T
            delta_r = dbc[..., :DT_RANK]
            Bp = dbc[..., DT_RANK:DT_RANK + D_STATE]
            Cp = dbc[..., DT_RANK + D_STATE:]
            delta = jax.nn.softplus(delta_r @ dt_proj_W.T + dt_proj_b) * 0.001
            return selective_scan(x, delta, A, Bp, Cp, D_param.astype(jnp.float32))
        residual = feat_patch
        x = layer_norm(feat_patch, ln_w, ln_b)
        x = x @ in_proj_W.T
        x_ncl = jnp.swapaxes(x, 1, 2)
        x_ncl = jax.lax.conv_general_dilated(x_ncl, conv_w, window_strides=(1,), padding=((1, 1),), dimension_numbers=('NCH', 'OIH', 'NCH'), feature_group_count=96)
        x_ncl = x_ncl + conv_b[None, :, None]
        x = jnp.swapaxes(x_ncl, 1, 2)
        x = jax.nn.silu(x)
        y = ssm(x, x_proj_W, dt_proj_W, dt_proj_b, A_log, D_param)
        out = y @ out_proj_W.T
        return out + residual

    def _L0_xattn_ref(hidden_q, kv_c, Wq, w_kc_q, w_kc_kv, W_qr, W_kr, Wo):
        import jax, jax.numpy as jnp
        import numpy as np
        B, S, L = (2, 128, 128)
        DIM_Q, H, K, D_C, D_CQ, R = (256, 16, 128, 64, 192, 64)

        def _rope_tables(length, dim):
            inv = 1.0 / 10000.0 ** (jnp.arange(0, dim, 2, dtype=jnp.float32) / dim)
            f = jnp.arange(length, dtype=jnp.float32)[:, None] * inv[None, :]
            sin = jnp.repeat(jnp.sin(f), 2, axis=-1)
            cos = jnp.repeat(jnp.cos(f), 2, axis=-1)
            return (sin, cos)

        def _rotate_half(x):
            half = x.shape[-1] // 2
            return jnp.concatenate([-x[..., half:], x[..., :half]], axis=-1)

        def _apply_rope(x, sin, cos):
            return x * cos + _rotate_half(x) * sin
        Bv, Sv, _ = hidden_q.shape
        _, Lv, _ = kv_c.shape
        q_hk = (hidden_q @ Wq.T).reshape(Bv, Sv, H, K)
        q_big = jnp.einsum('bshk,hkq->bshq', q_hk, w_kc_q)
        sin_q, cos_q = _rope_tables(Sv, D_CQ)
        q_big = _apply_rope(q_big, sin_q[None, :, None, :], cos_q[None, :, None, :])
        sin_k, cos_k = _rope_tables(Lv, D_C)
        kv_r = _apply_rope(kv_c, sin_k[None], cos_k[None])
        q_r = jnp.einsum('bshq,hqr->bhsr', q_big, W_qr)
        k_r = jnp.einsum('bld,hdr->bhlr', kv_r, W_kr)
        scores = jnp.einsum('bhsr,bhlr->bhsl', q_r, k_r)
        attn = jax.nn.softmax(scores, axis=-1)
        ctx_c = jnp.einsum('bhsl,bld->bhsd', attn, kv_r)
        ctx_lat = jnp.einsum('bhsd,hkd->bhsk', ctx_c, w_kc_kv)
        ctx = ctx_lat.transpose(0, 2, 1, 3).reshape(Bv, Sv, H * K)
        return ctx @ Wo.T

    def _L0_ffn_ref(x, gate_w, up_w, down_w, gate_s, up_s, down_s):
        import jax, jax.numpy as jnp
        import numpy as np
        HIDDEN = 256
        INTER = 704
        B, S = (2, 256)

        def _ternary(key, shape):
            return jax.random.randint(key, shape, -1, 2).astype(jnp.float32)
        b, s, h = x.shape
        xf = x.reshape(b * s, h)
        g = jnp.einsum('th,ih->ti', xf, gate_w) * gate_s
        u = jnp.einsum('th,ih->ti', xf, up_w) * up_s
        hdn = jax.nn.silu(g) * u
        out = jnp.einsum('ti,hi->th', hdn, down_w) * down_s
        return out.reshape(b, s, -1)

    def _L1_attn_ref(x, Wq1, Wq2, Wk, Wv, Wlam, Wo):
        import jax, jax.numpy as jnp
        import numpy as np
        H = 16

        def _split_heads(x, h):
            B, T, D = x.shape
            return x.reshape(B, T, h, D // h).transpose(0, 2, 1, 3)
        B, T, D = x.shape
        d = D // H
        q1 = _split_heads(x @ Wq1, H)
        q2 = _split_heads(x @ Wq2, H)
        k = _split_heads(x @ Wk, H)
        v = _split_heads(x @ Wv, H)
        q = jnp.concatenate([q1, q2], axis=1)
        k2 = jnp.repeat(k, 2, axis=1)
        v2 = jnp.repeat(v, 2, axis=1)
        scale = 1.0 / jnp.sqrt(jnp.asarray(d, dtype=x.dtype))
        scores = jnp.einsum('bhqd,bhkd->bhqk', q, k2) * scale
        causal = jnp.tril(jnp.ones((T, T), dtype=bool))
        scores = jnp.where(causal, scores, jnp.finfo(scores.dtype).min)
        p = jax.nn.softmax(scores, axis=-1)
        y = jnp.einsum('bhqk,bhkd->bhqd', p, v2)
        y1, y2 = (y[:, :H], y[:, H:])
        lam = jax.nn.sigmoid(x @ Wlam).transpose(0, 2, 1)[..., None]
        y = y1 - lam * y2
        y = y.transpose(0, 2, 1, 3).reshape(B, T, D)
        return y @ Wo

    def _L1_xattn_ref(q, latent_kv, Wq, Wkv_expand, Wout):
        import jax, jax.numpy as jnp
        import numpy as np
        B, S, H, NH, L = (2, 256, 256, 16, 64)
        HD = H // NH
        b, sq, _ = q.shape
        sk = latent_kv.shape[1]
        qp = q @ Wq.T
        kv = latent_kv @ Wkv_expand.T
        k, v = jnp.split(kv, 2, axis=-1)
        qh = qp.reshape(b, sq, NH, HD).transpose(0, 2, 1, 3)
        kh = k.reshape(b, sk, NH, HD).transpose(0, 2, 1, 3)
        vh = v.reshape(b, sk, NH, HD).transpose(0, 2, 1, 3)
        inv_sqrt_d = 1.0 / jnp.sqrt(jnp.float32(HD))
        scores = jnp.einsum('bhqd,bhkd->bhqk', qh, kh) * inv_sqrt_d
        causal = jnp.tril(jnp.ones((sq, sk), dtype=bool))
        scores = jnp.where(causal, scores, jnp.finfo(scores.dtype).min)
        attn = jax.nn.softmax(scores, axis=-1)
        out = jnp.einsum('bhqk,bhkd->bhqd', attn, vh)
        out = out.transpose(0, 2, 1, 3).reshape(b, sq, H)
        return out @ Wout.T

    def _L1_ffn_ref(hidden_states, router_w, router_bias, w_gate, w_up, w_down, sw_gate, sw_up, sw_down):
        import jax, jax.numpy as jnp
        import numpy as np
        B, S, H = (2, 256, 256)
        E, G, TKG, K = (32, 8, 4, 8)
        I, SI = (128, 256)
        ROUTED_SCALE = 2.5

        def _moe_forward(hidden_states, router_w, router_bias, w_gate, w_up, w_down, sw_gate, sw_up, sw_down):
            x = hidden_states.reshape(-1, H)
            T = x.shape[0]
            logits = x.astype(jnp.float32) @ router_w.astype(jnp.float32)
            scores = jax.nn.sigmoid(logits)
            scores_grouped = (scores + router_bias).reshape(T, G, E // G)
            top2, _ = jax.lax.top_k(scores_grouped, 2)
            group_scores = top2.sum(-1)
            _, top_groups = jax.lax.top_k(group_scores, TKG)
            mask = jnp.ones((T, G), bool).at[jnp.arange(T)[:, None], top_groups].set(False)
            masked = jnp.where(mask[:, :, None], 0.0, scores_grouped).reshape(T, E)
            _, top_k_index = jax.lax.top_k(masked, K)
            tkw = jnp.take_along_axis(scores, top_k_index, axis=-1)
            tkw = tkw / tkw.sum(-1, keepdims=True)
            tkw = (tkw * ROUTED_SCALE).astype(hidden_states.dtype)
            flat_idx = top_k_index.reshape(-1)
            sort_idx = jnp.argsort(flat_idx)
            xs = jnp.repeat(x, K, axis=0)[sort_idx]
            group_sizes = jnp.bincount(flat_idx, length=E).astype(jnp.int32)
            gate = jax.lax.ragged_dot(xs, w_gate, group_sizes)
            up = jax.lax.ragged_dot(xs, w_up, group_sizes)
            down = jax.lax.ragged_dot(jax.nn.silu(gate) * up, w_down, group_sizes)
            unsort = jnp.argsort(sort_idx)
            routed = (down[unsort].reshape(T, K, H) * tkw[..., None]).sum(axis=1)
            shared = jax.nn.silu(x @ sw_gate) * (x @ sw_up) @ sw_down
            return (routed + shared).reshape(hidden_states.shape)
        return _moe_forward(hidden_states, router_w, router_bias, w_gate, w_up, w_down, sw_gate, sw_up, sw_down)
    x = _layernorm(x + _L0_attn_ref(x, L0_attn_ln_w, L0_attn_ln_b, L0_attn_in_proj_W, L0_attn_conv_w, L0_attn_conv_b, L0_attn_x_proj_W, L0_attn_dt_proj_W, L0_attn_dt_proj_b, L0_attn_A_log, L0_attn_D_param, L0_attn_out_proj_W), axis=-1)
    x = _layernorm(x + _L0_xattn_ref(x, ctx_512, L0_xattn_Wq, L0_xattn_w_kc_q, L0_xattn_w_kc_kv, L0_xattn_W_qr, L0_xattn_W_kr, L0_xattn_Wo), axis=-1)
    x = _layernorm(x + _L0_ffn_ref(x, L0_ffn_gate_w, L0_ffn_up_w, L0_ffn_down_w, L0_ffn_gate_s, L0_ffn_up_s, L0_ffn_down_s), axis=-1)
    x = _layernorm(x + _L1_attn_ref(x, L1_attn_Wq1, L1_attn_Wq2, L1_attn_Wk, L1_attn_Wv, L1_attn_Wlam, L1_attn_Wo), axis=-1)
    x = _layernorm(x + _L1_xattn_ref(x, ctx_512, L1_xattn_Wq, L1_xattn_Wkv_expand, L1_xattn_Wout), axis=-1)
    x = _layernorm(x + _L1_ffn_ref(x, L1_ffn_router_w, L1_ffn_router_bias, L1_ffn_w_gate, L1_ffn_w_up, L1_ffn_w_down, L1_ffn_sw_gate, L1_ffn_sw_up, L1_ffn_sw_down), axis=-1)
    return x

_drawn_inputs = setup_inputs


def setup_inputs(seed=0):
    import zlib

    import numpy as np

    out = dict(_drawn_inputs(seed))
    spreads = {'L0_attn_ln_w': (1.0, 0.2),
     'L0_attn_ln_b': (0.0, 0.1),
     'L0_attn_conv_b': (0.0, 0.1),
     'L0_attn_dt_proj_b': (0.0, 0.8),
     'L0_attn_D_param': (1.0, 0.2),
     'L1_ffn_router_bias': (0.0, 0.1)}
    factors = {'L0_attn_x_proj_W': 7.135,
     'L0_attn_dt_proj_W': 8.0,
     'L0_attn_A_log': 8.0,
     'L1_attn_Wq1': 4.096,
     'L1_attn_Wq2': 3.654,
     'L1_attn_Wk': 2.774,
     'L1_attn_Wlam': 2.902,
     'L1_xattn_Wq': 6.458}
    for name, (base, spread) in spreads.items():
        noise = np.random.default_rng([zlib.crc32(name.encode()), seed]).standard_normal(out[name].shape)
        drawn = base * np.exp(spread * noise) if base else spread * noise
        out[name] = jnp.asarray(drawn.astype(out[name].dtype))
    for name, factor in factors.items():
        out[name] = (out[name] * factor).astype(out[name].dtype)
    return out
```

```python
import numpy as np

import concourse.bass as bass
from concourse import mybir
from concourse.alu_op_type import AluOpType as ALU

F32 = mybir.dt.float32
BF16 = mybir.dt.bfloat16
ACT = mybir.ActivationFunctionType
AX = mybir.AxisListType

NSEQ, S, D = 32, 56, 256
T = NSEQ * S
TILE = 2 * S
NT = T // TILE
CHUNK = 8 * S
NCH = T // CHUNK
TPC = CHUNK // TILE
KD = D // 128
EPS = 1e-5

DI, NS, DTR, KW = 96, 16, 6, 3
H = 16
LK, DC, DCQ = 1500, 64, 192
KP, KC = 125, 12
HALFQ = DCQ // 2
NQ = H * S
INTER = 704
FB = 6
HD = D // H
NE, NEX, NG, TOPG, TOPK, IE = 32, 34, 8, 4, 8, 128
ROUTED_SCALE = 2.5
NEG = -1e30
ATANH = [2.00000001, 0.66666316, 0.40024854, 0.27961419, 0.28174657]


class Signal:

    def __init__(self, nc, name, credit=0):
        self.sem, self.credit = nc.alloc_semaphore(name), credit

    def at(self, count):
        return count + self.credit


class Chain:

    def __init__(self, nc, name):
        self.sem, self.base, self.n = nc.alloc_semaphore(name), 0, 0

    def one(self):
        self.n += 1
        return 1

    def all(self):
        return self.base + self.n

    def enter(self, i, per):
        self.start = self.base + self.n
        self.base, self.n, self.per = self.start + i * per, 0, per

    def leave(self, times):
        assert self.n == self.per, (self.n, self.per)
        self.base, self.n = self.start + times * self.per, 0


def build(nc, a, out, stages=6):
    cursor = [((nc.sbuf_base + 63) // 64) * 64]

    def sb(name, shape, dt=F32):
        size = int(np.prod(shape[1:])) * (2 if dt == BF16 else 4)
        size = (size + 63) // 64 * 64
        h = nc.alloc_sbuf_tensor_at(name, shape, dt, offset=cursor[0])
        cursor[0] += size
        return h

    def sig(name, credit=0):
        s = Signal(nc, name, credit)
        if credit:
            rings.append(s)
        return s

    rings = []
    ps = nc.alloc_psum_tensor("ps", [128, 8, 512], F32)

    x_tok = sb("x_tok", [TILE, NT, D])
    feat_base = cursor[0]
    x_feat = sb("x_feat", [128, KD, T])
    ident = sb("ident", [128, 128])
    ident_bf = sb("ident_bf", [TILE, TILE], BF16)
    xn = sb("xn", [TILE, 2, D])
    ln_stats = sb("ln_stats", [TILE, NT, 6])
    ln_a = sb("ln_a", [TILE, NT])
    ln_b = sb("ln_b", [TILE, NT])
    ln_d = sb("ln_d", [TILE, NT])
    ln_sq = sb("ln_sq", [TILE, NT])
    ln_mean = sb("ln_mean", [TILE, NT])
    ln_var = sb("ln_var", [TILE, NT])
    ln_std = sb("ln_std", [TILE, NT])
    ln_rstd = sb("ln_rstd", [TILE, NT])
    phase_base = cursor[0]

    m_lnw = sb("m_lnw", [128, KD])
    m_lnb = sb("m_lnb", [128, KD])
    m_in = sb("m_in", [128, KD, DI])
    m_cw = sb("m_cw", [DI, KW])
    m_cb = sb("m_cb", [DI, 1])
    m_xp = sb("m_xp", [DI, DTR + 2 * NS])
    m_dt = sb("m_dt", [DTR, DI])
    m_dtb = sb("m_dtb", [DI, 1])
    m_al = sb("m_al", [DI, NS])
    m_a = sb("m_a", [DI, NS])
    m_dp = sb("m_dp", [DI, 1])
    m_out = sb("m_out", [DI, D])
    m_pad = sb("m_pad", [DI, NSEQ, S + 2])
    m_c = sb("m_c", [DI, NSEQ, S])
    m_u = sb("m_u", [DI, T])
    m_t1 = sb("m_t1", [DI, T])
    m_t2 = sb("m_t2", [DI, T])
    m_delta = sb("m_delta", [DI, NSEQ, S])
    m_du = sb("m_du", [DI, T])
    m_ud = sb("m_ud", [DI, T])
    m_ud2 = sb("m_ud2", [DI, T])
    m_sq = sb("m_sq", [DI, T])
    m_dbc = sb("m_dbc", [DTR + 2 * NS, T])
    m_da = sb("m_da", [DI, 2, NSEQ, S])
    m_dbu = sb("m_dbu", [DI, 2, T])
    m_bb = sb("m_bb", [DI, 2, T])
    m_cc = sb("m_cc", [DI, 2, T])
    m_h = sb("m_h", [DI, 2, T])
    m_y = sb("m_y", [DI, 2, TILE])

    cursor[0] = phase_base
    q_all = sb("q_all", [DC, H, T])
    w3 = sb("w3", [128, H // 2, D])
    after_q = cursor[0]
    a_wq = sb("a_wq", [128, 2, D])
    a_wkq = sb("a_wkq", [128, 2, DCQ])
    a_wqr = sb("a_wqr", [64, 2, DCQ])
    a_wkr = sb("a_wkr", [64, 2, DC])
    a_wkv = sb("a_wkv", [128, 2, DC])
    a_wo = sb("a_wo", [128, 2, D])
    a_wf = sb("a_wf", [128, 2, KD, DCQ])
    a_w2 = sb("a_w2", [HALFQ, 2, 2, DC])
    a_rope = sb("a_rope", [HALFQ, 4, S])
    a_prod = sb("a_prod", [HALFQ, 2, 4, CHUNK])
    a_rot = sb("a_rot", [HALFQ, 2, 2, CHUNK])
    cursor[0] = after_q
    b_kv = sb("b_kv", [KP, 2, KC, DC])
    b_rope = sb("b_rope", [KP, 2, KC, DC])
    b_tmp = sb("b_tmp", [KP, KC, DC])
    b_kvr = sb("b_kvr", [KP, 2, KC, DC + 1])
    b_q = sb("b_q", [DC + 1, 2, NQ])
    b_pt = sb("b_pt", [KP, 3, NQ])
    b_mx3 = sb("b_mx3", [TILE, 2, H // 2, 3])
    b_mx = sb("b_mx", [TILE, 2, H // 2])
    b_rs = sb("b_rs", [TILE, 2, H // 2])
    b_ctx = sb("b_ctx", [TILE, 2, H // 2, DC])
    cursor[0] = feat_base
    b_kt = sb("b_kt", [DC + 1, 2, KC * KP])
    cursor[0] = after_q
    c_ctx = sb("c_ctx", [TILE, 2, H * DC])
    c_ctxT = sb("c_ctxT", [128, 2, H // 2, TILE])

    cursor[0] = after_q
    f_g = sb("f_g", [128, KD, INTER])
    f_u = sb("f_u", [128, KD, INTER])
    f_d = sb("f_d", [128, FB, D])
    f_gs = sb("f_gs", [128, FB])
    f_us = sb("f_us", [128, FB])
    f_ds = sb("f_ds", [TILE, D])
    f_act = sb("f_act", [128, 2, CHUNK])
    f_h = sb("f_h", [128, FB, CHUNK])
    f_y = sb("f_y", [TILE, 2, D])

    cursor[0] = phase_base
    n_w = sb("n_w", [128, 4, KD, D])
    n_lam = sb("n_lam", [128, KD, H])
    n_wo = sb("n_wo", [128, KD, D])
    z_wq = sb("z_wq", [128, KD, D])
    z_wkv = sb("z_wkv", [DC, 2 * D])
    z_wo = sb("z_wo", [128, KD, D])
    z_ctx = sb("z_ctx", [DC, T])
    n_hm = sb("n_hm", [128, 8])
    n_caus = sb("n_caus", [TILE, S])
    n_caus_bf = sb("n_caus_bf", [TILE, 8, S], BF16)
    n_xf = sb("n_xf", [128, 2, KD, TILE])
    n_kf = sb("n_kf", [128, 2, 2, TILE])
    n_qz = sb("n_qz", [128, 2, 4, 2, TILE])
    n_km = sb("n_km", [128, 2, 4, 8, S])
    n_v = sb("n_v", [S, 2, 2, H, 2 * HD])
    n_e = sb("n_e", [TILE, 2, 4 * CHUNK])
    n_mx = sb("n_mx", [TILE, 2, 32])
    n_sum = sb("n_sum", [TILE, 2, 32])
    n_r = sb("n_r", [TILE, 2, 32])
    n_l = sb("n_l", [TILE, 2, 16])
    n_l2 = sb("n_l2", [TILE, 2, 16])
    n_l3 = sb("n_l3", [TILE, 2, 16])
    n_pt = sb("n_pt", [S, 8, CHUNK])
    n_yt = sb("n_yt", [128, 2, 2, TILE])

    cursor[0] = phase_base
    r_w = sb("r_w", [128, KD, NE])
    r_b = sb("r_b", [TILE, NE])
    r_lt = sb("r_lt", [TILE, NG, NG])
    r_xf = sb("r_xf", [128, 2, KD, TILE])
    r_s = sb("r_s", [TILE, NT, NE])
    r_sb = sb("r_sb", [TILE, NT, NE])
    r_hi = sb("r_hi", [TILE, NT, NG, 2])
    r_lo = sb("r_lo", [TILE, NT, NG, 2])
    r_g1 = sb("r_g1", [TILE, NT, NG])
    r_g2 = sb("r_g2", [TILE, NT, NG])
    r_g3 = sb("r_g3", [TILE, NT, NG])
    r_c1 = sb("r_c1", [TILE, NT, NG, NG])
    r_c2 = sb("r_c2", [TILE, NT, NG, NG])
    r_top = sb("r_top", [TILE, NT, 8])
    r_m = sb("r_m", [TILE, NT, NE])
    r_m2 = sb("r_m2", [TILE, NT, NE])
    r_den = sb("r_den", [TILE, NT])
    r_rden = sb("r_rden", [TILE, NT])
    r_wt = sb("r_wt", [NEX, T])
    e_wgu = sb("e_wgu", [128, 2, 2 * D])
    e_wd = sb("e_wd", [128, 2, D])
    e_tw = sb("e_tw", [128, 2, CHUNK])
    e_act = sb("e_act", [128, 2, CHUNK])
    e_aw = sb("e_aw", [128, 2, CHUNK])
    e_h = sb("e_h", [128, 2, CHUNK])
    e_z = sb("e_z", [1, CHUNK])
    e_y = sb("e_y", [128, 2, CHUNK])

    bc_dram = nc.dram_tensor("bc_rows", (2 * NS, T), F32, kind="Internal").ap()
    ctx_dram = nc.dram_tensor("ctx_rows", (T, H, DC), F32, kind="Internal").ap()
    rw_dram = nc.dram_tensor("route_rows", (NEX, T), F32, kind="Internal").ap()

    x_ld = sig("x_ld")
    tail_rdy = sig("tail_rdy", 2)
    tail_used = sig("tail_used", 2)
    ln_st = sig("ln_st")
    std_req, std_rdy = sig("std_req"), sig("std_rdy")
    xn_rdy = sig("xn_rdy")
    xt_mm = sig("xt_mm", 2)
    xcp = sig("xcp", 2)
    xt_rdy = sig("xt_rdy", 2)
    w_ld = [sig(f"w_ld{k}") for k in range(6)]
    c_ld = sig("c_ld")

    m_ev, m_mm = sig("m_ev"), sig("m_mm")
    m_padz, m_convd, m_exp, m_silu, m_abs, m_ln, m_dl = (sig(n) for n in (
        "m_padz", "m_convd", "m_exp", "m_silu", "m_abs", "m_ln", "m_dl"))
    m_dbc_ev, m_bc_st = sig("m_dbc_ev"), sig("m_bc_st")
    m_bld = [sig(f"m_bld{j}") for j in range(2)]
    m_cld = [sig(f"m_cld{j}") for j in range(2)]
    m_dbu_rdy, m_scan, m_hc, m_ymm = sig("m_dbu_rdy", 2), sig("m_scan", 2), sig("m_hc", 2), sig("m_ymm", 2)
    m_da_rdy, m_yev, m_az = sig("m_da_rdy"), sig("m_yev"), sig("m_az")

    a_ld = [sig(f"a_ld{j}") for j in range(2)]
    a_prep, a_prep_ev = sig("a_prep", 2), sig("a_prep_ev", 2)
    a_qb, a_pr, a_rt, a_qq, a_qev = sig("a_qb"), sig("a_pr", 2), sig("a_rt", 2), sig("a_qq", 2), sig("a_qev", 2)

    b_ld = [sig(f"b_ld{j}") for j in range(2)]
    b_kvr_rdy, b_q_rdy = sig("b_kvr_rdy"), sig("b_q_rdy")
    b_rmm = sig("b_rmm")
    b_ktev, b_mxd, b_mxc, b_row = sig("b_ktev"), sig("b_mxd"), sig("b_mxc"), sig("b_row")
    b_st, b_exp, b_pv, b_cev = sig("b_st", 1), sig("b_exp", 3), sig("b_pv", 3), sig("b_cev", 1)
    b_cst = [sig(f"b_cst{j}", 1) for j in range(2)]
    b_one = sig("b_one")
    c_in = [sig(f"c_in{j}") for j in range(2)]
    c_tr, c_tev = sig("c_tr", 2), sig("c_tev", 2)

    f_gu, f_sl, f_hr = sig("f_gu"), sig("f_sl", 2), sig("f_hr", 2)

    n_cst = sig("n_cst")
    n_proj = sig("n_proj", 4)
    n_zero = sig("n_zero")
    n_xfr, n_qe, n_ke, n_ve, n_kmr = sig("n_xfr"), sig("n_qe"), sig("n_ke"), sig("n_ve"), sig("n_kmr", 2)
    n_sc, n_sub, n_exp, n_rr, n_p = sig("n_sc", 2), sig("n_sub"), sig("n_exp"), sig("n_rr", 2), sig("n_p")
    n_tr, n_te, n_pvm, n_ye, n_le = sig("n_tr"), sig("n_te", 1), sig("n_pvm", 2), sig("n_ye", 1), sig("n_le")

    r_mm = sig("r_mm", 2)
    r_cp, r_ex, r_sel, r_tr, r_te, r_st = (sig(n) for n in ("r_cp", "r_ex", "r_sel", "r_tr", "r_te", "r_st"))
    e_ld = [sig(f"e_ld{j}") for j in range(2)]
    e_tld = [sig(f"e_tld{j}") for j in range(2)]
    e_dld = [sig(f"e_dld{j}") for j in range(2)]
    e_gu, e_sl, e_awr, e_hr, e_dn = sig("e_gu", 2), sig("e_sl", 2), sig("e_awr", 2), sig("e_hr", 2), sig("e_dn", 2)
    e_yev, e_zr = sig("e_yev", 1), sig("e_zr")
    pe_passed = sig("pe_passed")
    out_st = [sig(f"out_st{j}", 1) for j in range(2)]

    import contextlib
    stack = contextlib.ExitStack()
    block = stack.enter_context(nc.Block())

    def turned(layer, t):
        return 8 * t if layer == 0 else 8 * NT + 4 * t

    TAIL = [4, 5]
    XT = [6, 7]

    @block.sync
    def _(sp):
        def store_result():
            with sp.Fori(0, NT // 2) as i:
                for j in range(2):
                    sp.wait_ge(xn_rdy.sem, xn_rdy.at(stages * NT + 2 * i + j + 1))
                    sp.dma_start(out.rearrange("(t p) d -> t p d", p=TILE)[2 * i + j], xn[:, j, :]
                                 ).then_inc(out_st[j].sem, 16)
            for j in range(2):
                sp.wait_ge(out_st[j].sem, out_st[j].at(8 * NT))

        for s in rings:
            sp.sem_inc(s.sem, s.credit)
        sp.dma_start(x_tok[:], a["x"].rearrange("(t p) d -> p t d", p=TILE)).then_inc(x_ld.sem, 16)
        for dst, src in ((ident[:], a["c_ident"]), (m_lnw[:], a["ln_w"]), (m_lnb[:], a["ln_b"])):
            sp.dma_start(dst, src).then_inc(c_ld.sem, 16)
        for dst, src in ((m_in[:], a["in_proj_T"].rearrange("(k p) n -> p k n", p=128)),
                         (m_cw[:], a["conv_w"]), (m_cb[:], a["conv_b"]), (m_xp[:], a["x_proj_T"]),
                         (m_dt[:], a["dt_proj_T"]), (m_dtb[:], a["dt_proj_b"]), (m_al[:], a["A_log"]),
                         (m_dp[:], a["D_param"]), (m_out[:], a["out_proj_T"])):
            sp.dma_start(dst, src).then_inc(w_ld[0].sem, 16)

        sp.wait_ge(m_dbc_ev.sem, m_dbc_ev.at(NCH))
        sp.dma_start(bc_dram, m_dbc[DTR:DTR + 2 * NS, :]).then_inc(m_bc_st.sem, 16)
        sp.wait_ge(m_bc_st.sem, m_bc_st.at(16))
        with sp.Fori(0, NS // 2) as i:
            for j in range(2):
                n = 2 * i + j
                sp.wait_ge(m_dbu_rdy.sem, m_dbu_rdy.at(n - 1))
                sp.dma_start(m_bb[:, j, :], bc_dram[n].partition_broadcast(DI)).then_inc(m_bld[j].sem, 16)
                sp.wait_ge(m_hc.sem, m_hc.at(n - 1))
                sp.dma_start(m_cc[:, j, :], bc_dram[n + NS].partition_broadcast(DI)).then_inc(m_cld[j].sem, 16)
        if stages < 2:
            store_result()
            return

        sp.wait_ge(xt_rdy.sem, xt_rdy.at(2 * NT))
        sp.dma_start(a_rope[:], a["c_ropeq"]).then_inc(w_ld[1].sem, 16)
        with sp.Fori(0, H // 2) as i:
            for j in range(2):
                h = 2 * i + j
                sp.wait_ge(a_prep.sem, a_prep.at(2 * i + j - 1))
                for dst, src in ((a_wq[:, j, :], a["Wq"][h]), (a_wkq[:, j, :], a["w_kc_q"][h]),
                                 (a_wqr[:, j, :], a["W_qr_T"][h]), (a_wkr[:, j, :], a["W_kr_T"][h]),
                                 (a_wkv[:, j, :], a["w_kc_kv"][h]), (a_wo[:, j, :], a["Wo_T"][h])):
                    sp.dma_start(dst, src).then_inc(a_ld[j].sem, 16)

        sp.wait_ge(a_qev.sem, a_qev.at(H * NCH))
        sp.dma_start(b_rope[:], a["c_ropek"]).then_inc(w_ld[1].sem, 16)

        def load_kv(b, j):
            sp.dma_start(b_kv[:, j, :, :], a["ctx"][b].rearrange("(p c) d -> p c d", c=KC)).then_inc(b_ld[j].sem, 16)

        def store_ctx(b, j):
            sp.wait_ge(b_cev.sem, b_cev.at(2 * (b + 1)))
            for e in range(2):
                sp.dma_start(ctx_dram.rearrange("(b s) (i e) d -> b e s i d", s=S, e=2)[b, e],
                             b_ctx[S * e:S * e + S, j, :, :]).then_inc(b_cst[j].sem, 16)

        load_kv(0, 0)
        load_kv(1, 1)
        with sp.Fori(0, NSEQ // 2 - 1) as i:
            for j in range(2):
                b = 2 * i + j
                sp.wait_ge(b_kvr_rdy.sem, b_kvr_rdy.at(b + 1))
                load_kv(b + 2, j)
                store_ctx(b, j)
        for j in range(2):
            store_ctx(NSEQ - 2 + j, j)
        sp.wait_ge(b_cst[0].sem, b_cst[0].at(16 * NSEQ))
        sp.wait_ge(b_cst[1].sem, b_cst[1].at(16 * NSEQ))
        sp.wait_ge(b_pv.sem, b_pv.at(NSEQ * KC))
        with sp.Fori(0, NT // 2) as i:
            for j in range(2):
                sp.wait_ge(c_tr.sem, c_tr.at(2 * i + j - 1))
                sp.dma_start(c_ctx[:, j, :], ctx_dram.rearrange("(t p) h d -> t p (h d)", p=TILE)[2 * i + j]
                             ).then_inc(c_in[j].sem, 16)
        if stages < 3:
            store_result()
            return

        sp.wait_ge(xt_rdy.sem, xt_rdy.at(3 * NT))
        for dst, src in ((f_g[:], a["gate_T"].rearrange("(k p) n -> p k n", p=128)),
                         (f_u[:], a["up_T"].rearrange("(k p) n -> p k n", p=128)),
                         (f_d[:, 0:5, :], a["down_T"][0:640].rearrange("(k p) n -> p k n", p=128)),
                         (f_d[0:64, 5, :], a["down_T"][640:704]),
                         (f_gs[:], a["gate_s"]), (f_us[:], a["up_s"]),
                         (f_ds[:], a["down_s"].partition_broadcast(TILE))):
            sp.dma_start(dst, src).then_inc(w_ld[2].sem, 16)
        if stages < 4:
            store_result()
            return

        sp.wait_ge(xt_rdy.sem, xt_rdy.at(4 * NT))
        for k, name in enumerate(("N_Wq1", "N_Wq2", "N_Wk", "N_Wv")):
            sp.dma_start(n_w[:, k, :, :], a[name].rearrange("(k p) n -> p k n", p=128)).then_inc(w_ld[3].sem, 16)
        for dst, src in ((n_lam[:], a["N_Wlam"].rearrange("(k p) n -> p k n", p=128)),
                         (n_wo[:], a["N_Wo"].rearrange("(k p) n -> p k n", p=128)),
                         (z_wq[:], a["Z_Wq_T"].rearrange("(k p) n -> p k n", p=128)),
                         (z_wkv[:], a["Z_Wkv_T"]),
                         (z_wo[:], a["Z_Wout_T"].rearrange("(k p) n -> p k n", p=128)),
                         (z_ctx[:], a["ctx_head_T"]), (n_hm[:], a["c_headmask"]), (n_caus[:], a["c_causal"])):
            sp.dma_start(dst, src).then_inc(w_ld[3].sem, 16)
        if stages < 6:
            store_result()
            return

        sp.wait_ge(xt_rdy.sem, xt_rdy.at(6 * NT))
        for dst, src in ((r_w[:], a["router_w"].rearrange("(k p) n -> p k n", p=128)),
                         (r_b[:], a["router_bias"].partition_broadcast(TILE)),
                         (r_lt[:], a["c_lower"].partition_broadcast(TILE))):
            sp.dma_start(dst, src).then_inc(w_ld[5].sem, 16)
        sp.dma_start(r_wt[NE:NEX, :], a["c_ones"]).then_inc(w_ld[5].sem, 16)
        sp.wait_ge(r_te.sem, r_te.at(NCH))
        sp.dma_start(rw_dram, r_wt[:]).then_inc(r_st.sem, 16)
        sp.wait_ge(r_st.sem, r_st.at(16))
        with sp.Fori(0, NCH) as c:
            with sp.Fori(0, NEX // 2) as i:
                for j in range(2):
                    u = NEX * c + 2 * i + j
                    sp.wait_ge(e_gu.sem, e_gu.at(u - 1))
                    sp.dma_start(e_wgu[:, j, :], a["W_exp"][2 * i + j][:, 0:2 * D]).then_inc(e_ld[j].sem, 16)
                    sp.wait_ge(e_awr.sem, e_awr.at(u - 1))
                    sp.dma_start(e_tw[:, j, :], rw_dram[2 * i + j, bass.ds(CHUNK * c, CHUNK)].partition_broadcast(128)
                                 ).then_inc(e_tld[j].sem, 16)
                    sp.wait_ge(e_dn.sem, e_dn.at(u - 1))
                    sp.dma_start(e_wd[:, j, :], a["W_exp"][2 * i + j][:, 2 * D:3 * D]).then_inc(e_dld[j].sem, 16)
        store_result()

    @block.vector
    def _(dve):
        ch = Chain(nc, "dve_chain")
        v = nc.vector

        def residual(k, t, bank, mul=1.0):
            dve.wait_ge(tail_rdy.sem, tail_rdy.at((k - 1) * NT + t + 1))
            v.scalar_tensor_tensor(x_tok[:, t, :], x_tok[:, t, :], mul, ps[0:TILE, bank, 0:D],
                                   ALU.mult, ALU.add).then_inc(tail_used.sem, 1)
            dve.wait_ge(tail_used.sem, tail_used.at((k - 1) * NT + t + 1))
            v.bn_stats(ln_stats[:, t, :], x_tok[:, t, :]).then_inc(ln_st.sem, 1)

        def norm(k):
            dve.wait_ge(ln_st.sem, ln_st.at((k + 1) * NT))
            me, mo, ve, vo = (ln_stats[:, :, q] for q in (1, 4, 2, 5))
            v.tensor_tensor(ln_a[:], me, mo, ALU.add).then_inc(ch.sem, ch.one())
            v.tensor_tensor(ln_d[:], me, mo, ALU.subtract).then_inc(ch.sem, ch.one())
            v.tensor_tensor(ln_b[:], ve, vo, ALU.add).then_inc(ch.sem, ch.one())
            dve.wait_ge(ch.sem, ch.all())
            v.tensor_scalar(ln_mean[:], ln_a[:], 0.5, None, ALU.mult).then_inc(ch.sem, ch.one())
            v.tensor_tensor(ln_sq[:], ln_d[:], ln_d[:], ALU.mult).then_inc(ch.sem, ch.one())
            v.tensor_scalar(ln_b[:], ln_b[:], 1.0 / D, EPS, ALU.mult, ALU.add).then_inc(ch.sem, ch.one())
            dve.wait_ge(ch.sem, ch.all())
            v.scalar_tensor_tensor(ln_var[:], ln_sq[:], 0.25, ln_b[:], ALU.mult, ALU.add).then_inc(std_req.sem, 1)
            dve.wait_ge(std_rdy.sem, std_rdy.at(k + 1))
            v.reciprocal(ln_rstd[:], ln_std[:]).then_inc(ch.sem, ch.one())
            dve.wait_ge(ch.sem, ch.all())
            with dve.Fori(0, NT // 2) as i:
                for j in range(2):
                    t = 2 * i + j
                    if k == stages:
                        dve.wait_ge(out_st[j].sem, out_st[j].at(16 * i))
                    else:
                        dve.wait_ge(xt_mm.sem, xt_mm.at(k * NT + t - 1))
                    if 0 < k < stages:
                        dve.wait_ge(xcp.sem, xcp.at((k - 1) * NT + t - 1))
                    v.tensor_scalar(xn[:, j, :], x_tok[:, t, :], ln_mean[:, bass.ds(t, 1)], ln_rstd[:, bass.ds(t, 1)],
                                    ALU.subtract, ALU.mult).then_inc(xn_rdy.sem, 1)

        dve.wait_ge(x_ld.sem, x_ld.at(16))
        with dve.Fori(0, NT) as t:
            v.bn_stats(ln_stats[:, t, :], x_tok[:, t, :]).then_inc(ln_st.sem, 1)
        norm(0)

        dve.wait_ge(w_ld[0].sem, w_ld[0].at(9 * 16))
        dve.wait_ge(m_ev.sem, m_ev.at(NCH))
        dve.wait_ge(m_padz.sem, m_padz.at(2))
        v.tensor_scalar(m_c[:], m_pad[:, :, 0:S], m_cw[:, 0:1], m_cb[:, 0:1], ALU.mult, ALU.add).then_inc(ch.sem, ch.one())
        dve.wait_ge(ch.sem, ch.all())
        v.scalar_tensor_tensor(m_c[:], m_pad[:, :, 1:1 + S], m_cw[:, 1:2], m_c[:], ALU.mult, ALU.add).then_inc(ch.sem, ch.one())
        dve.wait_ge(ch.sem, ch.all())
        v.scalar_tensor_tensor(m_c[:], m_pad[:, :, 2:2 + S], m_cw[:, 2:3], m_c[:], ALU.mult, ALU.add
                               ).then_inc(m_convd.sem, 1)
        flat_c = m_c[:].rearrange("p a b -> p (a b)")
        dve.wait_ge(m_exp.sem, m_exp.at(2))
        v.tensor_scalar(m_t1[:], m_t1[:], 1.0, None, ALU.add).then_inc(ch.sem, ch.one())
        dve.wait_ge(ch.sem, ch.all())
        v.reciprocal(m_t2[:], m_t1[:]).then_inc(ch.sem, ch.one())
        v.tensor_scalar(m_a[:], m_a[:], -1.0, None, ALU.mult).then_inc(ch.sem, ch.one())
        dve.wait_ge(ch.sem, ch.all())
        v.tensor_tensor(m_u[:], flat_c, m_t2[:], ALU.mult).then_inc(m_silu.sem, 1)
        dve.wait_ge(m_silu.sem, m_silu.at(1))
        v.tensor_scalar(m_ud[:], m_u[:], m_dp[:, 0:1], None, ALU.mult).then_inc(m_silu.sem, 1)
        dve.wait_ge(m_mm.sem, m_mm.at(3 * NCH))
        zt = ps[0:DI, 4:8, 0:CHUNK]
        v4 = lambda t: t[:].rearrange("p (c n) -> p c n", c=NCH)
        v.tensor_scalar(v4(m_t1), zt, m_dtb[:, 0:1], 0.0, ALU.add, ALU.min).then_inc(ch.sem, ch.one())
        v.tensor_scalar(v4(m_t2), zt, m_dtb[:, 0:1], 0.0, ALU.add, ALU.max).then_inc(ch.sem, ch.one())
        dve.wait_ge(ch.sem, ch.all())
        v.tensor_tensor(m_t1[:], m_t1[:], m_t2[:], ALU.subtract).then_inc(m_abs.sem, 1)
        dve.wait_ge(m_ln.sem, m_ln.at(1))
        v.tensor_scalar(m_ud2[:], m_t1[:], 2.0, None, ALU.add).then_inc(ch.sem, ch.one())
        dve.wait_ge(ch.sem, ch.all())
        v.reciprocal(m_sq[:], m_ud2[:]).then_inc(ch.sem, ch.one())
        dve.wait_ge(ch.sem, ch.all())
        v.tensor_tensor(m_t1[:], m_t1[:], m_sq[:], ALU.mult).then_inc(ch.sem, ch.one())
        dve.wait_ge(ch.sem, ch.all())
        v.tensor_tensor(m_sq[:], m_t1[:], m_t1[:], ALU.mult).then_inc(ch.sem, ch.one())
        dve.wait_ge(ch.sem, ch.all())
        v.tensor_scalar(m_ud2[:], m_sq[:], ATANH[-1], None, ALU.mult).then_inc(ch.sem, ch.one())
        for coef in ATANH[-2:0:-1]:
            dve.wait_ge(ch.sem, ch.all())
            v.scalar_tensor_tensor(m_ud2[:], m_ud2[:], coef, m_sq[:], ALU.add, ALU.mult).then_inc(ch.sem, ch.one())
        dve.wait_ge(ch.sem, ch.all())
        v.scalar_tensor_tensor(m_t1[:], m_ud2[:], ATANH[0], m_t1[:], ALU.add, ALU.mult).then_inc(ch.sem, ch.one())
        dve.wait_ge(ch.sem, ch.all())
        v.tensor_tensor(m_t2[:], m_t2[:], m_t1[:], ALU.add).then_inc(ch.sem, ch.one())
        dve.wait_ge(ch.sem, ch.all())
        flat_delta = m_delta[:].rearrange("p a b -> p (a b)")
        v.tensor_scalar(flat_delta, m_t2[:], 0.001, None, ALU.mult).then_inc(m_dl.sem, 1)
        dve.wait_ge(m_dl.sem, m_dl.at(1))
        v.tensor_tensor(m_du[:], flat_delta, m_u[:], ALU.mult).then_inc(m_dl.sem, 1)
        with dve.Fori(0, NS // 2) as i:
            for j in range(2):
                n = 2 * i + j
                dve.wait_ge(m_da_rdy.sem, m_da_rdy.at(n + 1))
                dve.wait_ge(m_dbu_rdy.sem, m_dbu_rdy.at(n + 1))
                dve.wait_ge(m_ymm.sem, m_ymm.at(n - 1))
                v.tensor_tensor_scan(m_h[:, j, :], m_da[:, j, :, :].rearrange("p a b -> p (a b)"), m_dbu[:, j, :],
                                     0.0, ALU.mult, ALU.add).then_inc(m_scan.sem, 1)
                dve.wait_ge(m_scan.sem, m_scan.at(n + 1))
                dve.wait_ge(m_cld[j].sem, m_cld[j].at(16 * (i + 1)))
                v.tensor_tensor(m_h[:, j, :], m_h[:, j, :], m_cc[:, j, :], ALU.mult).then_inc(m_hc.sem, 1)
        with dve.Fori(0, NT // 2) as i:
            for j in range(2):
                residual(1, 2 * i + j, TAIL[j], 2.0)
        norm(1)
        if stages < 2:
            return

        dve.wait_ge(w_ld[1].sem, w_ld[1].at(16))
        with dve.Fori(0, H // 2) as i:
            for j in range(2):
                for c in range(NCH):
                    u = 8 * i + 4 * j + c
                    q = c % 2
                    dve.wait_ge(a_qb.sem, a_qb.at(u + 1))
                    dve.wait_ge(a_rt.sem, a_rt.at(u - 1))
                    for k, (half, tab) in enumerate(((0, 0), (1, 1), (1, 2), (0, 3))):
                        ins = v.tensor_tensor(
                            a_prod[:, q, k, :].rearrange("p (b s) -> p b s", s=S),
                            ps[0:HALFQ, 2 * q + half, 0:CHUNK].rearrange("p (b s) -> p b s", s=S),
                            a_rope[:, tab, :].unsqueeze(1).broadcast_to([HALFQ, 8, S]), ALU.mult)
                    ins.then_inc(a_pr.sem, 1)

        def maxima(b, j):
            for c in range(8):
                for u in range(3):
                    dve.wait_ge(b_rmm.sem, b_rmm.at(30 * b + 3 + 3 * c + u + 1))
                    v.tensor_reduce(b_mx3[:, j, c, u:u + 1], ps[0:TILE, u, 0:4 * KP], AX.X, ALU.max
                                    ).then_inc(b_mxd.sem, 1)
            dve.wait_ge(b_mxd.sem, b_mxd.at(24 * (b + 1)))
            v.tensor_reduce(b_mx[:, j, :], b_mx3[:, j, :, :], AX.X, ALU.max).then_inc(b_mxc.sem, 1)

        def outputs(b, j):
            dve.wait_ge(b_pv.sem, b_pv.at(KC * (b + 1)))
            for g in range(2):
                o = ps[0:TILE, 6 + g, 0:4 * (DC + 1)].rearrange("p (i d) -> p i d", i=4)
                v.reciprocal(b_rs[:, j, 4 * g:4 * g + 4], o[:, :, DC]).then_inc(ch.sem, ch.one())
            dve.wait_ge(ch.sem, ch.all())
            dve.wait_ge(b_cst[j].sem, b_cst[j].at(ctx_stored(b, j)))
            for g in range(2):
                o = ps[0:TILE, 6 + g, 0:4 * (DC + 1)].rearrange("p (i d) -> p i d", i=4)
                v.tensor_tensor(b_ctx[:, j, 4 * g:4 * g + 4, :], o[:, :, 0:DC],
                                b_rs[:, j, 4 * g:4 * g + 4].unsqueeze(2).broadcast_to([TILE, 4, DC]), ALU.mult
                                ).then_inc(b_cev.sem, 1)

        def ctx_stored(b, j):
            return 16 * (b - j)

        maxima(0, 0)
        dve.wait_ge(xcp.sem, xcp.at(NT))
        with dve.Fori(0, NSEQ // 2 - 1) as i:
            ch.enter(i, 4)
            for j in range(2):
                maxima(2 * i + j + 1, 1 - j)
                outputs(2 * i + j, j)
            ch.leave(NSEQ // 2 - 1)
        maxima(NSEQ - 1, 1)
        outputs(NSEQ - 2, 0)
        outputs(NSEQ - 1, 1)
        with dve.Fori(0, NT // 2) as i:
            for j in range(2):
                residual(2, 2 * i + j, TAIL[j])
        norm(2)
        if stages < 3:
            return

        dve.wait_ge(w_ld[2].sem, w_ld[2].at(7 * 16))
        dve.wait_ge(xcp.sem, xcp.at(2 * NT))
        with dve.Fori(0, NCH) as c:
            for b in range(FB):
                q, m = b % 2, (128 if b < 5 else 64)
                dve.wait_ge(f_sl.sem, f_sl.at(FB * c + b + 1))
                if b == 0:
                    dve.wait_ge(tail_rdy.sem, tail_rdy.at(2 * NT + 4 * c))
                v.scalar_tensor_tensor(f_h[0:m, b, :], ps[0:m, 2 + q, 0:CHUNK], f_us[0:m, b:b + 1],
                                       f_act[0:m, q, :], ALU.mult, ALU.mult).then_inc(f_hr.sem, 1)
            ch.enter(c, TPC)
            for s in range(TPC):
                t, j = TPC * c + s, s % 2
                dve.wait_ge(tail_rdy.sem, tail_rdy.at(2 * NT + t + 1))
                v.tensor_tensor(f_y[:, j, :], ps[0:TILE, TAIL[j], 0:D], f_ds[:], ALU.mult).then_inc(ch.sem, ch.one())
                dve.wait_ge(ch.sem, ch.all())
                v.tensor_tensor(x_tok[:, t, :], x_tok[:, t, :], f_y[:, j, :], ALU.add).then_inc(tail_used.sem, 1)
                dve.wait_ge(tail_used.sem, tail_used.at(2 * NT + t + 1))
                v.bn_stats(ln_stats[:, t, :], x_tok[:, t, :]).then_inc(ln_st.sem, 1)
            ch.leave(NCH)
        norm(3)
        if stages < 4:
            return

        dve.wait_ge(w_ld[3].sem, w_ld[3].at(12 * 16))
        v.tensor_copy(n_caus_bf[:], n_caus[:].unsqueeze(1).broadcast_to([TILE, 8, S])).then_inc(n_cst.sem, 1)
        v.tensor_copy(ident_bf[:], ident[0:TILE, 0:TILE]).then_inc(n_cst.sem, 1)

        def softmax(base, t, j, ns):
            hh = ns * H
            sc = ps[0:TILE, 3:3 + 2 * ns, 0:CHUNK].rearrange("p q (h k) -> p q h k", k=S)
            dve.wait_ge(n_sc.sem, n_sc.at(base + t + 1))
            v.tensor_reduce(n_mx[:, j, 0:hh].rearrange("p (q h) -> p q h", h=8), sc, AX.X, ALU.max).then_inc(ch.sem, ch.one())
            dve.wait_ge(ch.sem, ch.all())
            for q in range(2 * ns):
                ins = v.tensor_tensor(n_e[:, j, CHUNK * q:CHUNK * q + CHUNK].rearrange("p (h k) -> p h k", k=S),
                                      sc[:, q, :, :],
                                      n_mx[:, j, 8 * q:8 * q + 8].unsqueeze(2).broadcast_to([TILE, 8, S]),
                                      ALU.subtract)
            ins.then_inc(n_sub.sem, 1)
            dve.wait_ge(n_exp.sem, n_exp.at(base + t + 1))
            v.tensor_reduce(n_sum[:, j, 0:hh], n_e[:, j, 0:hh * S].rearrange("p (h k) -> p h k", k=S),
                               AX.X, ALU.add).then_inc(ch.sem, ch.one())
            dve.wait_ge(ch.sem, ch.all())
            if ns == 1:
                v.reciprocal(n_r[:, j, 0:H], n_sum[:, j, 0:H]).then_inc(n_rr.sem, 1)
            else:
                v.reciprocal(n_r[:, j, :], n_sum[:, j, :]).then_inc(ch.sem, ch.one())
                dve.wait_ge(n_le.sem, n_le.at(t + 1))
                v.tensor_scalar(n_l2[:, j, :], n_l[:, j, :], 1.0, None, ALU.add).then_inc(ch.sem, ch.one())
                dve.wait_ge(ch.sem, ch.all())
                v.reciprocal(n_l3[:, j, :], n_l2[:, j, :]).then_inc(ch.sem, ch.one())
                dve.wait_ge(ch.sem, ch.all())
                v.scalar_tensor_tensor(n_r[:, j, H:2 * H], n_r[:, j, H:2 * H], -1.0, n_l3[:, j, :],
                                       ALU.mult, ALU.mult).then_inc(n_rr.sem, 1)

        for layer, ns in ((0, 2), (1, 1)):
            per = 2 if ns == 1 else 5
            base = layer * NT
            if layer == 1 and stages < 5:
                return
            softmax(base, 0, 0, ns)
            dve.wait_ge(xcp.sem, xcp.at((3 + layer) * NT))
            with dve.Fori(0, NT // 2 - 1) as i:
                ch.enter(i, 2 * per)
                for j in range(2):
                    softmax(base, 2 * i + j + 1, 1 - j, ns)
                    residual(4 + layer, 2 * i + j, 7)
                ch.leave(NT // 2 - 1)
            softmax(base, NT - 1, 1, ns)
            residual(4 + layer, NT - 2, 7)
            residual(4 + layer, NT - 1, 7)
            norm(4 + layer)
        if stages < 6:
            return

        dve.wait_ge(w_ld[5].sem, w_ld[5].at(4 * 16))
        dve.wait_ge(r_ex.sem, r_ex.at(1))
        flat = lambda t: t[:].rearrange("p a b -> p (a b)")

        def step(ins):
            ins.then_inc(ch.sem, ch.one())
            dve.wait_ge(ch.sem, ch.all())

        step(v.tensor_scalar(flat(r_s), flat(r_m), 1.0, None, ALU.add))
        step(v.reciprocal(flat(r_s), flat(r_s)))
        step(v.tensor_tensor(r_sb[:], r_s[:], r_b[:].unsqueeze(1).broadcast_to([TILE, NT, NE]), ALU.add))
        quad = r_sb[:].rearrange("p t (g e) -> p (t g) e", e=4)
        f3 = lambda t: t[:].rearrange("p t g e -> p (t g) e")
        f2 = lambda t: t[:].rearrange("p t g -> p (t g)")
        v.tensor_tensor(f3(r_hi), quad[:, :, 0:2], quad[:, :, 2:4], ALU.max).then_inc(ch.sem, ch.one())
        step(v.tensor_tensor(f3(r_lo), quad[:, :, 0:2], quad[:, :, 2:4], ALU.min))
        v.tensor_tensor(f2(r_g1), f3(r_hi)[:, :, 0], f3(r_hi)[:, :, 1], ALU.max).then_inc(ch.sem, ch.one())
        v.tensor_tensor(f2(r_g2), f3(r_hi)[:, :, 0], f3(r_hi)[:, :, 1], ALU.min).then_inc(ch.sem, ch.one())
        step(v.tensor_tensor(f2(r_g3), f3(r_lo)[:, :, 0], f3(r_lo)[:, :, 1], ALU.max))
        step(v.tensor_tensor(r_g2[:], r_g2[:], r_g3[:], ALU.max))
        step(v.tensor_tensor(r_g1[:], r_g1[:], r_g2[:], ALU.add))
        other = r_g1[:].unsqueeze(2).broadcast_to([TILE, NT, NG, NG])
        own = r_g1[:].unsqueeze(3).broadcast_to([TILE, NT, NG, NG])
        for t in range(NT):
            v.tensor_tensor(r_c1[:, t, :, :], other[:, t, :, :], own[:, t, :, :], ALU.is_gt).then_inc(ch.sem, ch.one())
            v.tensor_tensor(r_c2[:, t, :, :], other[:, t, :, :], own[:, t, :, :], ALU.is_equal).then_inc(ch.sem, ch.one())
        dve.wait_ge(ch.sem, ch.all())
        c3 = lambda t: t[:].rearrange("p t g e -> p t (g e)")
        step(v.tensor_tensor(c3(r_c2), c3(r_c2), r_lt[:].rearrange("p g e -> p (g e)").unsqueeze(1).broadcast_to(
            [TILE, NT, NG * NG]), ALU.mult))
        step(v.tensor_tensor(f3(r_c1), f3(r_c1), f3(r_c2), ALU.add))
        step(v.tensor_reduce(f2(r_g2), f3(r_c1), AX.X, ALU.add))
        step(v.tensor_scalar(r_g3[:], r_g2[:], TOPG - 0.5, None, ALU.is_lt))
        step(v.tensor_tensor(r_m[:].rearrange("p t (g e) -> p (t g) e", e=4), quad,
                             f2(r_g3).unsqueeze(2).broadcast_to([TILE, NT * NG, 4]), ALU.mult))
        for t in range(NT):
            v.max(r_top[:, t, :], r_m[:, t, :]).then_inc(ch.sem, ch.one())
        dve.wait_ge(ch.sem, ch.all())
        for t in range(NT):
            v.match_replace(r_m2[:, t, :], r_top[:, t, :], r_m[:, t, :], NEG).then_inc(ch.sem, ch.one())
        dve.wait_ge(ch.sem, ch.all())
        step(v.tensor_scalar(r_m2[:], r_m2[:], NEG / 2, None, ALU.is_lt))
        step(v.tensor_tensor(r_m[:], r_m2[:], r_s[:], ALU.mult))
        step(v.tensor_reduce(r_den[:], r_m[:], AX.X, ALU.add))
        step(v.reciprocal(r_rden[:], r_den[:]))
        step(v.tensor_scalar(r_rden[:], r_rden[:], ROUTED_SCALE, None, ALU.mult))
        v.tensor_tensor(r_m2[:], r_m[:], r_rden[:].unsqueeze(2).broadcast_to([TILE, NT, NE]), ALU.mult
                        ).then_inc(r_sel.sem, 1)

        dve.wait_ge(xcp.sem, xcp.at(5 * NT))
        with dve.Fori(0, NCH) as c:
            with dve.Fori(0, NEX // 2) as i:
                for j in range(2):
                    u = NEX * c + 2 * i + j
                    dve.wait_ge(e_awr.sem, e_awr.at(u + 1))
                    dve.wait_ge(e_dn.sem, e_dn.at(u - 1))
                    v.tensor_tensor(e_h[:, j, :], e_aw[:, j, :], ps[:, 2 + j, 0:CHUNK], ALU.mult
                                    ).then_inc(e_hr.sem, 1)
            for s in range(TPC):
                residual(6, TPC * c + s, 6 + s % 2)
        norm(6)


    @block.scalar
    def _(act):
        copy = lambda dst, src, **kw: nc.scalar.activation(dst, src, ACT.Copy, **kw)
        ch = Chain(nc, "act_chain")

        def norm(k):
            act.wait_ge(std_req.sem, std_req.at(k + 1))
            nc.scalar.activation(ln_std[:], ln_var[:], ACT.Sqrt).then_inc(std_rdy.sem, 1)
            if k == stages:
                return
            with act.Fori(0, NT // 2) as i:
                for j in range(2):
                    t = 2 * i + j
                    act.wait_ge(xt_mm.sem, xt_mm.at(k * NT + t + 1))
                    src = ps[:, XT[j], 0:KD * TILE].rearrange("p (k n) -> p k n", k=KD)
                    if k == 0:
                        nc.scalar.activation(x_feat[:, 0, bass.ds(TILE * t, TILE)], src[:, 0, :], ACT.Identity,
                                             scale=m_lnw[:, 0:1], bias=m_lnb[:, 0:1])
                        nc.scalar.activation(x_feat[:, 1, bass.ds(TILE * t, TILE)], src[:, 1, :], ACT.Identity,
                                             scale=m_lnw[:, 1:2], bias=m_lnb[:, 1:2]).then_inc(xt_rdy.sem, 1)
                    else:
                        copy(x_feat[:, :, bass.ds(TILE * t, TILE)], src).then_inc(xt_rdy.sem, 1)

        act.wait_ge(c_ld.sem, c_ld.at(48))
        norm(0)

        act.wait_ge(m_padz.sem, m_padz.at(2))
        for c in range(NCH):
            act.wait_ge(m_mm.sem, m_mm.at(c + 1))
            copy(m_pad[:, 8 * c:8 * c + 8, 1:1 + S],
                 ps[0:DI, c, 0:CHUNK].rearrange("p (b s) -> p b s", s=S)).then_inc(m_ev.sem, 1)
        act.wait_ge(w_ld[0].sem, w_ld[0].at(9 * 16))
        nc.scalar.activation(m_a[:], m_al[:], ACT.Exp).then_inc(m_exp.sem, 1)
        act.wait_ge(m_convd.sem, m_convd.at(1))
        nc.scalar.activation(m_t1[:], m_c[:].rearrange("p a b -> p (a b)"), ACT.Exp, scale=-1.0
                             ).then_inc(m_exp.sem, 1)
        for c in range(NCH):
            act.wait_ge(m_mm.sem, m_mm.at(NCH + c + 1))
            copy(m_dbc[:, CHUNK * c:CHUNK * c + CHUNK], ps[0:DTR + 2 * NS, c, 0:CHUNK]).then_inc(m_dbc_ev.sem, 1)
        act.wait_ge(m_abs.sem, m_abs.at(1))
        nc.scalar.activation(m_t1[:], m_t1[:], ACT.Exp).then_inc(m_ln.sem, 1)
        act.wait_ge(m_dl.sem, m_dl.at(1))
        act.wait_ge(m_padz.sem, m_padz.at(3))
        with act.Fori(0, NS // 2) as i:
            for j in range(2):
                n = 2 * i + j
                act.wait_ge(m_scan.sem, m_scan.at(n - 1))
                nc.scalar.activation(m_da[:, j, :, 1:S], m_delta[:, :, 1:S], ACT.Exp, scale=m_a[:, bass.ds(n, 1)]
                                     ).then_inc(m_da_rdy.sem, 1)
        act.wait_ge(m_ymm.sem, m_ymm.at(NS))
        with act.Fori(0, NCH) as c:
            for s in range(TPC):
                t, j = TPC * c + s, s % 2
                act.wait_ge(tail_rdy.sem, tail_rdy.at(t - 1))
                copy(m_y[:, j, :], ps[0:DI, c, TILE * s:TILE * s + TILE]).then_inc(m_yev.sem, 1)
        norm(1)
        if stages < 2:
            return

        with act.Fori(0, H // 2) as i:
            for j in range(2):
                act.wait_ge(a_prep.sem, a_prep.at(2 * i + j + 1))
                copy(a_wf[:, j, :, :], ps[:, 6, 0:KD * DCQ].rearrange("p (k n) -> p k n", k=KD))
                copy(a_w2[:, j, :, :], ps[0:HALFQ, 7, 0:2 * DC].rearrange("p (k n) -> p k n", k=2))
                copy(w3[64 * j:64 * j + 64, i, :], ps[64 * j:64 * j + 64, 7, 256:512]).then_inc(a_prep_ev.sem, 1)
            for j in range(2):
                for c in range(NCH):
                    u = 8 * i + 4 * j + c
                    act.wait_ge(a_qq.sem, a_qq.at(u + 1))
                    copy(q_all[:, 2 * i + j, CHUNK * c:CHUNK * c + CHUNK], ps[0:DC, 4 + c % 2, 0:CHUNK]
                         ).then_inc(a_qev.sem, 1)

        def keys_out(nb, nj):
            if not (isinstance(nb, int) and nb == 0):
                act.wait_ge(b_st.sem, b_st.at(2 * KC * (nb - 1)))
            for r in range(3):
                act.wait_ge(b_rmm.sem, b_rmm.at(30 * nb + r + 1))
                copy(b_kt[:, nj, 4 * KP * r:4 * KP * r + 4 * KP], ps[0:DC + 1, r, 0:4 * KP]).then_inc(b_ktev.sem, 1)

        def rows_out(nb, nj):
            for r, n in enumerate((3, 3, 2)):
                act.wait_ge(b_rmm.sem, b_rmm.at(30 * nb + 27 + r + 1))
                nc.scalar.activation(b_q[DC:DC + 1, nj, 3 * TILE * r:3 * TILE * r + n * TILE], ps[0:1, r, 0:n * TILE],
                                     ACT.Copy, scale=-1.0).then_inc(b_row.sem, 1)

        def exps(b, c):
            act.wait_ge(b_pv.sem, b_pv.at(KC * b + c - 2))
            for g in range(2):
                act.wait_ge(b_st.sem, b_st.at(2 * KC * b + 2 * c + g + 1))
                nc.scalar.activation(b_pt[:, c % 3, CHUNK * g:CHUNK * g + CHUNK], ps[0:KP, 3 + (2 * c + g) % 3, 0:CHUNK],
                                     ACT.Exp).then_inc(b_exp.sem, 1)

        def sequence(b, nb, nj):
            for c in range(KC):
                exps(b, c)
                if nb is not None and c == 0:
                    keys_out(nb, nj)
                if nb is not None and c == 10:
                    rows_out(nb, nj)

        keys_out(0, 0)
        rows_out(0, 0)
        with act.Fori(0, NSEQ // 2 - 1) as i:
            for j in range(2):
                sequence(2 * i + j, 2 * i + j + 1, 1 - j)
        sequence(NSEQ - 2, NSEQ - 1, 1)
        sequence(NSEQ - 1, None, None)
        with act.Fori(0, NT // 2) as i:
            for j in range(2):
                t = 2 * i + j
                act.wait_ge(c_tr.sem, c_tr.at(t + 1))
                act.wait_ge(tail_rdy.sem, tail_rdy.at(NT + t - 1))
                copy(c_ctxT[:, j, :, :].rearrange("p (q e) n -> p q (e n)", q=2), ps[:, 2 * j:2 * j + 2, 0:CHUNK]
                     ).then_inc(c_tev.sem, 1)
        norm(2)
        if stages < 3:
            return

        act.wait_ge(w_ld[2].sem, w_ld[2].at(7 * 16))
        with act.Fori(0, NCH) as c:
            for b in range(FB):
                q, m = b % 2, (128 if b < 5 else 64)
                act.wait_ge(f_gu.sem, f_gu.at(FB * c + b + 1))
                act.wait_ge(f_hr.sem, f_hr.at(FB * c + b - 1))
                nc.scalar.activation(f_act[0:m, q, :], ps[0:m, q, 0:CHUNK], ACT.Silu, scale=f_gs[0:m, b:b + 1]
                                     ).then_inc(f_sl.sem, 1)
        norm(3)
        if stages < 4:
            return

        def evac(base, t, j, ns):
            act.wait_ge(n_proj.sem, n_proj.at(2 * (base + t) + 1))
            act.wait_ge(n_sc.sem, n_sc.at(base + t - 1))
            src = ps[:, 0, 0:2 * ns * TILE].rearrange("p (q n) -> p q n", n=TILE)
            for e in range(2):
                ins = copy(n_qz[:, j, 0:2 * ns, e, S * e:S * e + S], src[:, :, S * e:S * e + S], scale=HD ** -0.5)
            ins.then_inc(n_qe.sem, 1)
            act.wait_ge(n_proj.sem, n_proj.at(2 * (base + t) + 2))
            act.wait_ge(n_kmr.sem, n_kmr.at(base + t - 1))
            copy(n_kf[:, j, :, :], ps[:, 1, 0:2 * TILE].rearrange("p (q n) -> p q n", n=TILE)).then_inc(n_ke.sem, 1)
            if ns == 2:
                act.wait_ge(n_rr.sem, n_rr.at(base + t - 1))
                nc.scalar.activation(n_l[:, j, :], ps[0:TILE, 1, 2 * TILE:2 * TILE + H], ACT.Exp, scale=-1.0
                                     ).then_inc(n_le.sem, 1)
            act.wait_ge(n_pvm.sem, n_pvm.at(base + t - 1))
            vsrc = ps[0:S, 2, :].rearrange("p (b g e d) -> p b g e d", b=2, g=H // 2, e=2)
            vdst = n_v[:, j, :, :, :].rearrange("p b (g e) d -> p b g e d", e=2)
            for e in range(2):
                ins = copy(vdst[:, :, :, e, HD * e:HD * e + HD], vsrc[:, :, :, e, :])
            ins.then_inc(n_ve.sem, 1)

        def finish(layer, t, j):
            base = layer * NT
            act.wait_ge(n_pvm.sem, n_pvm.at(base + t))
            for g in range(4 * (2 - layer)):
                act.wait_ge(n_tr.sem, n_tr.at(turned(layer, t) + g + 1))
                copy(n_pt[:, g, :], ps[0:S, 2 * (g % 2), 0:CHUNK]).then_inc(n_te.sem, 1)
            act.wait_ge(n_pvm.sem, n_pvm.at(base + t + 1))
            act.wait_ge(tail_rdy.sem, tail_rdy.at((3 + layer) * NT + t - 1))
            copy(n_yt[:, j, :, :], ps[:, 1, 256:256 + 2 * TILE].rearrange("p (k n) -> p k n", k=2)).then_inc(n_ye.sem, 1)

        def exps2(base, t, j, ns):
            act.wait_ge(n_sub.sem, n_sub.at(base + t + 1))
            nc.scalar.activation(n_e[:, j, 0:2 * ns * CHUNK], n_e[:, j, 0:2 * ns * CHUNK], ACT.Exp
                                 ).then_inc(n_exp.sem, 1)

        act.wait_ge(n_zero.sem, n_zero.at(3))
        for layer, ns in ((0, 2), (1, 1)):
            base = layer * NT
            if layer == 1 and stages < 5:
                return
            evac(base, 0, 0, ns)
            exps2(base, 0, 0, ns)
            with act.Fori(0, NT // 2 - 1) as i:
                for j in range(2):
                    t = 2 * i + j
                    evac(base, t + 1, 1 - j, ns)
                    finish(layer, t, j)
                    exps2(base, t + 1, 1 - j, ns)
            evac(base, NT - 1, 1, ns)
            finish(layer, NT - 2, 0)
            exps2(base, NT - 1, 1, ns)
            finish(layer, NT - 1, 1)
            norm(4 + layer)
        if stages < 6:
            return

        act.wait_ge(r_mm.sem, r_mm.at(NT))
        nc.scalar.activation(r_m[:].rearrange("p a b -> p (a b)"), ps[0:TILE, 0, :], ACT.Exp, scale=-1.0
                             ).then_inc(r_ex.sem, 1)
        for c in range(NCH):
            act.wait_ge(r_tr.sem, r_tr.at(c + 1))
            copy(r_wt[0:NE, CHUNK * c:CHUNK * c + CHUNK], ps[0:NE, c, 0:CHUNK]).then_inc(r_te.sem, 1)
        with act.Fori(0, NCH) as c:
            with act.Fori(0, NEX // 2) as i:
                for j in range(2):
                    u = NEX * c + 2 * i + j
                    act.wait_ge(e_gu.sem, e_gu.at(u + 1))
                    act.wait_ge(e_awr.sem, e_awr.at(u - 1))
                    nc.scalar.activation(e_act[:, j, :], ps[:, j, 0:CHUNK], ACT.Silu).then_inc(e_sl.sem, 1)
            act.wait_ge(e_dn.sem, e_dn.at(NEX * (c + 1)))
            act.wait_ge(tail_rdy.sem, tail_rdy.at(5 * NT + TPC * c))
            for g in range(2):
                copy(e_y[:, g, :], ps[:, 4 + g, 0:CHUNK]).then_inc(e_yev.sem, 1)
        norm(6)

    @block.gpsimd
    def _(pool):
        p = nc.gpsimd
        ch = Chain(nc, "pool_chain")

        def norm(k):
            if k == 0 or k == stages:
                return
            with pool.Fori(0, NT // 2) as i:
                for j in range(2):
                    t = 2 * i + j
                    pool.wait_ge(xn_rdy.sem, xn_rdy.at(k * NT + t + 1))
                    p.tensor_copy(x_tok[:, t, :], xn[:, j, :]).then_inc(xcp.sem, 1)

        p.memset(m_pad[:, :, 0:1], 0.0).then_inc(m_padz.sem, 1)
        p.memset(m_pad[:, :, S + 1:S + 2], 0.0).then_inc(m_padz.sem, 1)
        p.memset(m_da[:, :, :, 0:1], 0.0).then_inc(m_padz.sem, 1)
        norm(0)
        pool.wait_ge(m_dl.sem, m_dl.at(2))
        with pool.Fori(0, NS // 2) as i:
            for j in range(2):
                n = 2 * i + j
                pool.wait_ge(m_bld[j].sem, m_bld[j].at(16 * (i + 1)))
                pool.wait_ge(m_scan.sem, m_scan.at(n - 1))
                p.tensor_tensor(m_dbu[:, j, :], m_du[:], m_bb[:, j, :], ALU.mult).then_inc(m_dbu_rdy.sem, 1)
        norm(1)
        if stages < 2:
            return

        with pool.Fori(0, H // 2) as i:
            for j in range(2):
                for c in range(NCH):
                    u, q = 8 * i + 4 * j + c, c % 2
                    pool.wait_ge(a_pr.sem, a_pr.at(u + 1))
                    pool.wait_ge(a_qq.sem, a_qq.at(u - 1))
                    p.tensor_tensor(a_rot[:, q, 0, :], a_prod[:, q, 0, :], a_prod[:, q, 1, :], ALU.subtract)
                    p.tensor_tensor(a_rot[:, q, 1, :], a_prod[:, q, 2, :], a_prod[:, q, 3, :], ALU.add
                                    ).then_inc(a_rt.sem, 1)

        def prepare(nb, nj):
            pool.wait_ge(b_ld[nj].sem, b_ld[nj].at(8 * (nb - nj) + 16))
            if not (isinstance(nb, int) and nb == 0):
                pool.wait_ge(b_pv.sem, b_pv.at(KC * (nb - 1)))
            src, dst = b_kv[:, nj, :, :], b_kvr[:, nj, :, 0:DC]
            hd = DC // 2
            p.tensor_tensor(dst, src, b_rope[:, 0, :, :], ALU.mult).then_inc(ch.sem, ch.one())
            p.tensor_tensor(b_tmp[:, :, 0:hd], src[:, :, hd:DC], b_rope[:, 1, :, 0:hd], ALU.mult).then_inc(ch.sem, ch.one())
            p.tensor_tensor(b_tmp[:, :, hd:DC], src[:, :, 0:hd], b_rope[:, 1, :, hd:DC], ALU.mult).then_inc(ch.sem, ch.one())
            pool.wait_ge(ch.sem, ch.all())
            p.tensor_tensor(dst, dst, b_tmp[:], ALU.add).then_inc(b_kvr_rdy.sem, 1)
            p.tensor_copy(b_q[0:DC, nj, :].rearrange("p (h s) -> p h s", s=S), q_all[:, :, bass.ds(S * nb, S)]
                          ).then_inc(b_q_rdy.sem, 1)
            pool.wait_ge(b_kvr_rdy.sem, b_kvr_rdy.at(nb + 1))

        pool.wait_ge(a_qev.sem, a_qev.at(H * NCH))
        pool.wait_ge(w_ld[1].sem, w_ld[1].at(32))
        p.memset(b_kvr[:, :, :, DC:DC + 1], 1.0).then_inc(b_one.sem, 1)
        prepare(0, 0)
        with pool.Fori(0, NSEQ // 2 - 1) as i:
            ch.enter(i, 6)
            for j in range(2):
                prepare(2 * i + j + 1, 1 - j)
            ch.leave(NSEQ // 2 - 1)
        prepare(NSEQ - 1, 1)
        norm(2)
        if stages < 3:
            return
        norm(3)
        if stages < 4:
            return

        pool.wait_ge(xt_rdy.sem, xt_rdy.at(4 * NT))
        p.memset(n_qz[:], 0.0).then_inc(n_zero.sem, 1)
        p.memset(n_v[:], 0.0).then_inc(n_zero.sem, 1)
        pool.wait_ge(w_ld[3].sem, w_ld[3].at(12 * 16))
        pool.sem_inc(n_zero.sem, 1)

        def stationary(base, t, j, ns):
            pool.wait_ge(n_proj.sem, n_proj.at(2 * (base + t) - 2))
            if ns == 2:
                p.tensor_copy(n_xf[:, j, :, :], x_feat[:, :, bass.ds(TILE * t, TILE)]).then_inc(n_xfr.sem, 1)
            else:
                p.tensor_copy(n_xf[0:DC, j, 0, :], z_ctx[:, bass.ds(TILE * t, TILE)]).then_inc(n_xfr.sem, 1)
            pool.wait_ge(n_ke.sem, n_ke.at(base + t + 1))
            pool.wait_ge(n_sc.sem, n_sc.at(base + t - 1))
            for half in range(2):
                for e in range(2):
                    ins = p.tensor_tensor(n_km[:, j, 2 * half + e, :, :],
                                          n_kf[:, j, half, S * e:S * e + S].unsqueeze(1).broadcast_to([128, 8, S]),
                                          n_hm[:].unsqueeze(2).broadcast_to([128, 8, S]), ALU.mult)
            ins.then_inc(n_kmr.sem, 1)

        def weigh(base, t, j, ns):
            pool.wait_ge(n_rr.sem, n_rr.at(base + t + 1))
            e4 = n_e[:, j, 0:2 * ns * CHUNK].rearrange("p (h k) -> p h k", k=S)
            p.tensor_tensor(e4, e4, n_r[:, j, 0:ns * H].unsqueeze(2).broadcast_to([TILE, ns * H, S]), ALU.mult
                            ).then_inc(n_p.sem, 1)

        for layer, ns in ((0, 2), (1, 1)):
            base = layer * NT
            if layer == 1 and stages < 5:
                return
            if layer == 1:
                pool.wait_ge(n_proj.sem, n_proj.at(2 * base))
            stationary(base, 0, 0, ns)
            weigh(base, 0, 0, ns)
            with pool.Fori(0, NT // 2 - 1) as i:
                for j in range(2):
                    stationary(base, 2 * i + j + 1, 1 - j, ns)
                    weigh(base, 2 * i + j + 1, 1 - j, ns)
            stationary(base, NT - 1, 1, ns)
            weigh(base, NT - 1, 1, ns)
            norm(4 + layer)
        if stages < 6:
            return

        pool.wait_ge(xt_rdy.sem, xt_rdy.at(6 * NT))
        p.memset(e_z[:], 0.0).then_inc(e_zr.sem, 1)
        with pool.Fori(0, NT // 2) as i:
            for j in range(2):
                t = 2 * i + j
                pool.wait_ge(r_mm.sem, r_mm.at(t - 1))
                p.tensor_copy(r_xf[:, j, :, :], x_feat[:, :, bass.ds(TILE * t, TILE)]).then_inc(r_cp.sem, 1)
        with pool.Fori(0, NCH) as c:
            with pool.Fori(0, NEX // 2) as i:
                for j in range(2):
                    u = NEX * c + 2 * i + j
                    pool.wait_ge(e_sl.sem, e_sl.at(u + 1))
                    pool.wait_ge(e_tld[j].sem, e_tld[j].at(8 * (u - j) + 16))
                    pool.wait_ge(e_hr.sem, e_hr.at(u - 1))
                    p.tensor_tensor(e_aw[:, j, :], e_act[:, j, :], e_tw[:, j, :], ALU.mult).then_inc(e_awr.sem, 1)
        norm(6)

    @block.tensor
    def _(pe):
        mm = nc.tensor.matmul

        def take_waits():
            pe.sem_inc(pe_passed.sem, 1)

        def norm(k):
            if k == stages:
                return
            with pe.Fori(0, NT // 2) as i:
                for j in range(2):
                    t = 2 * i + j
                    pe.wait_ge(xn_rdy.sem, xn_rdy.at(k * NT + t + 1))
                    pe.wait_ge(xt_rdy.sem, xt_rdy.at(k * NT + t - 1))
                    for q in range(KD):
                        ins = nc.tensor.transpose(ps[:, XT[j], TILE * q:TILE * q + TILE],
                                                  xn[:, j, 128 * q:128 * q + 128], ident[0:TILE, 0:TILE])
                    ins.then_inc(xt_mm.sem, 1)

        pe.wait_ge(c_ld.sem, c_ld.at(48))
        norm(0)

        pe.wait_ge(w_ld[0].sem, w_ld[0].at(9 * 16))
        for c in range(NCH):
            pe.wait_ge(xt_rdy.sem, xt_rdy.at(TPC * (c + 1)))
            for k in range(KD):
                ins = mm(ps[0:DI, c, 0:CHUNK], m_in[:, k, :], x_feat[:, k, CHUNK * c:CHUNK * c + CHUNK],
                         start=k == 0, stop=k == KD - 1)
            ins.then_inc(m_mm.sem, 1)
        pe.wait_ge(m_silu.sem, m_silu.at(1))
        pe.wait_ge(m_ev.sem, m_ev.at(NCH))
        for c in range(NCH):
            mm(ps[0:DTR + 2 * NS, c, 0:CHUNK], m_xp[:], m_u[:, CHUNK * c:CHUNK * c + CHUNK],
               start=True, stop=True).then_inc(m_mm.sem, 1)
        for c in range(NCH):
            pe.wait_ge(m_dbc_ev.sem, m_dbc_ev.at(c + 1))
            mm(ps[0:DI, 4 + c, 0:CHUNK], m_dt[:], m_dbc[0:DTR, CHUNK * c:CHUNK * c + CHUNK],
               start=True, stop=True).then_inc(m_mm.sem, 1)
        pe.wait_ge(m_silu.sem, m_silu.at(2))
        for c in range(NCH):
            mm(ps[0:DI, c, 0:CHUNK], ident[0:DI, 0:DI], m_ud[:, CHUNK * c:CHUNK * c + CHUNK],
               start=True, stop=False, skip_group_check=True)

        def add_state(n, j, last):
            pe.wait_ge(m_hc.sem, m_hc.at(n + 1))
            for c in range(NCH):
                ins = mm(ps[0:DI, c, 0:CHUNK], ident[0:DI, 0:DI], m_h[:, j, CHUNK * c:CHUNK * c + CHUNK],
                         start=False, stop=last, skip_group_check=True)
            ins.then_inc(m_ymm.sem, 1)

        with pe.Fori(0, NS // 2 - 1) as i:
            for j in range(2):
                add_state(2 * i + j, j, False)
        add_state(NS - 2, 0, False)
        add_state(NS - 1, 1, True)
        pe.wait_ge(m_dl.sem, m_dl.at(2))
        with pe.Fori(0, NT // 2) as i:
            for j in range(2):
                t = 2 * i + j
                pe.wait_ge(m_yev.sem, m_yev.at(t + 1))
                pe.wait_ge(tail_used.sem, tail_used.at(t - 1))
                mm(ps[0:TILE, TAIL[j], 0:D], m_y[:, j, :], m_out[:], start=True, stop=True).then_inc(tail_rdy.sem, 1)
        norm(1)
        if stages < 2:
            return

        pe.wait_ge(xt_rdy.sem, xt_rdy.at(2 * NT))
        with pe.Fori(0, H // 2) as i:
            for j in range(2):
                pe.wait_ge(a_ld[j].sem, a_ld[j].at(96 * (i + 1)))
                pe.wait_ge(a_prep_ev.sem, a_prep_ev.at(2 * i + j))
                for k in range(KD):
                    mm(ps[:, 6, DCQ * k:DCQ * k + DCQ], a_wq[:, j, 128 * k:128 * k + 128], a_wkq[:, j, :],
                       start=True, stop=True)
                for k in range(2):
                    mm(ps[0:HALFQ, 7, DC * k:DC * k + DC], a_wqr[:, j, HALFQ * k:HALFQ * k + HALFQ], a_wkr[:, j, :],
                       start=True, stop=True)
                mm(ps[64 * j:64 * j + 64, 7, 256:512], a_wkv[:, j, :], a_wo[:, j, :], start=True, stop=True
                   ).then_inc(a_prep.sem, 1)

            def latent(j, c):
                u, q = 8 * i + 4 * j + c, c % 2
                pe.wait_ge(a_prep_ev.sem, a_prep_ev.at(2 * i + j + 1))
                pe.wait_ge(a_pr.sem, a_pr.at(u - 1))
                for half in range(2):
                    for k in range(KD):
                        ins = mm(ps[0:HALFQ, 2 * q + half, 0:CHUNK], a_wf[:, j, k, HALFQ * half:HALFQ * half + HALFQ],
                                 x_feat[:, k, CHUNK * c:CHUNK * c + CHUNK], start=k == 0, stop=k == KD - 1)
                ins.then_inc(a_qb.sem, 1)

            def query(j, c):
                u, q = 8 * i + 4 * j + c, c % 2
                pe.wait_ge(a_rt.sem, a_rt.at(u + 1))
                pe.wait_ge(a_qev.sem, a_qev.at(u - 1))
                for half in range(2):
                    ins = mm(ps[0:DC, 4 + q, 0:CHUNK], a_w2[:, j, half, :], a_rot[:, q, half, :],
                             start=half == 0, stop=half == 1)
                ins.then_inc(a_qq.sem, 1)

            for u in range(2 * NCH):
                latent(u // NCH, u % NCH)
                if u:
                    query((u - 1) // NCH, (u - 1) % NCH)
            query(1, NCH - 1)

        def key_transposes(nb, nj):
            pe.wait_ge(b_kvr_rdy.sem, b_kvr_rdy.at(nb + 1))
            pe.wait_ge(b_row.sem, b_row.at(3 * nb))
            for r in range(3):
                for q in range(4):
                    ins = nc.tensor.transpose(ps[0:DC + 1, r, KP * q:KP * q + KP], b_kvr[:, nj, 4 * r + q, :],
                                              ident[0:KP, 0:KP])
                ins.then_inc(b_rmm.sem, 1)

        def row_scores(nb, nj, i):
            pe.wait_ge(b_q_rdy.sem, b_q_rdy.at(nb + 1))
            for r in range(3):
                if i == 0:
                    pe.wait_ge(b_ktev.sem, b_ktev.at(3 * nb + r + 1))
                else:
                    pe.wait_ge(b_mxd.sem, b_mxd.at(24 * nb + 3 * (i - 1) + r + 1))
                mm(ps[0:TILE, r, 0:4 * KP], b_q[0:DC, nj, TILE * i:TILE * i + TILE],
                   b_kt[0:DC, nj, 4 * KP * r:4 * KP * r + 4 * KP], start=True, stop=True).then_inc(b_rmm.sem, 1)

        def maxima_rows(nb, nj):
            pe.wait_ge(b_mxc.sem, b_mxc.at(nb + 1))
            for r, n in enumerate((3, 3, 2)):
                for q in range(n):
                    ins = mm(ps[0:1, r, TILE * q:TILE * q + TILE], b_mx[:, nj, 3 * r + q:3 * r + q + 1],
                             ident[0:TILE, 0:TILE], start=True, stop=True)
                ins.then_inc(b_rmm.sem, 1)

        def key_scores(b, j, c):
            for g in range(2):
                pe.wait_ge(b_exp.sem, b_exp.at(2 * KC * b + 2 * c + g - 2))
                mm(ps[0:KP, 3 + (2 * c + g) % 3, 0:CHUNK], b_kt[:, j, KP * c:KP * c + KP],
                   b_q[:, j, CHUNK * g:CHUNK * g + CHUNK], start=True, stop=True).then_inc(b_st.sem, 1)

        def values(b, j, c):
            pe.wait_ge(b_exp.sem, b_exp.at(2 * KC * b + 2 * c + 2))
            if c == 0:
                pe.wait_ge(b_cev.sem, b_cev.at(2 * b))
            for i in range(H // 2):
                ins = mm(ps[0:TILE, 6 + i // 4, (DC + 1) * (i % 4):(DC + 1) * (i % 4) + DC + 1],
                         b_pt[:, c % 3, TILE * i:TILE * i + TILE], b_kvr[:, j, c, :],
                         start=c == 0 and i % 4 == 0, stop=c == KC - 1, skip_group_check=True)
            ins.then_inc(b_pv.sem, 1)

        def sequence(b, j, nb):
            pe.wait_ge(b_row.sem, b_row.at(3 * (b + 1)))
            for c in range(KC):
                key_scores(b, j, c)
                if nb is not None:
                    if c == 0:
                        key_transposes(nb, 1 - j)
                    elif c <= 8:
                        row_scores(nb, 1 - j, c - 1)
                    elif c == 10:
                        maxima_rows(nb, 1 - j)
                if c:
                    values(b, j, c - 1)
            values(b, j, KC - 1)

        pe.wait_ge(b_one.sem, b_one.at(1))
        key_transposes(0, 0)
        for i in range(8):
            row_scores(0, 0, i)
        maxima_rows(0, 0)
        with pe.Fori(0, NSEQ // 2 - 1) as i:
            for j in range(2):
                sequence(2 * i + j, j, 2 * i + j + 1)
        sequence(NSEQ - 2, 0, NSEQ - 1)
        sequence(NSEQ - 1, 1, None)
        with pe.Fori(0, NT // 2) as i:
            for j in range(2):
                t = 2 * i + j
                pe.wait_ge(c_in[j].sem, c_in[j].at(16 * (i + 1)))
                pe.wait_ge(c_tev.sem, c_tev.at(t - 1))
                for q in range(H // 2):
                    ins = nc.tensor.transpose(ps[:, 2 * j + q // 4, TILE * (q % 4):TILE * (q % 4) + TILE],
                                              c_ctx[:, j, 128 * q:128 * q + 128], ident[0:TILE, 0:TILE])
                ins.then_inc(c_tr.sem, 1)
            for j in range(2):
                t = 2 * i + j
                pe.wait_ge(c_tev.sem, c_tev.at(t + 1))
                pe.wait_ge(tail_used.sem, tail_used.at(NT + t - 1))
                for q in range(H // 2):
                    ins = mm(ps[0:TILE, TAIL[j], 0:D], c_ctxT[:, j, q, :], w3[:, q, :],
                             start=q == 0, stop=q == H // 2 - 1)
                ins.then_inc(tail_rdy.sem, 1)
        norm(2)
        if stages < 3:
            return

        pe.wait_ge(xt_rdy.sem, xt_rdy.at(3 * NT))
        pe.wait_ge(w_ld[2].sem, w_ld[2].at(7 * 16))
        with pe.Fori(0, NCH) as c:
            for b in range(FB):
                q, m = b % 2, (128 if b < 5 else 64)
                pe.wait_ge(f_sl.sem, f_sl.at(FB * c + b - 1))
                pe.wait_ge(f_hr.sem, f_hr.at(FB * c + b - 1))
                if m < 128:
                    take_waits()
                for w, bank in ((f_g, q), (f_u, 2 + q)):
                    for k in range(KD):
                        ins = mm(ps[0:m, bank, 0:CHUNK], w[:, k, 128 * b:128 * b + m],
                                 x_feat[:, k, bass.ds(CHUNK * c, CHUNK)], start=k == 0, stop=k == KD - 1)
                ins.then_inc(f_gu.sem, 1)
            pe.wait_ge(f_hr.sem, f_hr.at(FB * (c + 1)))
            for s in range(TPC):
                pe.wait_ge(tail_used.sem, tail_used.at(2 * NT + TPC * c + s - 1))
                for b in range(FB):
                    m = 128 if b < 5 else 64
                    ins = mm(ps[0:TILE, TAIL[s % 2], 0:D], f_h[0:m, b, TILE * s:TILE * s + TILE], f_d[0:m, b, :],
                             start=b == 0, stop=b == FB - 1)
                ins.then_inc(tail_rdy.sem, 1)
        norm(3)
        if stages < 4:
            return

        def scores(base, t, j, ns):
            first = isinstance(t, int) and t == 0
            pe.wait_ge(n_te.sem, n_te.at(turned(2 - ns, 0) if first else turned(2 - ns, t - 1)))
            for q in range(2 * ns):
                for k in range(KD):
                    w = n_w[:, q // 2, k, :] if ns == 2 else z_wq[:, k, :]
                    ins = mm(ps[:, 0, TILE * q:TILE * q + TILE], w[:, 128 * (q % 2):128 * (q % 2) + 128],
                             x_feat[:, k, bass.ds(TILE * t, TILE)], start=k == 0, stop=k == KD - 1)
            ins.then_inc(n_proj.sem, 1)
            pe.wait_ge(n_ke.sem, n_ke.at(base + t))
            pe.wait_ge(n_ye.sem, n_ye.at(base if first else base + t - 1))
            if ns == 2:
                pe.wait_ge(n_le.sem, n_le.at(t))
                for q in range(2):
                    for k in range(KD):
                        mm(ps[:, 1, TILE * q:TILE * q + TILE], n_w[:, 2, k, 128 * q:128 * q + 128],
                           x_feat[:, k, bass.ds(TILE * t, TILE)], start=k == 0, stop=k == KD - 1)
                pe.wait_ge(n_xfr.sem, n_xfr.at(base + t + 1))
                pe.wait_ge(n_ve.sem, n_ve.at(base + t))
                for k in range(KD):
                    mm(ps[0:TILE, 1, 2 * TILE:2 * TILE + H], n_xf[:, j, k, :], n_lam[:, k, :],
                       start=k == 0, stop=k == KD - 1)
            else:
                for q in range(2):
                    mm(ps[:, 1, TILE * q:TILE * q + TILE], z_wkv[:, 128 * q:128 * q + 128],
                       z_ctx[:, bass.ds(TILE * t, TILE)], start=True, stop=True)
                pe.wait_ge(n_xfr.sem, n_xfr.at(base + t + 1))
                pe.wait_ge(n_ve.sem, n_ve.at(base + t))
                take_waits()
            for e in range(2):
                if ns == 2:
                    for k in range(KD):
                        ins = mm(ps[0:S, 2, D * e:D * e + D], n_xf[:, j, k, S * e:S * e + S], n_w[:, 3, k, :],
                                 start=k == 0, stop=k == KD - 1)
                else:
                    ins = mm(ps[0:S, 2, D * e:D * e + D], n_xf[0:DC, j, 0, S * e:S * e + S], z_wkv[:, D:2 * D],
                             start=True, stop=True)
            ins.then_inc(n_proj.sem, 1)
            pe.wait_ge(n_qe.sem, n_qe.at(base + t + 1))
            pe.wait_ge(n_kmr.sem, n_kmr.at(base + t + 1))
            pe.wait_ge(n_sub.sem, n_sub.at(base + t))
            for q in range(2 * ns):
                o = ps[0:TILE, 3 + q, 0:CHUNK]
                for e in range(2):
                    mm(o, n_qz[:, j, q, e, :], n_km[:, j, 2 * (q // 2 if ns == 2 else q) + e, :, :].rearrange("p h k -> p (h k)"),
                       start=e == 0, stop=False)
                ins = mm(o, ident_bf[:], n_caus_bf[:].rearrange("p h k -> p (h k)"), start=False, stop=True)
            ins.then_inc(n_sc.sem, 1)

        def attend(layer, t, j, ahead):
            base = layer * NT
            sets = 2 - layer
            for g in range(4 * sets):
                if g == 0:
                    pe.wait_ge(n_p.sem, n_p.at(base + t + 1))
                    pe.wait_ge(n_qe.sem, n_qe.at(base + t + 1 + ahead))
                    pe.wait_ge(n_ve.sem, n_ve.at(base + t + 1 + ahead))
                    take_waits()
                if g >= 2:
                    pe.wait_ge(n_te.sem, n_te.at(turned(layer, t) + g - 1))
                    take_waits()
                for q in range(4):
                    ins = nc.tensor.transpose(ps[0:S, 2 * (g % 2), TILE * q:TILE * q + TILE],
                                              n_e[:, j, S * (4 * g + q):S * (4 * g + q) + S], ident[0:TILE, 0:TILE])
                ins.then_inc(n_tr.sem, 1)
            pe.wait_ge(n_te.sem, n_te.at(turned(layer, t) + 4 * sets))
            pe.wait_ge(n_ke.sem, n_ke.at(base + t + 1 + ahead))
            if layer == 0:
                pe.wait_ge(n_le.sem, n_le.at(t + 1 + ahead))
            pe.wait_ge(n_ye.sem, n_ye.at(base + t))
            take_waits()
            for slot in range(0, H, 2):
                r, col = 32 * ((slot // 2) % 4), 256 + TILE * (slot // 8)
                for e in range(2):
                    for o in range(2 * sets):
                        at = slot + o % 2 + H * (o // 2)
                        head = 8 * (o // 2) + at % 8 if sets == 2 else at
                        ins = mm(ps[r:r + 32, 1, col + S * e:col + S * e + S], n_v[:, j, e, head, :],
                                 n_pt[:, at // 4, TILE * (at % 4) + S * e:TILE * (at % 4) + S * e + S],
                                 start=o == 0, stop=o == 2 * sets - 1)
            ins.then_inc(n_pvm.sem, 1)
            pe.wait_ge(n_ye.sem, n_ye.at(base + t + 1))
            pe.wait_ge(tail_used.sem, tail_used.at((3 + layer) * NT + t))
            wo = n_wo if layer == 0 else z_wo
            for k in range(KD):
                ins = mm(ps[0:TILE, 7, 0:D], n_yt[:, j, k, :], wo[:, k, :], start=k == 0, stop=k == KD - 1)
            ins.then_inc(tail_rdy.sem, 1)

        pe.wait_ge(w_ld[3].sem, w_ld[3].at(12 * 16))
        pe.wait_ge(n_zero.sem, n_zero.at(3))
        pe.wait_ge(n_cst.sem, n_cst.at(2))
        for layer, ns in ((0, 2), (1, 1)):
            base = layer * NT
            if layer == 1 and stages < 5:
                return
            pe.wait_ge(xt_rdy.sem, xt_rdy.at((4 + layer) * NT))
            scores(base, 0, 0, ns)
            with pe.Fori(0, NT // 2 - 1) as i:
                for j in range(2):
                    scores(base, 2 * i + j + 1, 1 - j, ns)
                    attend(layer, 2 * i + j, j, 1)
            scores(base, NT - 1, 1, ns)
            attend(layer, NT - 2, 0, 1)
            attend(layer, NT - 1, 1, 0)
            norm(4 + layer)
        if stages < 6:
            return

        pe.wait_ge(w_ld[5].sem, w_ld[5].at(4 * 16))
        with pe.Fori(0, NT // 2) as i:
            for j in range(2):
                t = 2 * i + j
                pe.wait_ge(r_cp.sem, r_cp.at(t + 1))
                for k in range(KD):
                    ins = mm(ps[0:TILE, 0, bass.ds(NE * t, NE)], r_xf[:, j, k, :], r_w[:, k, :],
                             start=k == 0, stop=k == KD - 1)
                ins.then_inc(r_mm.sem, 1)
        pe.wait_ge(r_sel.sem, r_sel.at(1))
        for c in range(NCH):
            for s in range(TPC):
                ins = nc.tensor.transpose(ps[0:NE, c, TILE * s:TILE * s + TILE], r_m2[:, TPC * c + s, :],
                                          ident[0:TILE, 0:TILE])
            ins.then_inc(r_tr.sem, 1)

        pe.wait_ge(r_te.sem, r_te.at(NCH))
        pe.wait_ge(e_zr.sem, e_zr.at(1))
        with pe.Fori(0, NCH) as c:
            def gate_up(e, j):
                u = NEX * c + e
                pe.wait_ge(e_ld[j].sem, e_ld[j].at(8 * (u - j) + 16))
                pe.wait_ge(e_sl.sem, e_sl.at(u - 1))
                pe.wait_ge(e_hr.sem, e_hr.at(u - 1))
                for w in range(2):
                    for k in range(KD):
                        ins = mm(ps[:, 2 * w + j, 0:CHUNK], e_wgu[:, j, D * w + 128 * k:D * w + 128 * k + 128],
                                 x_feat[:, k, bass.ds(CHUNK * c, CHUNK)], start=k == 0, stop=k == KD - 1)
                ins.then_inc(e_gu.sem, 1)

            def down(e, j, last=False):
                pe.wait_ge(e_dld[j].sem, e_dld[j].at(8 * (NEX * c + e - j) + 16))
                pe.wait_ge(e_hr.sem, e_hr.at(NEX * c + e + 1))
                for g in range(2):
                    ins = mm(ps[:, 4 + g, 0:CHUNK], e_wd[:, j, 128 * g:128 * g + 128], e_h[:, j, :],
                             start=False, stop=last, skip_group_check=True)
                ins.then_inc(e_dn.sem, 1)

            pe.wait_ge(e_yev.sem, e_yev.at(2 * c))
            for g in range(2):
                mm(ps[:, 4 + g, 0:CHUNK], e_z[:, 0:128], e_z[:], start=True, stop=False, skip_group_check=True)
            gate_up(0, 0)
            with pe.Fori(0, NEX // 2 - 1) as i:
                gate_up(2 * i + 1, 1)
                down(2 * i, 0)
                gate_up(2 * i + 2, 0)
                down(2 * i + 1, 1)
            gate_up(NEX - 1, 1)
            down(NEX - 2, 0)
            down(NEX - 1, 1, True)
            pe.wait_ge(e_yev.sem, e_yev.at(2 * (c + 1)))
            for s in range(TPC):
                pe.wait_ge(tail_used.sem, tail_used.at(5 * NT + TPC * c + s - 1))
                for g in range(2):
                    ins = nc.tensor.transpose(ps[0:TILE, 6 + s % 2, 128 * g:128 * g + 128],
                                              e_y[:, g, TILE * s:TILE * s + TILE], ident[:])
                ins.then_inc(tail_rdy.sem, 1)
        norm(6)

    stack.close()


def _rope(length, dim):
    inv = (1.0 / np.float32(10000.0) ** (np.arange(0, dim, 2, dtype=np.float32) / np.float32(dim))).astype(np.float32)
    f = np.arange(length, dtype=np.float32)[:, None] * inv[None, :]
    return np.repeat(np.sin(f), 2, axis=-1), np.repeat(np.cos(f), 2, axis=-1)


def _tables():
    sq, cq = _rope(S, DCQ)
    ropeq = np.stack([cq[:, :HALFQ].T, sq[:, :HALFQ].T, cq[:, HALFQ:].T, sq[:, HALFQ:].T], axis=1)
    sk, ck = _rope(LK, DC)
    signed = np.concatenate([-sk[:, :DC // 2], sk[:, DC // 2:]], axis=-1)
    ropek = np.stack([ck.reshape(KP, KC, DC), signed.reshape(KP, KC, DC)], axis=1)
    q = np.arange(TILE)[:, None] % S
    return {"c_ident": np.eye(128, dtype=np.float32),
            "c_ropeq": ropeq, "c_ropek": ropek,
            "c_headmask": (np.arange(128)[:, None] // HD == np.arange(8)[None, :]).astype(np.float32),
            "c_causal": np.where(np.arange(S)[None, :] <= q, 0.0, NEG).astype(np.float32),
            "c_lower": (np.arange(NG)[None, :] < np.arange(NG)[:, None]).astype(np.float32),
            "c_ones": np.ones((NEX - NE, T), np.float32)}


def kernel(**inputs):
    import concourse.bacc as bacc
    from concourse.bass_utils import run_bass_kernel_spmd

    g = {k: np.asarray(v) for k, v in inputs.items()}
    m, z, f = (lambda n: g["L0_attn_" + n]), (lambda n: g["L0_xattn_" + n]), (lambda n: g["L0_ffn_" + n])
    n, y, e = (lambda k: g["L1_attn_" + k]), (lambda k: g["L1_xattn_" + k]), (lambda k: g["L1_ffn_" + k])
    split = lambda w: w.reshape(w.shape[0], KD, 128, -1).transpose(0, 2, 1, 3).reshape(w.shape[0], 128, -1)
    shared = lambda w: w.reshape(D, 2, IE).transpose(1, 0, 2)
    order = np.r_[0:H:2, 1:H:2]
    even_first = lambda w: w.reshape(D, H, HD)[:, order].reshape(D, D)
    blocks = lambda w: np.pad(w, (0, FB * 128 - INTER)).reshape(FB, 128).T
    gates = split(np.concatenate([e("w_gate"), shared(e("sw_gate"))]))
    ups = split(np.concatenate([e("w_up"), shared(e("sw_up"))]))
    downs = np.concatenate([e("w_down"), e("sw_down").reshape(2, IE, D)])
    laid = {
        "x": g["x"].reshape(T, D), "ctx": g["ctx_512"],
        "ctx_head_T": g["ctx_512"][:, :S].transpose(2, 0, 1).reshape(DC, T),
        "ln_w": m("ln_w").reshape(KD, 128).T, "ln_b": m("ln_b").reshape(KD, 128).T,
        "in_proj_T": m("in_proj_W").T, "conv_w": m("conv_w")[:, 0, :], "conv_b": m("conv_b")[:, None],
        "x_proj_T": m("x_proj_W").T, "dt_proj_T": m("dt_proj_W").T, "dt_proj_b": m("dt_proj_b")[:, None],
        "A_log": m("A_log"), "D_param": m("D_param")[:, None], "out_proj_T": m("out_proj_W").T,
        "Wq": z("Wq").reshape(H, 128, D), "w_kc_q": z("w_kc_q"), "W_qr_T": z("W_qr").transpose(0, 2, 1),
        "W_kr_T": z("W_kr").transpose(0, 2, 1), "w_kc_kv": z("w_kc_kv"), "Wo_T": z("Wo").T.reshape(H, 128, D),
        "gate_T": f("gate_w").T, "up_T": f("up_w").T, "down_T": f("down_w").T,
        "gate_s": blocks(f("gate_s")), "up_s": blocks(f("up_s")), "down_s": f("down_s"),
        "N_Wq1": even_first(n("Wq1")), "N_Wq2": even_first(n("Wq2")), "N_Wk": n("Wk"), "N_Wv": n("Wv"),
        "N_Wlam": n("Wlam")[:, order], "N_Wo": even_first(n("Wo").T).T,
        "Z_Wq_T": y("Wq").T, "Z_Wkv_T": y("Wkv_expand").T, "Z_Wout_T": y("Wout").T,
        "router_w": e("router_w"), "router_bias": e("router_bias"),
        "W_exp": np.concatenate([gates, ups, downs], axis=2),
    }
    laid.update(_tables())
    nc = bacc.Bacc("TRN2", target_bir_lowering=False, num_devices=1)
    arrays, aps = {}, {}
    for name, arr in laid.items():
        arr = np.ascontiguousarray(arr)
        arrays["in_" + name] = arr
        aps[name] = nc.dram_tensor("in_" + name, arr.shape, mybir.dt.from_np(arr.dtype), kind="ExternalInput").ap()
    out = nc.dram_tensor("out_x", (T, D), F32, kind="ExternalOutput").ap()
    build(nc, aps, out)
    r = run_bass_kernel_spmd(nc, [arrays], core_ids=[0])
    return r.results[0]["out_x"].reshape(NSEQ, S, D)
```

```python
import numpy as np

import concourse.bass as bass
from concourse import mybir
from concourse.alu_op_type import AluOpType as ALU

F32 = mybir.dt.float32
F32R = mybir.dt.float32r
BF16 = mybir.dt.bfloat16
ACT = mybir.ActivationFunctionType
AX = mybir.AxisListType

NSEQ, S, D = 32, 56, 256
T = NSEQ * S
TILE = 2 * S
NT = T // TILE
CHUNK = 8 * S
NCH = T // CHUNK
TPC = CHUNK // TILE
KD = D // 128
EPS = 1e-5

DI, NS, DTR, KW = 96, 16, 6, 3
H = 16
LK, DC, DCQ = 1500, 64, 192
KP, KC = 125, 12
HALFQ = DCQ // 2
MROW = 96
NQ = H * S
INTER = 704
FB = 6
HD = D // H
NE, NEX, NG, TOPG, TOPK, IE = 32, 34, 8, 4, 8, 128
ROUTED_SCALE = 2.5
NEG = -1e30
ATANH = [2.00000001, 0.66666316, 0.40024854, 0.27961419, 0.28174657]


class Signal:

    def __init__(self, nc, name, credit=0):
        self.sem, self.credit = nc.alloc_semaphore(name), credit

    def at(self, count):
        return count + self.credit


class Chain:

    def __init__(self, nc, name):
        self.sem, self.base, self.n = nc.alloc_semaphore(name), 0, 0

    def one(self):
        self.n += 1
        return 1

    def all(self):
        return self.base + self.n

    def enter(self, i, per):
        self.start = self.base + self.n
        self.base, self.n, self.per = self.start + i * per, 0, per

    def leave(self, times):
        assert self.n == self.per, (self.n, self.per)
        self.base, self.n = self.start + times * self.per, 0


def build(nc, a, out, stages=6):
    cursor = [((nc.sbuf_base + 63) // 64) * 64]

    def sb(name, shape, dt=F32):
        size = int(np.prod(shape[1:])) * (2 if dt == BF16 else 4)
        size = (size + 63) // 64 * 64
        h = nc.alloc_sbuf_tensor_at(name, shape, dt, offset=cursor[0])
        cursor[0] += size
        return h

    def sig(name, credit=0):
        s = Signal(nc, name, credit)
        if credit:
            rings.append(s)
        return s

    rings = []
    ps = nc.alloc_psum_tensor("ps", [128, 8, 512], F32)

    x_tok = sb("x_tok", [TILE, NT, D])
    feat_base = cursor[0]
    x_feat = sb("x_feat", [128, KD, T])
    ident = sb("ident", [128, 128])
    xn_base = cursor[0]
    xn = sb("xn", [TILE, 2, D])
    ln_stats = sb("ln_stats", [TILE, NT, 6])
    ln_a = sb("ln_a", [TILE, NT])
    ln_b = sb("ln_b", [TILE, NT])
    ln_d = sb("ln_d", [TILE, NT])
    ln_sq = sb("ln_sq", [TILE, NT])
    ln_mean = sb("ln_mean", [TILE, NT])
    ln_var = sb("ln_var", [TILE, NT])
    ln_std = sb("ln_std", [TILE, NT])
    ln_rstd = sb("ln_rstd", [TILE, NT])
    phase_base = cursor[0]

    m_lnw = sb("m_lnw", [128, KD])
    m_lnb = sb("m_lnb", [128, KD])
    m_in = sb("m_in", [128, KD, DI])
    m_cw = sb("m_cw", [DI, KW])
    m_cb = sb("m_cb", [DI, 1])
    m_xp = sb("m_xp", [DI, DTR + 2 * NS])
    m_dt = sb("m_dt", [DTR, DI])
    m_dtb = sb("m_dtb", [DI, 1])
    m_al = sb("m_al", [DI, NS])
    m_a = sb("m_a", [DI, NS])
    m_dp = sb("m_dp", [DI, 1])
    m_out = sb("m_out", [DI, D])
    m_pad = sb("m_pad", [DI, NSEQ, S + 2])
    m_c = sb("m_c", [DI, NSEQ, S])
    m_u = sb("m_u", [DI, T])
    m_t1 = sb("m_t1", [DI, T])
    m_t2 = sb("m_t2", [DI, T])
    m_delta = sb("m_delta", [DI, NSEQ, S])
    m_du = sb("m_du", [DI, T])
    m_ud = sb("m_ud", [DI, T])
    m_ud2 = sb("m_ud2", [DI, T])
    m_sq = sb("m_sq", [DI, T])
    m_dbc = sb("m_dbc", [DTR + 2 * NS, T])
    m_da = sb("m_da", [DI, 2, NSEQ, S])
    m_dbu = sb("m_dbu", [DI, 2, T])
    m_bb = sb("m_bb", [DI, 2, T])
    m_cc = sb("m_cc", [DI, 2, T])
    m_h = sb("m_h", [DI, 2, T])
    m_y = sb("m_y", [DI, 2, TILE])
    m_end = cursor[0]

    cursor[0] = phase_base
    q_all = sb("q_all", [128, H, T], F32R)
    w3 = sb("w3", [128, H // 2, D])
    after_q = cursor[0]
    a_whi = sb("a_whi", [128, 2, KD, DCQ], F32R)
    a_wlo = sb("a_wlo", [128, 2, KD, DCQ], F32R)
    a_w2 = sb("a_w2", [HALFQ, 2, 2, 2, DC])
    a_prod = sb("a_prod", [HALFQ, 2, 4, CHUNK])
    a_rot = sb("a_rot", [HALFQ, 2, 2, CHUNK])
    cursor[0] = xn_base
    a_rope = sb("a_rope", [HALFQ, 4, S])
    cursor[0] = m_end
    a_wq = sb("a_wq", [128, 2, D])
    a_wkq = sb("a_wkq", [128, 2, DCQ])
    a_wqr = sb("a_wqr", [64, 2, DCQ])
    a_wkr = sb("a_wkr", [64, 2, DC])
    a_wkv = sb("a_wkv", [128, 2, DC])
    a_wo = sb("a_wo", [128, 2, D])
    a_xhi = sb("a_xhi", [128, KD, T], F32R)
    cursor[0] = feat_base
    a_xlo = sb("a_xlo", [128, KD, T], F32R)
    cursor[0] = after_q
    b_q = sb("b_q", [128, 2, NQ], F32R)
    b_of = sb("b_of", [DC + 1, 2, CHUNK])
    b_klo = sb("b_klo", [128, 2, KC * KP], F32R)
    b_pt = sb("b_pt", [KP, 2, NQ])
    b_ctx = sb("b_ctx", [TILE, 2, H // 2, DC])
    b_kv = sb("b_kv", [KP, 2, KC, DC])
    b_rope = sb("b_rope", [KP, 2, KC, DC])
    b_tmp = sb("b_tmp", [KP, KC, DC])
    b_kvr = sb("b_kvr", [KP, 2, KC, DC + 1])
    cursor[0] = feat_base
    b_khi = sb("b_khi", [128, 2, KC * KP], F32R)
    b_mx3 = sb("b_mx3", [TILE, 2, H // 2, 3])
    b_mx = sb("b_mx", [TILE, 2, H // 2])
    b_rs = sb("b_rs", [TILE, 2, H // 2])
    cursor[0] = after_q
    c_ctx = sb("c_ctx", [TILE, 2, H * DC])
    c_ctxT = sb("c_ctxT", [128, 2, H // 2, TILE])

    f_g = sb("f_g", [128, KD, INTER])
    f_u = sb("f_u", [128, KD, INTER])
    f_d = sb("f_d", [128, FB, D])
    f_gs = sb("f_gs", [128, FB])
    f_us = sb("f_us", [128, FB])
    f_ds = sb("f_ds", [TILE, D])
    f_act = sb("f_act", [128, 2, CHUNK])
    f_h = sb("f_h", [128, FB, CHUNK])
    f_y = sb("f_y", [TILE, 2, D])

    cursor[0] = phase_base
    n_w = sb("n_w", [128, 4, KD, D])
    n_lam = sb("n_lam", [128, KD, H])
    n_wo = sb("n_wo", [128, KD, D])
    z_wq = sb("z_wq", [128, KD, D])
    z_wkv = sb("z_wkv", [DC, 2 * D])
    z_wo = sb("z_wo", [128, KD, D])
    z_ctx = sb("z_ctx", [DC, T])
    n_hm = sb("n_hm", [128, 8])
    n_caus = sb("n_caus", [TILE, S])
    ident_bf = sb("ident_bf", [TILE, TILE], BF16)
    n_caus_bf = sb("n_caus_bf", [TILE, 8, S], BF16)
    n_xf = sb("n_xf", [128, 2, KD, TILE])
    n_kf = sb("n_kf", [128, 2, 2, TILE])
    n_qz = sb("n_qz", [128, 2, 4, 2, TILE])
    n_km = sb("n_km", [128, 2, 4, 8, S])
    n_v = sb("n_v", [S, 2, 2, H, 2 * HD])
    n_e = sb("n_e", [TILE, 2, 4 * CHUNK])
    n_mx = sb("n_mx", [TILE, 2, 32])
    n_sum = sb("n_sum", [TILE, 2, 32])
    n_r = sb("n_r", [TILE, 2, 32])
    n_l = sb("n_l", [TILE, 2, 16])
    n_l2 = sb("n_l2", [TILE, 2, 16])
    n_l3 = sb("n_l3", [TILE, 2, 16])
    n_pt = sb("n_pt", [S, 8, CHUNK])
    n_yt = sb("n_yt", [128, 2, 2, TILE])

    assert cursor[0] <= after_q - 4 * (H // 2) * D, "the last block's output weights lie beyond"

    r_w = sb("r_w", [128, KD, NE])
    r_b = sb("r_b", [TILE, NE])
    r_lt = sb("r_lt", [TILE, NG, NG])
    r_xf = sb("r_xf", [128, 2, KD, TILE])
    r_s = sb("r_s", [TILE, NT, NE])
    r_sb = sb("r_sb", [TILE, NT, NE])
    r_hi = sb("r_hi", [TILE, NT, NG, 2])
    r_lo = sb("r_lo", [TILE, NT, NG, 2])
    r_g1 = sb("r_g1", [TILE, NT, NG])
    r_g2 = sb("r_g2", [TILE, NT, NG])
    r_g3 = sb("r_g3", [TILE, NT, NG])
    r_c1 = sb("r_c1", [TILE, NT, NG, NG])
    r_c2 = sb("r_c2", [TILE, NT, NG, NG])
    r_top = sb("r_top", [TILE, NT, 8])
    r_m = sb("r_m", [TILE, NT, NE])
    r_m2 = sb("r_m2", [TILE, NT, NE])
    r_den = sb("r_den", [TILE, NT])
    r_rden = sb("r_rden", [TILE, NT])
    r_wt = sb("r_wt", [NEX, T])
    e_wgu = sb("e_wgu", [128, 2, 2 * D])
    e_wd = sb("e_wd", [128, 2, D])
    e_tw = sb("e_tw", [128, 2, CHUNK])
    e_act = sb("e_act", [128, 2, CHUNK])
    e_aw = sb("e_aw", [128, 2, CHUNK])
    e_h = sb("e_h", [128, 2, CHUNK])
    e_z = sb("e_z", [1, CHUNK])
    e_y = sb("e_y", [128, 2, CHUNK])

    bc_dram = nc.dram_tensor("bc_rows", (2 * NS, T), F32, kind="Internal").ap()
    ctx_dram = nc.dram_tensor("ctx_rows", (T, H, DC), F32, kind="Internal").ap()
    rw_dram = nc.dram_tensor("route_rows", (NEX, T), F32, kind="Internal").ap()

    x_ld = sig("x_ld")
    tail_rdy = sig("tail_rdy", 2)
    tail_used = sig("tail_used", 2)
    ln_st = sig("ln_st")
    std_req, std_rdy = sig("std_req"), sig("std_rdy")
    xn_rdy = sig("xn_rdy")
    xt_mm = sig("xt_mm")
    xt_rdy = sig("xt_rdy")
    w_ld = [sig(f"w_ld{k}") for k in range(6)]
    c_ld = sig("c_ld")

    m_ev, m_mm = sig("m_ev"), sig("m_mm")
    m_padz, m_convd, m_exp, m_silu, m_abs, m_ln, m_dl = (sig(n) for n in (
        "m_padz", "m_convd", "m_exp", "m_silu", "m_abs", "m_ln", "m_dl"))
    m_dbc_ev, m_bc_st = sig("m_dbc_ev"), sig("m_bc_st")
    m_bld = [sig(f"m_bld{j}") for j in range(2)]
    m_cld = [sig(f"m_cld{j}") for j in range(2)]
    m_dbu_rdy, m_scan, m_hc, m_ymm = sig("m_dbu_rdy", 2), sig("m_scan", 2), sig("m_hc", 2), sig("m_ymm", 2)
    m_da_rdy, m_yev, m_az = sig("m_da_rdy"), sig("m_yev"), sig("m_az")

    a_ld = [sig(f"a_ld{j}") for j in range(2)]
    a_prep, a_prep_ev = sig("a_prep", 2), sig("a_prep_ev", 2)
    a_qb, a_pr, a_rt, a_qq, a_qev = sig("a_qb"), sig("a_pr", 2), sig("a_rt", 2), sig("a_qq", 2), sig("a_qev", 2)
    a_qhi, a_xh, a_xl, a_wl = sig("a_qhi"), sig("a_xh"), sig("a_xl"), sig("a_wl", 1)

    b_ld = [sig(f"b_ld{j}") for j in range(2)]
    b_kvr_rdy, b_q_rdy = sig("b_kvr_rdy", 1), sig("b_q_rdy")
    b_rmm = sig("b_rmm")
    b_ktev, b_klev, b_mxd, b_mxc, b_row = sig("b_ktev"), sig("b_klev"), sig("b_mxd"), sig("b_mxc"), sig("b_row")
    b_st, b_exp, b_pv, b_cev = sig("b_st", 1), sig("b_exp", 3), sig("b_pv", 2), sig("b_cev", 1)
    b_cst = [sig(f"b_cst{j}", 1) for j in range(2)]
    b_one, b_oev, b_otr = sig("b_one"), sig("b_oev", 1), sig("b_otr")
    c_in = [sig(f"c_in{j}") for j in range(2)]
    c_tr, c_tev = sig("c_tr", 2), sig("c_tev", 2)

    f_gu, f_sl, f_hr = sig("f_gu"), sig("f_sl", 2), sig("f_hr", 2)

    n_cst = sig("n_cst")
    n_qp, n_kp, n_vp = sig("n_qp"), sig("n_kp"), sig("n_vp", 2)
    n_zero = sig("n_zero")
    n_xfr, n_qe, n_ke, n_ve, n_kmr = sig("n_xfr"), sig("n_qe"), sig("n_ke"), sig("n_ve"), sig("n_kmr", 2)
    n_sc, n_sub, n_exp, n_rr, n_p = sig("n_sc", 2), sig("n_sub"), sig("n_exp"), sig("n_rr", 2), sig("n_p")
    n_tr, n_te, n_pvm, n_ye, n_le = sig("n_tr"), sig("n_te", 1), sig("n_pvm", 2), sig("n_ye", 1), sig("n_le")

    r_mm = sig("r_mm", 2)
    r_cp, r_ex, r_sel, r_tr, r_te, r_st = (sig(n) for n in ("r_cp", "r_ex", "r_sel", "r_tr", "r_te", "r_st"))
    e_ld = [sig(f"e_ld{j}") for j in range(2)]
    e_tld = [sig(f"e_tld{j}") for j in range(2)]
    e_dld = [sig(f"e_dld{j}") for j in range(2)]
    e_gu, e_sl, e_awr, e_hr, e_dn = sig("e_gu", 2), sig("e_sl", 2), sig("e_awr", 2), sig("e_hr", 2), sig("e_dn", 2)
    e_yev, e_zr = sig("e_yev", 1), sig("e_zr")
    pe_passed = sig("pe_passed")
    out_st = sig("out_st")

    import contextlib
    stack = contextlib.ExitStack()
    block = stack.enter_context(nc.Block())

    def turned(layer, t):
        return 8 * t if layer == 0 else 8 * NT + 4 * t

    TAIL = [4, 5]
    XT = [6, 7]

    @block.sync
    def _(sp):
        def store_result():
            for c in range(NCH):
                sp.wait_ge(xn_rdy.sem, xn_rdy.at(stages * NT + TPC * (c + 1)))
                sp.dma_start(out.rearrange("(t p) d -> p t d", p=TILE)[:, TPC * c:TPC * c + TPC, :],
                             x_tok[:, TPC * c:TPC * c + TPC, :]).then_inc(out_st.sem, 16)
            sp.wait_ge(out_st.sem, out_st.at(16 * NCH))

        for s in rings:
            sp.sem_inc(s.sem, s.credit)
        sp.dma_start(x_tok[:], a["x"].rearrange("(t p) d -> p t d", p=TILE)).then_inc(x_ld.sem, 16)
        for dst, src in ((ident[:], a["c_ident"]), (m_lnw[:], a["ln_w"]), (m_lnb[:], a["ln_b"])):
            sp.dma_start(dst, src).then_inc(c_ld.sem, 16)
        for dst, src in ((m_in[:], a["in_proj_T"].rearrange("(k p) n -> p k n", p=128)),
                         (m_cw[:], a["conv_w"]), (m_cb[:], a["conv_b"]), (m_xp[:], a["x_proj_T"]),
                         (m_dt[:], a["dt_proj_T"]), (m_dtb[:], a["dt_proj_b"]), (m_al[:], a["A_log"]),
                         (m_dp[:], a["D_param"]), (m_out[:], a["out_proj_T"])):
            sp.dma_start(dst, src).then_inc(w_ld[0].sem, 16)

        sp.wait_ge(m_dbc_ev.sem, m_dbc_ev.at(NCH))
        sp.dma_start(bc_dram, m_dbc[DTR:DTR + 2 * NS, :]).then_inc(m_bc_st.sem, 16)
        sp.wait_ge(m_bc_st.sem, m_bc_st.at(16))
        with sp.Fori(0, NS // 2) as i:
            for j in range(2):
                n = 2 * i + j
                sp.wait_ge(m_dbu_rdy.sem, m_dbu_rdy.at(n - 1))
                sp.dma_start(m_bb[:, j, :], bc_dram[n].partition_broadcast(DI)).then_inc(m_bld[j].sem, 16)
                sp.wait_ge(m_hc.sem, m_hc.at(n - 1))
                sp.dma_start(m_cc[:, j, :], bc_dram[n + NS].partition_broadcast(DI)).then_inc(m_cld[j].sem, 16)
        if stages < 2:
            store_result()
            return

        sp.dma_start(a_rope[:], a["c_ropeq"]).then_inc(w_ld[1].sem, 16)
        with sp.Fori(0, H // 2) as i:
            for j in range(2):
                h = 2 * i + j
                sp.wait_ge(a_prep.sem, a_prep.at(2 * i + j - 1))
                for dst, src in ((a_wq[:, j, :], a["Wq"][h]), (a_wkq[:, j, :], a["w_kc_q"][h]),
                                 (a_wqr[:, j, :], a["W_qr_T"][h]), (a_wkr[:, j, :], a["W_kr_T"][h]),
                                 (a_wkv[:, j, :], a["w_kc_kv"][h]), (a_wo[:, j, :], a["Wo_T"][h])):
                    sp.dma_start(dst, src).then_inc(a_ld[j].sem, 16)

        sp.wait_ge(a_qb.sem, a_qb.at(H * NCH))
        sp.dma_start(b_rope[:], a["c_ropek"]).then_inc(w_ld[1].sem, 16)

        def load_kv(b, j):
            sp.dma_start(b_kv[:, j, :, :], a["ctx"][b].rearrange("(p c) d -> p c d", c=KC)).then_inc(b_ld[j].sem, 16)

        def store_ctx(b, j):
            sp.wait_ge(b_cev.sem, b_cev.at(2 * (b + 1)))
            for e in range(2):
                sp.dma_start(ctx_dram.rearrange("(b s) (i e) d -> b e s i d", s=S, e=2)[b, e],
                             b_ctx[S * e:S * e + S, j, :, :]).then_inc(b_cst[j].sem, 16)

        load_kv(0, 0)
        load_kv(1, 1)
        with sp.Fori(0, NSEQ // 2 - 1) as i:
            for j in range(2):
                b = 2 * i + j
                sp.wait_ge(b_kvr_rdy.sem, b_kvr_rdy.at(b + 1))
                load_kv(b + 2, j)
                store_ctx(b, j)
        for j in range(2):
            store_ctx(NSEQ - 2 + j, j)
        sp.wait_ge(b_cst[0].sem, b_cst[0].at(16 * NSEQ))
        sp.wait_ge(b_cst[1].sem, b_cst[1].at(16 * NSEQ))
        sp.wait_ge(b_pv.sem, b_pv.at(NSEQ * KC))
        with sp.Fori(0, NT // 2) as i:
            for j in range(2):
                sp.wait_ge(c_tr.sem, c_tr.at(2 * i + j - 1))
                sp.dma_start(c_ctx[:, j, :], ctx_dram.rearrange("(t p) h d -> t p (h d)", p=TILE)[2 * i + j]
                             ).then_inc(c_in[j].sem, 16)
        if stages < 3:
            store_result()
            return

        for dst, src in ((f_g[:], a["gate_T"].rearrange("(k p) n -> p k n", p=128)),
                         (f_u[:], a["up_T"].rearrange("(k p) n -> p k n", p=128)),
                         (f_d[:, 0:5, :], a["down_T"][0:640].rearrange("(k p) n -> p k n", p=128)),
                         (f_d[0:64, 5, :], a["down_T"][640:704]),
                         (f_gs[:], a["gate_s"]), (f_us[:], a["up_s"]),
                         (f_ds[:], a["down_s"].partition_broadcast(TILE))):
            sp.dma_start(dst, src).then_inc(w_ld[2].sem, 16)
        if stages < 4:
            store_result()
            return

        for k, name in enumerate(("N_Wq1", "N_Wq2", "N_Wk", "N_Wv")):
            sp.dma_start(n_w[:, k, :, :], a[name].rearrange("(k p) n -> p k n", p=128)).then_inc(w_ld[3].sem, 16)
        for dst, src in ((n_lam[:], a["N_Wlam"].rearrange("(k p) n -> p k n", p=128)),
                         (n_wo[:], a["N_Wo"].rearrange("(k p) n -> p k n", p=128)),
                         (z_wq[:], a["Z_Wq_T"].rearrange("(k p) n -> p k n", p=128)),
                         (z_wkv[:], a["Z_Wkv_T"]),
                         (z_wo[:], a["Z_Wout_T"].rearrange("(k p) n -> p k n", p=128)),
                         (z_ctx[:], a["ctx_head_T"]), (n_hm[:], a["c_headmask"]), (n_caus[:], a["c_causal"])):
            sp.dma_start(dst, src).then_inc(w_ld[3].sem, 16)
        if stages < 6:
            store_result()
            return

        sp.wait_ge(xt_rdy.sem, xt_rdy.at(4 * NT))
        for dst, src in ((r_w[:], a["router_w"].rearrange("(k p) n -> p k n", p=128)),
                         (r_b[:], a["router_bias"].partition_broadcast(TILE)),
                         (r_lt[:], a["c_lower"].partition_broadcast(TILE))):
            sp.dma_start(dst, src).then_inc(w_ld[5].sem, 16)
        sp.dma_start(r_wt[NE:NEX, :], a["c_ones"]).then_inc(w_ld[5].sem, 16)
        sp.wait_ge(r_te.sem, r_te.at(NCH))
        sp.dma_start(rw_dram, r_wt[:]).then_inc(r_st.sem, 16)
        sp.wait_ge(r_st.sem, r_st.at(16))
        with sp.Fori(0, NCH) as c:
            with sp.Fori(0, NEX // 2) as i:
                for j in range(2):
                    u = NEX * c + 2 * i + j
                    sp.wait_ge(e_gu.sem, e_gu.at(u - 1))
                    sp.dma_start(e_wgu[:, j, :], a["W_exp"][2 * i + j][:, 0:2 * D]).then_inc(e_ld[j].sem, 16)
                    sp.wait_ge(e_awr.sem, e_awr.at(u - 1))
                    sp.dma_start(e_tw[:, j, :], rw_dram[2 * i + j, bass.ds(CHUNK * c, CHUNK)].partition_broadcast(128)
                                 ).then_inc(e_tld[j].sem, 16)
                    sp.wait_ge(e_dn.sem, e_dn.at(u - 1))
                    sp.dma_start(e_wd[:, j, :], a["W_exp"][2 * i + j][:, 2 * D:3 * D]).then_inc(e_dld[j].sem, 16)
        store_result()

    @block.vector
    def _(dve):
        ch = Chain(nc, "dve_chain")
        v = nc.vector

        def residual(k, t, bank, mul=1.0):
            dve.wait_ge(tail_rdy.sem, tail_rdy.at((k - 1) * NT + t + 1))
            v.scalar_tensor_tensor(x_tok[:, t, :], x_tok[:, t, :], mul, ps[0:TILE, bank, 0:D],
                                   ALU.mult, ALU.add).then_inc(tail_used.sem, 1)
            dve.wait_ge(tail_used.sem, tail_used.at((k - 1) * NT + t + 1))
            v.bn_stats(ln_stats[:, t, :], x_tok[:, t, :]).then_inc(ln_st.sem, 1)

        def norm(k):
            dve.wait_ge(ln_st.sem, ln_st.at((k + 1) * NT))
            me, mo, ve, vo = (ln_stats[:, :, q] for q in (1, 4, 2, 5))
            v.tensor_tensor(ln_a[:], me, mo, ALU.add).then_inc(ch.sem, ch.one())
            v.tensor_tensor(ln_d[:], me, mo, ALU.subtract).then_inc(ch.sem, ch.one())
            v.tensor_tensor(ln_b[:], ve, vo, ALU.add).then_inc(ch.sem, ch.one())
            dve.wait_ge(ch.sem, ch.all())
            v.tensor_scalar(ln_mean[:], ln_a[:], 0.5, None, ALU.mult).then_inc(ch.sem, ch.one())
            v.tensor_tensor(ln_sq[:], ln_d[:], ln_d[:], ALU.mult).then_inc(ch.sem, ch.one())
            v.tensor_scalar(ln_b[:], ln_b[:], 1.0 / D, EPS, ALU.mult, ALU.add).then_inc(ch.sem, ch.one())
            dve.wait_ge(ch.sem, ch.all())
            v.scalar_tensor_tensor(ln_var[:], ln_sq[:], 0.25, ln_b[:], ALU.mult, ALU.add).then_inc(std_req.sem, 1)
            dve.wait_ge(std_rdy.sem, std_rdy.at(k + 1))
            v.reciprocal(ln_rstd[:], ln_std[:]).then_inc(ch.sem, ch.one())
            dve.wait_ge(ch.sem, ch.all())
            for t in range(NT):
                if k == 0 and t >= 2:
                    dve.wait_ge(xt_mm.sem, xt_mm.at(t - 1))
                v.tensor_scalar(xn[:, t % 2, :] if k == 0 else x_tok[:, t, :], x_tok[:, t, :],
                                ln_mean[:, t:t + 1], ln_rstd[:, t:t + 1], ALU.subtract, ALU.mult
                                ).then_inc(xn_rdy.sem, 1)

        dve.wait_ge(x_ld.sem, x_ld.at(16))
        with dve.Fori(0, NT) as t:
            v.bn_stats(ln_stats[:, t, :], x_tok[:, t, :]).then_inc(ln_st.sem, 1)
        norm(0)

        dve.wait_ge(w_ld[0].sem, w_ld[0].at(9 * 16))
        dve.wait_ge(m_ev.sem, m_ev.at(NCH))
        dve.wait_ge(m_padz.sem, m_padz.at(2))
        v.tensor_scalar(m_c[:], m_pad[:, :, 0:S], m_cw[:, 0:1], m_cb[:, 0:1], ALU.mult, ALU.add).then_inc(ch.sem, ch.one())
        dve.wait_ge(ch.sem, ch.all())
        v.scalar_tensor_tensor(m_c[:], m_pad[:, :, 1:1 + S], m_cw[:, 1:2], m_c[:], ALU.mult, ALU.add).then_inc(ch.sem, ch.one())
        dve.wait_ge(ch.sem, ch.all())
        v.scalar_tensor_tensor(m_c[:], m_pad[:, :, 2:2 + S], m_cw[:, 2:3], m_c[:], ALU.mult, ALU.add
                               ).then_inc(m_convd.sem, 1)
        flat_c = m_c[:].rearrange("p a b -> p (a b)")
        dve.wait_ge(m_exp.sem, m_exp.at(2))
        v.tensor_scalar(m_t1[:], m_t1[:], 1.0, None, ALU.add).then_inc(ch.sem, ch.one())
        dve.wait_ge(ch.sem, ch.all())
        v.reciprocal(m_t2[:], m_t1[:]).then_inc(ch.sem, ch.one())
        v.tensor_scalar(m_a[:], m_a[:], -1.0, None, ALU.mult).then_inc(ch.sem, ch.one())
        dve.wait_ge(ch.sem, ch.all())
        v.tensor_tensor(m_u[:], flat_c, m_t2[:], ALU.mult).then_inc(m_silu.sem, 1)
        dve.wait_ge(m_silu.sem, m_silu.at(1))
        v.tensor_scalar(m_ud[:], m_u[:], m_dp[:, 0:1], None, ALU.mult).then_inc(m_silu.sem, 1)
        dve.wait_ge(m_mm.sem, m_mm.at(3 * NCH))
        zt = ps[0:DI, 4:8, 0:CHUNK]
        v4 = lambda t: t[:].rearrange("p (c n) -> p c n", c=NCH)
        v.tensor_scalar(v4(m_t1), zt, m_dtb[:, 0:1], 0.0, ALU.add, ALU.min).then_inc(ch.sem, ch.one())
        v.tensor_scalar(v4(m_t2), zt, m_dtb[:, 0:1], 0.0, ALU.add, ALU.max).then_inc(ch.sem, ch.one())
        dve.wait_ge(ch.sem, ch.all())
        v.tensor_tensor(m_t1[:], m_t1[:], m_t2[:], ALU.subtract).then_inc(m_abs.sem, 1)
        dve.wait_ge(m_ln.sem, m_ln.at(1))
        v.tensor_scalar(m_ud2[:], m_t1[:], 2.0, None, ALU.add).then_inc(ch.sem, ch.one())
        dve.wait_ge(ch.sem, ch.all())
        v.reciprocal(m_sq[:], m_ud2[:]).then_inc(ch.sem, ch.one())
        dve.wait_ge(ch.sem, ch.all())
        v.tensor_tensor(m_t1[:], m_t1[:], m_sq[:], ALU.mult).then_inc(ch.sem, ch.one())
        dve.wait_ge(ch.sem, ch.all())
        v.tensor_tensor(m_sq[:], m_t1[:], m_t1[:], ALU.mult).then_inc(ch.sem, ch.one())
        dve.wait_ge(ch.sem, ch.all())
        v.tensor_scalar(m_ud2[:], m_sq[:], ATANH[-1], None, ALU.mult).then_inc(ch.sem, ch.one())
        for coef in ATANH[-2:0:-1]:
            dve.wait_ge(ch.sem, ch.all())
            v.scalar_tensor_tensor(m_ud2[:], m_ud2[:], coef, m_sq[:], ALU.add, ALU.mult).then_inc(ch.sem, ch.one())
        dve.wait_ge(ch.sem, ch.all())
        v.scalar_tensor_tensor(m_t1[:], m_ud2[:], ATANH[0], m_t1[:], ALU.add, ALU.mult).then_inc(ch.sem, ch.one())
        dve.wait_ge(ch.sem, ch.all())
        v.tensor_tensor(m_t2[:], m_t2[:], m_t1[:], ALU.add).then_inc(ch.sem, ch.one())
        dve.wait_ge(ch.sem, ch.all())
        flat_delta = m_delta[:].rearrange("p a b -> p (a b)")
        v.tensor_scalar(flat_delta, m_t2[:], 0.001, None, ALU.mult).then_inc(m_dl.sem, 1)
        dve.wait_ge(m_dl.sem, m_dl.at(1))
        v.tensor_tensor(m_du[:], flat_delta, m_u[:], ALU.mult).then_inc(m_dl.sem, 1)
        with dve.Fori(0, NS // 2) as i:
            for j in range(2):
                n = 2 * i + j
                dve.wait_ge(m_da_rdy.sem, m_da_rdy.at(n + 1))
                dve.wait_ge(m_dbu_rdy.sem, m_dbu_rdy.at(n + 1))
                dve.wait_ge(m_ymm.sem, m_ymm.at(n - 1))
                v.tensor_tensor_scan(m_h[:, j, :], m_da[:, j, :, :].rearrange("p a b -> p (a b)"), m_dbu[:, j, :],
                                     0.0, ALU.mult, ALU.add).then_inc(m_scan.sem, 1)
                dve.wait_ge(m_scan.sem, m_scan.at(n + 1))
                dve.wait_ge(m_cld[j].sem, m_cld[j].at(16 * (i + 1)))
                v.tensor_tensor(m_h[:, j, :], m_h[:, j, :], m_cc[:, j, :], ALU.mult).then_inc(m_hc.sem, 1)
        with dve.Fori(0, NT // 2) as i:
            for j in range(2):
                residual(1, 2 * i + j, TAIL[j], 2.0)
        norm(1)
        if stages < 2:
            return

        dve.wait_ge(w_ld[1].sem, w_ld[1].at(16))
        def query_rest(i, v_):
            j, c = v_ // NCH, v_ % NCH
            dve.wait_ge(a_qhi.sem, a_qhi.at(8 * i + v_ + 1))
            rest = q_all[64:128, 2 * i + j, CHUNK * c:CHUNK * c + CHUNK]
            v.tensor_tensor(rest, ps[64:128, 4 + c % 2, 0:CHUNK], rest.bitcast(F32), ALU.subtract
                            ).then_inc(a_qev.sem, 1)

        def weights_rest(h, j):
            dve.wait_ge(a_prep_ev.sem, a_prep_ev.at(h + 1))
            v.tensor_tensor(a_wlo[:, j, :, :], ps[:, 6, 0:KD * DCQ].rearrange("p (k n) -> p k n", k=KD),
                            a_whi[:, j, :, :].bitcast(F32), ALU.subtract).then_inc(a_wl.sem, 1)

        for c in range(NCH):
            dve.wait_ge(a_xh.sem, a_xh.at(c + 1))
            cols = slice(CHUNK * c, CHUNK * c + CHUNK)
            v.tensor_tensor(a_xlo[:, :, cols], x_feat[:, :, cols], a_xhi[:, :, cols].bitcast(F32), ALU.subtract
                            ).then_inc(a_xl.sem, 1)
            if c == 0:
                weights_rest(0, 0)

        def rotate(i, last):
            for j in range(2):
                for c in range(NCH):
                    u = 8 * i + 4 * j + c
                    q = c % 2
                    dve.wait_ge(a_qb.sem, a_qb.at(u + 1))
                    dve.wait_ge(a_rt.sem, a_rt.at(u - 1))
                    for k, (half, tab) in enumerate(((0, 0), (1, 1), (1, 2), (0, 3))):
                        ins = v.tensor_tensor(
                            a_prod[:, q, k, :].rearrange("p (b s) -> p b s", s=S),
                            ps[0:HALFQ, 2 * q + half, 0:CHUNK].rearrange("p (b s) -> p b s", s=S),
                            a_rope[:, tab, :].unsqueeze(1).broadcast_to([HALFQ, 8, S]), ALU.mult)
                    ins.then_inc(a_pr.sem, 1)
                    if c == 2 and not (last and j == 1):
                        weights_rest(2 * i + j + 1, 1 - j)
                    if j or c:
                        query_rest(i, 4 * j + c - 1)
            query_rest(i, 7)

        with dve.Fori(0, H // 2 - 1) as i:
            rotate(i, False)
        rotate(H // 2 - 1, True)

        def maxima(b, j, done=None):
            for r in range(3):
                dve.wait_ge(b_ktev.sem, b_ktev.at(3 * b + r + 1))
                part = slice(4 * KP * r, 4 * KP * r + 4 * KP)
                v.tensor_tensor(b_klo[0:DC, j, part], ps[0:DC, r, 0:4 * KP], b_khi[0:DC, j, part].bitcast(F32),
                                ALU.subtract).then_inc(b_klev.sem, 1)
            for c in range(8):
                if c == 2 and done is not None:
                    outputs(done, j)
                for u in range(3):
                    dve.wait_ge(b_rmm.sem, b_rmm.at(30 * b + 3 + 3 * c + u + 1))
                    v.tensor_reduce(b_mx3[:, j, c, u:u + 1], ps[0:TILE, u, 0:4 * KP], AX.X, ALU.max
                                    ).then_inc(b_mxd.sem, 1)
            dve.wait_ge(b_mxd.sem, b_mxd.at(24 * (b + 1)))
            v.tensor_reduce(b_mx[:, j, :], b_mx3[:, j, :, :], AX.X, ALU.max).then_inc(b_mxc.sem, 1)

        def outputs(b, j):
            dve.wait_ge(b_otr.sem, b_otr.at(b + 1))
            for g in range(2):
                o = ps[0:TILE, g, 0:4 * (DC + 1)].rearrange("p (i d) -> p i d", i=4)
                v.reciprocal(b_rs[:, j, 4 * g:4 * g + 4], o[:, :, DC]).then_inc(ch.sem, ch.one())
            dve.wait_ge(ch.sem, ch.all())
            dve.wait_ge(b_cst[j].sem, b_cst[j].at(16 * (b - j)))
            for g in range(2):
                o = ps[0:TILE, g, 0:4 * (DC + 1)].rearrange("p (i d) -> p i d", i=4)
                v.tensor_tensor(b_ctx[:, j, 4 * g:4 * g + 4, :], o[:, :, 0:DC],
                                b_rs[:, j, 4 * g:4 * g + 4].unsqueeze(2).broadcast_to([TILE, 4, DC]), ALU.mult
                                ).then_inc(b_cev.sem, 1)

        maxima(0, 0)
        dve.wait_ge(xn_rdy.sem, xn_rdy.at(2 * NT))
        maxima(1, 1)
        with dve.Fori(0, NSEQ // 2 - 1) as i:
            ch.enter(i, 4)
            maxima(2 * i + 2, 0, 2 * i)
            maxima(2 * i + 3, 1, 2 * i + 1)
            ch.leave(NSEQ // 2 - 1)
        outputs(NSEQ - 2, 0)
        outputs(NSEQ - 1, 1)
        with dve.Fori(0, NT // 2) as i:
            for j in range(2):
                residual(2, 2 * i + j, TAIL[j])
        norm(2)
        if stages < 3:
            return

        dve.wait_ge(w_ld[2].sem, w_ld[2].at(7 * 16))
        dve.wait_ge(xn_rdy.sem, xn_rdy.at(3 * NT))
        with dve.Fori(0, NCH) as c:
            for b in range(FB):
                q, m = b % 2, (128 if b < 5 else 64)
                dve.wait_ge(f_sl.sem, f_sl.at(FB * c + b + 1))
                if b == 0:
                    dve.wait_ge(tail_rdy.sem, tail_rdy.at(2 * NT + 4 * c))
                v.scalar_tensor_tensor(f_h[0:m, b, :], ps[0:m, 2 + q, 0:CHUNK], f_us[0:m, b:b + 1],
                                       f_act[0:m, q, :], ALU.mult, ALU.mult).then_inc(f_hr.sem, 1)
            ch.enter(c, TPC)
            for s in range(TPC):
                t, j = TPC * c + s, s % 2
                dve.wait_ge(tail_rdy.sem, tail_rdy.at(2 * NT + t + 1))
                v.tensor_tensor(f_y[:, j, :], ps[0:TILE, TAIL[j], 0:D], f_ds[:], ALU.mult).then_inc(ch.sem, ch.one())
                dve.wait_ge(ch.sem, ch.all())
                v.tensor_tensor(x_tok[:, t, :], x_tok[:, t, :], f_y[:, j, :], ALU.add).then_inc(tail_used.sem, 1)
                dve.wait_ge(tail_used.sem, tail_used.at(2 * NT + t + 1))
                v.bn_stats(ln_stats[:, t, :], x_tok[:, t, :]).then_inc(ln_st.sem, 1)
            ch.leave(NCH)
        norm(3)
        if stages < 4:
            return

        dve.wait_ge(w_ld[3].sem, w_ld[3].at(12 * 16))
        v.tensor_copy(n_caus_bf[:], n_caus[:].unsqueeze(1).broadcast_to([TILE, 8, S])).then_inc(n_cst.sem, 1)
        v.tensor_copy(ident_bf[:], ident[0:TILE, 0:TILE]).then_inc(n_cst.sem, 1)

        def softmax(base, t, j, ns):
            hh = ns * H
            sc = ps[0:TILE, 3:3 + 2 * ns, 0:CHUNK].rearrange("p q (h k) -> p q h k", k=S)
            dve.wait_ge(n_sc.sem, n_sc.at(base + t + 1))
            v.tensor_reduce(n_mx[:, j, 0:hh].rearrange("p (q h) -> p q h", h=8), sc, AX.X, ALU.max).then_inc(ch.sem, ch.one())
            dve.wait_ge(ch.sem, ch.all())
            for q in range(2 * ns):
                ins = v.tensor_tensor(n_e[:, j, CHUNK * q:CHUNK * q + CHUNK].rearrange("p (h k) -> p h k", k=S),
                                      sc[:, q, :, :],
                                      n_mx[:, j, 8 * q:8 * q + 8].unsqueeze(2).broadcast_to([TILE, 8, S]),
                                      ALU.subtract)
            ins.then_inc(n_sub.sem, 1)
            dve.wait_ge(n_exp.sem, n_exp.at(base + t + 1))
            v.tensor_reduce(n_sum[:, j, 0:hh], n_e[:, j, 0:hh * S].rearrange("p (h k) -> p h k", k=S),
                               AX.X, ALU.add).then_inc(ch.sem, ch.one())
            dve.wait_ge(ch.sem, ch.all())
            if ns == 1:
                v.reciprocal(n_r[:, j, 0:H], n_sum[:, j, 0:H]).then_inc(n_rr.sem, 1)
            else:
                v.reciprocal(n_r[:, j, :], n_sum[:, j, :]).then_inc(ch.sem, ch.one())
                dve.wait_ge(n_le.sem, n_le.at(t + 1))
                v.tensor_scalar(n_l2[:, j, :], n_l[:, j, :], 1.0, None, ALU.add).then_inc(ch.sem, ch.one())
                dve.wait_ge(ch.sem, ch.all())
                v.reciprocal(n_l3[:, j, :], n_l2[:, j, :]).then_inc(ch.sem, ch.one())
                dve.wait_ge(ch.sem, ch.all())
                v.scalar_tensor_tensor(n_r[:, j, H:2 * H], n_r[:, j, H:2 * H], -1.0, n_l3[:, j, :],
                                       ALU.mult, ALU.mult).then_inc(n_rr.sem, 1)

        for layer, ns in ((0, 2), (1, 1)):
            per = 2 if ns == 1 else 5
            base = layer * NT
            if layer == 1 and stages < 5:
                return
            softmax(base, 0, 0, ns)
            dve.wait_ge(xn_rdy.sem, xn_rdy.at((4 + layer) * NT))
            with dve.Fori(0, NT // 2 - 1) as i:
                ch.enter(i, 2 * per)
                for j in range(2):
                    softmax(base, 2 * i + j + 1, 1 - j, ns)
                    residual(4 + layer, 2 * i + j, 7)
                ch.leave(NT // 2 - 1)
            softmax(base, NT - 1, 1, ns)
            residual(4 + layer, NT - 2, 7)
            residual(4 + layer, NT - 1, 7)
            norm(4 + layer)
        if stages < 6:
            return

        dve.wait_ge(w_ld[5].sem, w_ld[5].at(4 * 16))
        dve.wait_ge(r_ex.sem, r_ex.at(1))
        flat = lambda t: t[:].rearrange("p a b -> p (a b)")

        def step(ins):
            ins.then_inc(ch.sem, ch.one())
            dve.wait_ge(ch.sem, ch.all())

        step(v.tensor_scalar(flat(r_s), flat(r_m), 1.0, None, ALU.add))
        step(v.reciprocal(flat(r_s), flat(r_s)))
        step(v.tensor_tensor(r_sb[:], r_s[:], r_b[:].unsqueeze(1).broadcast_to([TILE, NT, NE]), ALU.add))
        quad = r_sb[:].rearrange("p t (g e) -> p (t g) e", e=4)
        f3 = lambda t: t[:].rearrange("p t g e -> p (t g) e")
        f2 = lambda t: t[:].rearrange("p t g -> p (t g)")
        v.tensor_tensor(f3(r_hi), quad[:, :, 0:2], quad[:, :, 2:4], ALU.max).then_inc(ch.sem, ch.one())
        step(v.tensor_tensor(f3(r_lo), quad[:, :, 0:2], quad[:, :, 2:4], ALU.min))
        v.tensor_tensor(f2(r_g1), f3(r_hi)[:, :, 0], f3(r_hi)[:, :, 1], ALU.max).then_inc(ch.sem, ch.one())
        v.tensor_tensor(f2(r_g2), f3(r_hi)[:, :, 0], f3(r_hi)[:, :, 1], ALU.min).then_inc(ch.sem, ch.one())
        step(v.tensor_tensor(f2(r_g3), f3(r_lo)[:, :, 0], f3(r_lo)[:, :, 1], ALU.max))
        step(v.tensor_tensor(r_g2[:], r_g2[:], r_g3[:], ALU.max))
        step(v.tensor_tensor(r_g1[:], r_g1[:], r_g2[:], ALU.add))
        other = r_g1[:].unsqueeze(2).broadcast_to([TILE, NT, NG, NG])
        own = r_g1[:].unsqueeze(3).broadcast_to([TILE, NT, NG, NG])
        for t in range(NT):
            v.tensor_tensor(r_c1[:, t, :, :], other[:, t, :, :], own[:, t, :, :], ALU.is_gt).then_inc(ch.sem, ch.one())
            v.tensor_tensor(r_c2[:, t, :, :], other[:, t, :, :], own[:, t, :, :], ALU.is_equal).then_inc(ch.sem, ch.one())
        dve.wait_ge(ch.sem, ch.all())
        c3 = lambda t: t[:].rearrange("p t g e -> p t (g e)")
        step(v.tensor_tensor(c3(r_c2), c3(r_c2), r_lt[:].rearrange("p g e -> p (g e)").unsqueeze(1).broadcast_to(
            [TILE, NT, NG * NG]), ALU.mult))
        step(v.tensor_tensor(f3(r_c1), f3(r_c1), f3(r_c2), ALU.add))
        step(v.tensor_reduce(f2(r_g2), f3(r_c1), AX.X, ALU.add))
        step(v.tensor_scalar(r_g3[:], r_g2[:], TOPG - 0.5, None, ALU.is_lt))
        step(v.tensor_tensor(r_m[:].rearrange("p t (g e) -> p (t g) e", e=4), quad,
                             f2(r_g3).unsqueeze(2).broadcast_to([TILE, NT * NG, 4]), ALU.mult))
        for t in range(NT):
            v.max(r_top[:, t, :], r_m[:, t, :]).then_inc(ch.sem, ch.one())
        dve.wait_ge(ch.sem, ch.all())
        for t in range(NT):
            v.match_replace(r_m2[:, t, :], r_top[:, t, :], r_m[:, t, :], NEG).then_inc(ch.sem, ch.one())
        dve.wait_ge(ch.sem, ch.all())
        step(v.tensor_scalar(r_m2[:], r_m2[:], NEG / 2, None, ALU.is_lt))
        step(v.tensor_tensor(r_m[:], r_m2[:], r_s[:], ALU.mult))
        step(v.tensor_reduce(r_den[:], r_m[:], AX.X, ALU.add))
        step(v.reciprocal(r_rden[:], r_den[:]))
        step(v.tensor_scalar(r_rden[:], r_rden[:], ROUTED_SCALE, None, ALU.mult))
        v.tensor_tensor(r_m2[:], r_m[:], r_rden[:].unsqueeze(2).broadcast_to([TILE, NT, NE]), ALU.mult
                        ).then_inc(r_sel.sem, 1)

        dve.wait_ge(xn_rdy.sem, xn_rdy.at(6 * NT))
        with dve.Fori(0, NCH) as c:
            with dve.Fori(0, NEX // 2) as i:
                for j in range(2):
                    u = NEX * c + 2 * i + j
                    dve.wait_ge(e_awr.sem, e_awr.at(u + 1))
                    dve.wait_ge(e_dn.sem, e_dn.at(u - 1))
                    v.tensor_tensor(e_h[:, j, :], e_aw[:, j, :], ps[:, 2 + j, 0:CHUNK], ALU.mult
                                    ).then_inc(e_hr.sem, 1)
            for s in range(TPC):
                residual(6, TPC * c + s, 6 + s % 2)
        norm(6)


    @block.scalar
    def _(act):
        copy = lambda dst, src, **kw: nc.scalar.activation(dst, src, ACT.Copy, **kw)
        ch = Chain(nc, "act_chain")

        def norm(k):
            act.wait_ge(std_req.sem, std_req.at(k + 1))
            nc.scalar.activation(ln_std[:], ln_var[:], ACT.Sqrt).then_inc(std_rdy.sem, 1)
            if k == stages:
                return
            for p in range(NT // 2):
                act.wait_ge(xt_mm.sem, xt_mm.at(k * NT + 2 * p + 2))
                src = ps[:, XT[p % 2], 0:KD * 2 * TILE].rearrange("p (k n) -> p k n", k=KD)
                cols = slice(2 * TILE * p, 2 * TILE * p + 2 * TILE)
                if k == 0:
                    nc.scalar.activation(x_feat[:, 0, cols], src[:, 0, :], ACT.Identity,
                                         scale=m_lnw[:, 0:1], bias=m_lnb[:, 0:1])
                    nc.scalar.activation(x_feat[:, 1, cols], src[:, 1, :], ACT.Identity,
                                         scale=m_lnw[:, 1:2], bias=m_lnb[:, 1:2]).then_inc(xt_rdy.sem, 2)
                else:
                    copy(x_feat[:, :, cols], src).then_inc(xt_rdy.sem, 2)

        act.wait_ge(c_ld.sem, c_ld.at(48))
        norm(0)

        act.wait_ge(m_padz.sem, m_padz.at(2))
        for c in range(NCH):
            act.wait_ge(m_mm.sem, m_mm.at(c + 1))
            copy(m_pad[:, 8 * c:8 * c + 8, 1:1 + S],
                 ps[0:DI, c, 0:CHUNK].rearrange("p (b s) -> p b s", s=S)).then_inc(m_ev.sem, 1)
        act.wait_ge(w_ld[0].sem, w_ld[0].at(9 * 16))
        nc.scalar.activation(m_a[:], m_al[:], ACT.Exp).then_inc(m_exp.sem, 1)
        act.wait_ge(m_convd.sem, m_convd.at(1))
        nc.scalar.activation(m_t1[:], m_c[:].rearrange("p a b -> p (a b)"), ACT.Exp, scale=-1.0
                             ).then_inc(m_exp.sem, 1)
        for c in range(NCH):
            act.wait_ge(m_mm.sem, m_mm.at(NCH + c + 1))
            copy(m_dbc[:, CHUNK * c:CHUNK * c + CHUNK], ps[0:DTR + 2 * NS, c, 0:CHUNK]).then_inc(m_dbc_ev.sem, 1)
        act.wait_ge(m_abs.sem, m_abs.at(1))
        nc.scalar.activation(m_t1[:], m_t1[:], ACT.Exp).then_inc(m_ln.sem, 1)
        act.wait_ge(m_dl.sem, m_dl.at(1))
        act.wait_ge(m_padz.sem, m_padz.at(3))
        with act.Fori(0, NS // 2) as i:
            for j in range(2):
                n = 2 * i + j
                act.wait_ge(m_scan.sem, m_scan.at(n - 1))
                nc.scalar.activation(m_da[:, j, :, 1:S], m_delta[:, :, 1:S], ACT.Exp, scale=m_a[:, bass.ds(n, 1)]
                                     ).then_inc(m_da_rdy.sem, 1)
        act.wait_ge(m_ymm.sem, m_ymm.at(NS))
        with act.Fori(0, NCH) as c:
            for s in range(TPC):
                t, j = TPC * c + s, s % 2
                act.wait_ge(tail_rdy.sem, tail_rdy.at(t - 1))
                copy(m_y[:, j, :], ps[0:DI, c, TILE * s:TILE * s + TILE]).then_inc(m_yev.sem, 1)
        norm(1)
        if stages < 2:
            return

        def weights_out(pair, j):
            act.wait_ge(a_prep.sem, a_prep.at(2 * pair + j + 1))
            copy(a_whi[:, j, :, :], ps[:, 6, 0:KD * DCQ].rearrange("p (k n) -> p k n", k=KD))
            for e in range(2):
                copy(a_w2[:, j, :, e, :], ps[0:HALFQ, 7, 0:2 * DC].rearrange("p (k n) -> p k n", k=2))
            copy(w3[64 * j:64 * j + 64, pair, :], ps[64 * j:64 * j + 64, 7, 256:512]).then_inc(a_prep_ev.sem, 1)

        def queries_out(i, last):
            for j in range(2):
                for c in range(NCH):
                    u = 8 * i + 4 * j + c
                    act.wait_ge(a_qq.sem, a_qq.at(u + 1))
                    copy(q_all[:, 2 * i + j, CHUNK * c:CHUNK * c + CHUNK], ps[:, 4 + c % 2, 0:CHUNK]
                         ).then_inc(a_qhi.sem, 1)
                    if c == 0 and not (last and j == 1):
                        weights_out(i + j, 1 - j)

        for c in range(NCH):
            cols = slice(CHUNK * c, CHUNK * c + CHUNK)
            copy(a_xhi[:, :, cols], x_feat[:, :, cols]).then_inc(a_xh.sem, 1)
            if c == 0:
                weights_out(0, 0)
        with act.Fori(0, H // 2 - 1) as i:
            queries_out(i, False)
        queries_out(H // 2 - 1, True)

        def keys_out(nb, nj):
            if not (isinstance(nb, int) and nb == 0):
                act.wait_ge(b_st.sem, b_st.at(2 * KC * (nb - 1)))
            for r in range(3):
                act.wait_ge(b_rmm.sem, b_rmm.at(30 * nb + r + 1))
                for e in range(2):
                    ins = copy(b_khi[64 * e:64 * e + 64, nj, 4 * KP * r:4 * KP * r + 4 * KP],
                               ps[0:DC, r, 0:4 * KP])
                ins.then_inc(b_ktev.sem, 1)

        def rows_out(nb, nj):
            for r, n in enumerate((3, 3, 2)):
                act.wait_ge(b_rmm.sem, b_rmm.at(30 * nb + 27 + r + 1))
                nc.scalar.activation(b_q[MROW:MROW + 1, nj, 3 * TILE * r:3 * TILE * r + n * TILE], ps[0:1, r, 0:n * TILE],
                                     ACT.Copy, scale=-1.0).then_inc(b_row.sem, 1)

        def exps(b, c):
            act.wait_ge(b_pv.sem, b_pv.at(KC * b + c - 2))
            for g in range(2):
                act.wait_ge(b_st.sem, b_st.at(2 * KC * b + 2 * c + g + 1))
                nc.scalar.activation(b_pt[:, c % 2, CHUNK * g:CHUNK * g + CHUNK], ps[0:KP, 3 + (2 * c + g) % 3, 0:CHUNK],
                                     ACT.Exp).then_inc(b_exp.sem, 1)

        def sums_out(b):
            act.wait_ge(b_pv.sem, b_pv.at(KC * (b + 1)))
            if not (isinstance(b, int) and b == 0):
                act.wait_ge(b_otr.sem, b_otr.at(b))
            for g in range(2):
                copy(b_of[:, g, :], ps[0:DC + 1, 6 + g, 0:CHUNK]).then_inc(b_oev.sem, 1)

        def sequence(b, nb, nj):
            if not (isinstance(b, int) and b == 0):
                sums_out(b - 1)
            for c in range(KC):
                exps(b, c)
                if nb is not None and c == 1:
                    keys_out(nb, nj)
                if nb is not None and c == 10:
                    rows_out(nb, nj)

        act.wait_ge(a_qev.sem, a_qev.at(H * NCH))
        copy(b_klo[64:128, :, :].rearrange("p a b -> p (a b)"),
             ident[64:128, MROW:MROW + 1].broadcast_to([64, 2 * KC * KP]))
        copy(b_q[64:128, :, :].rearrange("p a b -> p (a b)"), ident[64:128, 0:1].broadcast_to([64, 2 * NQ])
             ).then_inc(b_one.sem, 1)
        keys_out(0, 0)
        act.wait_ge(b_one.sem, b_one.at(2))
        rows_out(0, 0)
        sequence(0, 1, 1)
        with act.Fori(0, NSEQ // 2 - 1) as i:
            for j in range(2):
                sequence(2 * i + j + 1, 2 * i + j + 2, j)
        sequence(NSEQ - 1, None, None)
        sums_out(NSEQ - 1)
        with act.Fori(0, NT // 2) as i:
            for j in range(2):
                t = 2 * i + j
                act.wait_ge(c_tr.sem, c_tr.at(t + 1))
                act.wait_ge(tail_rdy.sem, tail_rdy.at(NT + t - 1))
                copy(c_ctxT[:, j, :, :].rearrange("p (q e) n -> p q (e n)", q=2), ps[:, 2 * j:2 * j + 2, 0:CHUNK]
                     ).then_inc(c_tev.sem, 1)
        norm(2)
        if stages < 3:
            return

        act.wait_ge(w_ld[2].sem, w_ld[2].at(7 * 16))
        with act.Fori(0, NCH) as c:
            for b in range(FB):
                q, m = b % 2, (128 if b < 5 else 64)
                act.wait_ge(f_gu.sem, f_gu.at(FB * c + b + 1))
                act.wait_ge(f_hr.sem, f_hr.at(FB * c + b - 1))
                nc.scalar.activation(f_act[0:m, q, :], ps[0:m, q, 0:CHUNK], ACT.Silu, scale=f_gs[0:m, b:b + 1]
                                     ).then_inc(f_sl.sem, 1)
        norm(3)
        if stages < 4:
            return

        def queries_keys(base, t, j, ns):
            act.wait_ge(n_qp.sem, n_qp.at(base + t + 1))
            act.wait_ge(n_sc.sem, n_sc.at(base + t - 1))
            src = ps[:, 0, 0:2 * ns * TILE].rearrange("p (q n) -> p q n", n=TILE)
            for e in range(2):
                ins = copy(n_qz[:, j, 0:2 * ns, e, S * e:S * e + S], src[:, :, S * e:S * e + S], scale=HD ** -0.5)
            ins.then_inc(n_qe.sem, 1)
            act.wait_ge(n_kp.sem, n_kp.at(base + t + 1))
            act.wait_ge(n_kmr.sem, n_kmr.at(base + t - 1))
            copy(n_kf[:, j, :, :], ps[:, 1, 0:2 * TILE].rearrange("p (q n) -> p q n", n=TILE)).then_inc(n_ke.sem, 1)
            if ns == 2:
                act.wait_ge(n_rr.sem, n_rr.at(base + t - 1))
                nc.scalar.activation(n_l[:, j, :], ps[0:TILE, 1, 2 * TILE:2 * TILE + H], ACT.Exp, scale=-1.0
                                     ).then_inc(n_le.sem, 1)

        def vals(base, t, j):
            act.wait_ge(n_vp.sem, n_vp.at(base + t + 1))
            act.wait_ge(n_pvm.sem, n_pvm.at(base + t - 1))
            vsrc = ps[0:S, 2, :].rearrange("p (b g e d) -> p b g e d", b=2, g=H // 2, e=2)
            vdst = n_v[:, j, :, :, :].rearrange("p b (g e) d -> p b g e d", e=2)
            for e in range(2):
                ins = copy(vdst[:, :, :, e, HD * e:HD * e + HD], vsrc[:, :, :, e, :])
            ins.then_inc(n_ve.sem, 1)

        def turned_out(layer, t, g):
            act.wait_ge(n_tr.sem, n_tr.at(turned(layer, t) + g + 1))
            copy(n_pt[:, g, :], ps[0:S, 2 - 2 * (g % 2), 0:CHUNK]).then_inc(n_te.sem, 1)

        def exps2(base, t, j, ns):
            act.wait_ge(n_sub.sem, n_sub.at(base + t + 1))
            nc.scalar.activation(n_e[:, j, 0:2 * ns * CHUNK], n_e[:, j, 0:2 * ns * CHUNK], ACT.Exp
                                 ).then_inc(n_exp.sem, 1)

        def finish(layer, t, j, ns, ahead):
            base = layer * NT
            act.wait_ge(n_pvm.sem, n_pvm.at(base + t))
            turned_out(layer, t, 0)
            turned_out(layer, t, 1)
            if ahead:
                exps2(base, t + 1, 1 - j, ns)
            for g in range(2, 4 * (2 - layer)):
                turned_out(layer, t, g)
            act.wait_ge(n_pvm.sem, n_pvm.at(base + t + 1))
            act.wait_ge(tail_rdy.sem, tail_rdy.at((3 + layer) * NT + t - 1))
            copy(n_yt[:, j, :, :], ps[:, 1, 256:256 + 2 * TILE].rearrange("p (k n) -> p k n", k=2)).then_inc(n_ye.sem, 1)

        act.wait_ge(n_zero.sem, n_zero.at(3))
        for layer, ns in ((0, 2), (1, 1)):
            base = layer * NT
            if layer == 1 and stages < 5:
                return
            queries_keys(base, 0, 0, ns)
            vals(base, 0, 0)
            queries_keys(base, 1, 1, ns)
            exps2(base, 0, 0, ns)
            vals(base, 1, 1)
            with act.Fori(0, NT // 2 - 1) as i:
                for j in range(2):
                    t = 2 * i + j
                    queries_keys(base, t + 2, j, ns)
                    finish(layer, t, j, ns, True)
                    vals(base, t + 2, j)
            finish(layer, NT - 2, 0, ns, True)
            finish(layer, NT - 1, 1, ns, False)
            norm(4 + layer)
        if stages < 6:
            return

        act.wait_ge(r_mm.sem, r_mm.at(NT))
        nc.scalar.activation(r_m[:].rearrange("p a b -> p (a b)"), ps[0:TILE, 0, :], ACT.Exp, scale=-1.0
                             ).then_inc(r_ex.sem, 1)
        for c in range(NCH):
            act.wait_ge(r_tr.sem, r_tr.at(c + 1))
            copy(r_wt[0:NE, CHUNK * c:CHUNK * c + CHUNK], ps[0:NE, c, 0:CHUNK]).then_inc(r_te.sem, 1)
        with act.Fori(0, NCH) as c:
            with act.Fori(0, NEX // 2) as i:
                for j in range(2):
                    u = NEX * c + 2 * i + j
                    act.wait_ge(e_gu.sem, e_gu.at(u + 1))
                    act.wait_ge(e_awr.sem, e_awr.at(u - 1))
                    nc.scalar.activation(e_act[:, j, :], ps[:, j, 0:CHUNK], ACT.Silu).then_inc(e_sl.sem, 1)
            act.wait_ge(e_dn.sem, e_dn.at(NEX * (c + 1)))
            act.wait_ge(tail_rdy.sem, tail_rdy.at(5 * NT + TPC * c))
            for g in range(2):
                copy(e_y[:, g, :], ps[:, 4 + g, 0:CHUNK]).then_inc(e_yev.sem, 1)
        norm(6)

    @block.gpsimd
    def _(pool):
        p = nc.gpsimd
        ch = Chain(nc, "pool_chain")

        p.memset(m_pad[:, :, 0:1], 0.0).then_inc(m_padz.sem, 1)
        p.memset(m_pad[:, :, S + 1:S + 2], 0.0).then_inc(m_padz.sem, 1)
        p.memset(m_da[:, :, :, 0:1], 0.0).then_inc(m_padz.sem, 1)
        pool.wait_ge(m_dl.sem, m_dl.at(2))
        with pool.Fori(0, NS // 2) as i:
            for j in range(2):
                n = 2 * i + j
                pool.wait_ge(m_bld[j].sem, m_bld[j].at(16 * (i + 1)))
                pool.wait_ge(m_scan.sem, m_scan.at(n - 1))
                p.tensor_tensor(m_dbu[:, j, :], m_du[:], m_bb[:, j, :], ALU.mult).then_inc(m_dbu_rdy.sem, 1)
        if stages < 2:
            return

        with pool.Fori(0, H // 2) as i:
            for j in range(2):
                for c in range(NCH):
                    u, q = 8 * i + 4 * j + c, c % 2
                    pool.wait_ge(a_pr.sem, a_pr.at(u + 1))
                    pool.wait_ge(a_qq.sem, a_qq.at(u - 1))
                    p.tensor_tensor(a_rot[:, q, 0, :], a_prod[:, q, 0, :], a_prod[:, q, 1, :], ALU.subtract)
                    p.tensor_tensor(a_rot[:, q, 1, :], a_prod[:, q, 2, :], a_prod[:, q, 3, :], ALU.add
                                    ).then_inc(a_rt.sem, 1)

        def prepare(nb, nj):
            pool.wait_ge(b_ld[nj].sem, b_ld[nj].at(8 * (nb - nj) + 16))
            kv, hd = b_kv[:, nj, :, :], DC // 2
            pool.wait_ge(b_kvr_rdy.sem, b_kvr_rdy.at(nb))
            p.tensor_tensor(b_tmp[:, :, 0:hd], kv[:, :, hd:DC], b_rope[:, 1, :, 0:hd], ALU.mult).then_inc(ch.sem, ch.one())
            p.tensor_tensor(b_tmp[:, :, hd:DC], kv[:, :, 0:hd], b_rope[:, 1, :, hd:DC], ALU.mult).then_inc(ch.sem, ch.one())
            pool.wait_ge(ch.sem, ch.all())
            p.tensor_tensor(kv, kv, b_rope[:, 0, :, :], ALU.mult).then_inc(ch.sem, ch.one())
            pool.wait_ge(ch.sem, ch.all())
            if not (isinstance(nb, int) and nb == 0):
                pool.wait_ge(b_pv.sem, b_pv.at(KC * (nb - 1)))
            p.tensor_tensor(b_kvr[:, nj, :, 0:DC], kv, b_tmp[:], ALU.add).then_inc(b_kvr_rdy.sem, 1)
            p.tensor_copy(b_q[0:DC, nj, :].rearrange("p (h s) -> p h s", s=S), q_all[0:DC, :, bass.ds(S * nb, S)]
                          ).then_inc(b_q_rdy.sem, 1)

        pool.wait_ge(a_qev.sem, a_qev.at(H * NCH))
        pool.wait_ge(w_ld[1].sem, w_ld[1].at(32))
        p.memset(b_kvr[:, :, :, DC:DC + 1], 1.0).then_inc(b_one.sem, 1)
        prepare(0, 0)
        with pool.Fori(0, NSEQ // 2 - 1) as i:
            ch.enter(i, 6)
            for j in range(2):
                prepare(2 * i + j + 1, 1 - j)
            ch.leave(NSEQ // 2 - 1)
        prepare(NSEQ - 1, 1)
        if stages < 3:
            return
        if stages < 4:
            return

        pool.wait_ge(b_pv.sem, b_pv.at(NSEQ * KC))
        p.memset(n_qz[:], 0.0).then_inc(n_zero.sem, 1)
        p.memset(n_v[:], 0.0).then_inc(n_zero.sem, 1)
        pool.wait_ge(w_ld[3].sem, w_ld[3].at(12 * 16))
        pool.sem_inc(n_zero.sem, 1)

        def stationary(base, t, j, ns):
            pool.wait_ge(n_vp.sem, n_vp.at(base + t - 1))
            if ns == 2:
                p.tensor_copy(n_xf[:, j, :, :], x_feat[:, :, bass.ds(TILE * t, TILE)]).then_inc(n_xfr.sem, 1)
            else:
                p.tensor_copy(n_xf[0:DC, j, 0, :], z_ctx[:, bass.ds(TILE * t, TILE)]).then_inc(n_xfr.sem, 1)
            pool.wait_ge(n_ke.sem, n_ke.at(base + t + 1))
            pool.wait_ge(n_sc.sem, n_sc.at(base + t - 1))
            for half in range(2):
                for e in range(2):
                    ins = p.tensor_tensor(n_km[:, j, 2 * half + e, :, :],
                                          n_kf[:, j, half, S * e:S * e + S].unsqueeze(1).broadcast_to([128, 8, S]),
                                          n_hm[:].unsqueeze(2).broadcast_to([128, 8, S]), ALU.mult)
            ins.then_inc(n_kmr.sem, 1)

        def weigh(base, t, j, ns):
            pool.wait_ge(n_rr.sem, n_rr.at(base + t + 1))
            e4 = n_e[:, j, 0:2 * ns * CHUNK].rearrange("p (h k) -> p h k", k=S)
            p.tensor_tensor(e4, e4, n_r[:, j, 0:ns * H].unsqueeze(2).broadcast_to([TILE, ns * H, S]), ALU.mult
                            ).then_inc(n_p.sem, 1)

        for layer, ns in ((0, 2), (1, 1)):
            base = layer * NT
            if layer == 1 and stages < 5:
                return
            if layer == 0:
                pool.wait_ge(xt_rdy.sem, xt_rdy.at(4 * NT))
            else:
                pool.wait_ge(n_vp.sem, n_vp.at(base))
            stationary(base, 0, 0, ns)
            stationary(base, 1, 1, ns)
            weigh(base, 0, 0, ns)
            with pool.Fori(0, NT // 2 - 1) as i:
                for j in range(2):
                    stationary(base, 2 * i + j + 2, j, ns)
                    weigh(base, 2 * i + j + 1, 1 - j, ns)
            weigh(base, NT - 1, 1, ns)
        if stages < 6:
            return

        pool.wait_ge(xt_rdy.sem, xt_rdy.at(6 * NT))
        p.memset(e_z[:], 0.0).then_inc(e_zr.sem, 1)
        with pool.Fori(0, NT // 2) as i:
            for j in range(2):
                t = 2 * i + j
                pool.wait_ge(r_mm.sem, r_mm.at(t - 1))
                p.tensor_copy(r_xf[:, j, :, :], x_feat[:, :, bass.ds(TILE * t, TILE)]).then_inc(r_cp.sem, 1)
        with pool.Fori(0, NCH) as c:
            with pool.Fori(0, NEX // 2) as i:
                for j in range(2):
                    u = NEX * c + 2 * i + j
                    pool.wait_ge(e_sl.sem, e_sl.at(u + 1))
                    pool.wait_ge(e_tld[j].sem, e_tld[j].at(8 * (u - j) + 16))
                    pool.wait_ge(e_hr.sem, e_hr.at(u - 1))
                    p.tensor_tensor(e_aw[:, j, :], e_act[:, j, :], e_tw[:, j, :], ALU.mult).then_inc(e_awr.sem, 1)

    @block.tensor
    def _(pe):
        mm = nc.tensor.matmul

        def take_waits():
            pe.sem_inc(pe_passed.sem, 1)

        def norm(k):
            if k == stages:
                return
            for t in range(NT):
                pe.wait_ge(xn_rdy.sem, xn_rdy.at(k * NT + t + 1))
                if t >= 4 or k:
                    pe.wait_ge(xt_rdy.sem, xt_rdy.at(k * NT + t - t % 2 - 2))
                for q in range(KD):
                    src = xn[:, t % 2, 128 * q:128 * q + 128] if k == 0 else x_tok[:, t, 128 * q:128 * q + 128]
                    at = TILE * (2 * q + t % 2)
                    ins = nc.tensor.transpose(ps[:, XT[t // 2 % 2], at:at + TILE], src, ident[0:TILE, 0:TILE])
                ins.then_inc(xt_mm.sem, 1)

        pe.wait_ge(c_ld.sem, c_ld.at(48))
        norm(0)

        pe.wait_ge(w_ld[0].sem, w_ld[0].at(9 * 16))
        for c in range(NCH):
            pe.wait_ge(xt_rdy.sem, xt_rdy.at(TPC * (c + 1)))
            for k in range(KD):
                ins = mm(ps[0:DI, c, 0:CHUNK], m_in[:, k, :], x_feat[:, k, CHUNK * c:CHUNK * c + CHUNK],
                         start=k == 0, stop=k == KD - 1)
            ins.then_inc(m_mm.sem, 1)
        pe.wait_ge(m_silu.sem, m_silu.at(1))
        pe.wait_ge(m_ev.sem, m_ev.at(NCH))
        for c in range(NCH):
            mm(ps[0:DTR + 2 * NS, c, 0:CHUNK], m_xp[:], m_u[:, CHUNK * c:CHUNK * c + CHUNK],
               start=True, stop=True).then_inc(m_mm.sem, 1)
        for c in range(NCH):
            pe.wait_ge(m_dbc_ev.sem, m_dbc_ev.at(c + 1))
            mm(ps[0:DI, 4 + c, 0:CHUNK], m_dt[:], m_dbc[0:DTR, CHUNK * c:CHUNK * c + CHUNK],
               start=True, stop=True).then_inc(m_mm.sem, 1)
        pe.wait_ge(m_silu.sem, m_silu.at(2))
        for c in range(NCH):
            mm(ps[0:DI, c, 0:CHUNK], ident[0:DI, 0:DI], m_ud[:, CHUNK * c:CHUNK * c + CHUNK],
               start=True, stop=False, skip_group_check=True)

        def add_state(n, j, last):
            pe.wait_ge(m_hc.sem, m_hc.at(n + 1))
            for c in range(NCH):
                ins = mm(ps[0:DI, c, 0:CHUNK], ident[0:DI, 0:DI], m_h[:, j, CHUNK * c:CHUNK * c + CHUNK],
                         start=False, stop=last, skip_group_check=True)
            ins.then_inc(m_ymm.sem, 1)

        with pe.Fori(0, NS // 2 - 1) as i:
            for j in range(2):
                add_state(2 * i + j, j, False)
        add_state(NS - 2, 0, False)
        add_state(NS - 1, 1, True)
        pe.wait_ge(m_dl.sem, m_dl.at(2))
        with pe.Fori(0, NT // 2) as i:
            for j in range(2):
                t = 2 * i + j
                pe.wait_ge(m_yev.sem, m_yev.at(t + 1))
                pe.wait_ge(tail_used.sem, tail_used.at(t - 1))
                mm(ps[0:TILE, TAIL[j], 0:D], m_y[:, j, :], m_out[:], start=True, stop=True).then_inc(tail_rdy.sem, 1)
        norm(1)
        if stages < 2:
            return

        pe.wait_ge(xt_rdy.sem, xt_rdy.at(2 * NT))
        def join(pair, j):
            pe.wait_ge(a_ld[j].sem, a_ld[j].at(96 * (pair + 1)))
            pe.wait_ge(a_wl.sem, a_wl.at(2 * pair + j))
            pe.wait_ge(a_prep_ev.sem, a_prep_ev.at(2 * pair + j))
            for k in range(KD):
                mm(ps[:, 6, DCQ * k:DCQ * k + DCQ], a_wq[:, j, 128 * k:128 * k + 128], a_wkq[:, j, :],
                   start=True, stop=True)
            for k in range(2):
                mm(ps[0:HALFQ, 7, DC * k:DC * k + DC], a_wqr[:, j, HALFQ * k:HALFQ * k + HALFQ], a_wkr[:, j, :],
                   start=True, stop=True)
            mm(ps[64 * j:64 * j + 64, 7, 256:512], a_wkv[:, j, :], a_wo[:, j, :], start=True, stop=True
               ).then_inc(a_prep.sem, 1)

        def latent(i, j, c):
            u, q = 8 * i + 4 * j + c, c % 2
            pe.wait_ge(a_wl.sem, a_wl.at(2 * i + j + 1))
            pe.wait_ge(a_xl.sem, a_xl.at(c + 1))
            pe.wait_ge(a_pr.sem, a_pr.at(u - 1))
            cols = slice(CHUNK * c, CHUNK * c + CHUNK)
            for half in range(2):
                rows = slice(HALFQ * half, HALFQ * half + HALFQ)
                parts = [(w[:, j, k, rows], x[:, k, cols]) for k in range(KD)
                         for w, x in ((a_whi, a_xhi), (a_whi, a_xlo), (a_wlo, a_xhi))]
                for n, (w, x) in enumerate(parts):
                    ins = mm(ps[0:HALFQ, 2 * q + half, 0:CHUNK], w, x, start=n == 0, stop=n == len(parts) - 1)
            ins.then_inc(a_qb.sem, 1)

        def query(i, j, c):
            u, q = 8 * i + 4 * j + c, c % 2
            pe.wait_ge(a_rt.sem, a_rt.at(u + 1))
            pe.wait_ge(a_qev.sem, a_qev.at(u - 1))
            for half in range(2):
                ins = mm(ps[:, 4 + q, 0:CHUNK], a_w2[:, j, half, :, :].rearrange("p e d -> p (e d)"),
                         a_rot[:, q, half, :], start=half == 0, stop=half == 1)
            ins.then_inc(a_qq.sem, 1)

        def two_heads(i, last):
            for u in range(2 * NCH):
                latent(i, u // NCH, u % NCH)
                if u:
                    query(i, (u - 1) // NCH, (u - 1) % NCH)
                if u == 1:
                    join(i, 1)
                if u == NCH + 1 and not last:
                    join(i + 1, 0)
            query(i, 1, NCH - 1)

        join(0, 0)
        with pe.Fori(0, H // 2 - 1) as i:
            two_heads(i, False)
        two_heads(H // 2 - 1, True)

        def key_transposes(nb, nj):
            pe.wait_ge(b_kvr_rdy.sem, b_kvr_rdy.at(nb + 1))
            pe.wait_ge(b_row.sem, b_row.at(3 * nb))
            take_waits()
            for r in range(3):
                for q in range(4):
                    ins = nc.tensor.transpose(ps[0:DC, r, KP * q:KP * q + KP], b_kvr[:, nj, 4 * r + q, 0:DC],
                                              ident[0:KP, 0:KP])
                ins.then_inc(b_rmm.sem, 1)

        def row_scores(nb, nj, i, outputs_before):
            pe.wait_ge(b_q_rdy.sem, b_q_rdy.at(nb + 1))
            for r in range(3):
                if i == 0:
                    pe.wait_ge(b_klev.sem, b_klev.at(3 * nb + r + 1))
                elif i == 2 and r < 2 and outputs_before:
                    pe.wait_ge(b_cev.sem, b_cev.at(2 * (nb - 2) + r + 1))
                else:
                    pe.wait_ge(b_mxd.sem, b_mxd.at(24 * nb + 3 * (i - 1) + r + 1))
                mm(ps[0:TILE, r, 0:4 * KP], b_q[0:MROW, nj, TILE * i:TILE * i + TILE],
                   b_khi[0:MROW, nj, 4 * KP * r:4 * KP * r + 4 * KP], start=True, stop=True).then_inc(b_rmm.sem, 1)

        def sums_transposes(b, reduced):
            pe.wait_ge(b_oev.sem, b_oev.at(2 * (b + 1)))
            pe.wait_ge(b_mxd.sem, b_mxd.at(reduced))
            take_waits()
            for i in range(H // 2):
                ins = nc.tensor.transpose(ps[0:TILE, i // 4, (DC + 1) * (i % 4):(DC + 1) * (i % 4) + DC + 1],
                                          b_of[:, i // 4, TILE * (i % 4):TILE * (i % 4) + TILE],
                                          ident[0:DC + 1, 0:DC + 1])
            ins.then_inc(b_otr.sem, 1)

        def maxima_rows(nb, nj):
            pe.wait_ge(b_mxc.sem, b_mxc.at(nb + 1))
            for r, n in enumerate((3, 3, 2)):
                for q in range(n):
                    ins = mm(ps[0:1, r, TILE * q:TILE * q + TILE], b_mx[:, nj, 3 * r + q:3 * r + q + 1],
                             ident[0:TILE, 0:TILE], start=True, stop=True)
                ins.then_inc(b_rmm.sem, 1)

        def key_scores(b, j, c):
            for g in range(2):
                pe.wait_ge(b_exp.sem, b_exp.at(2 * KC * b + 2 * c + g - 2))
                bank = ps[0:KP, 3 + (2 * c + g) % 3, 0:CHUNK]
                mm(bank, b_khi[:, j, KP * c:KP * c + KP],
                   q_all[:, 8 * g:8 * g + 8, bass.ds(S * b, S)], start=True, stop=False)
                mm(bank, b_klo[:, j, KP * c:KP * c + KP],
                   b_q[:, j, CHUNK * g:CHUNK * g + CHUNK], start=False, stop=True).then_inc(b_st.sem, 1)

        def values(b, j, c):
            pe.wait_ge(b_exp.sem, b_exp.at(2 * KC * b + 2 * c + 2))
            if c == 0:
                pe.wait_ge(b_oev.sem, b_oev.at(2 * b))
            for g in range(2):
                ins = mm(ps[0:DC + 1, 6 + g, 0:CHUNK], b_kvr[:, j, c, :], b_pt[:, c % 2, CHUNK * g:CHUNK * g + CHUNK],
                         start=c == 0, stop=c == KC - 1, skip_group_check=True)
            ins.then_inc(b_pv.sem, 1)

        def sequence(b, j, nb, first=False):
            pe.wait_ge(b_row.sem, b_row.at(3 * (b + 1)))
            for c in range(KC):
                key_scores(b, j, c)
                if nb is not None:
                    if c == 1:
                        key_transposes(nb, 1 - j)
                    elif 2 <= c <= 9:
                        if c == 4 and not first:
                            sums_transposes(b - 1, 24 * nb + 5)
                        row_scores(nb, 1 - j, c - 2, not first)
                    elif c == 10:
                        maxima_rows(nb, 1 - j)
                elif c == 3:
                    sums_transposes(b - 1, 24 * NSEQ)
                if c:
                    values(b, j, c - 1)
            values(b, j, KC - 1)

        pe.wait_ge(b_one.sem, b_one.at(2))
        key_transposes(0, 0)
        for i in range(8):
            row_scores(0, 0, i, False)
        maxima_rows(0, 0)
        sequence(0, 0, 1, True)
        with pe.Fori(0, NSEQ // 2 - 1) as i:
            for j in range(2):
                sequence(2 * i + j + 1, 1 - j, 2 * i + j + 2)
        sequence(NSEQ - 1, 1, None)
        pe.wait_ge(b_cev.sem, b_cev.at(2 * (NSEQ - 1)))
        sums_transposes(NSEQ - 1, 24 * NSEQ)
        with pe.Fori(0, NT // 2) as i:
            for j in range(2):
                t = 2 * i + j
                pe.wait_ge(c_in[j].sem, c_in[j].at(16 * (i + 1)))
                pe.wait_ge(c_tev.sem, c_tev.at(t - 1))
                for q in range(H // 2):
                    ins = nc.tensor.transpose(ps[:, 2 * j + q // 4, TILE * (q % 4):TILE * (q % 4) + TILE],
                                              c_ctx[:, j, 128 * q:128 * q + 128], ident[0:TILE, 0:TILE])
                ins.then_inc(c_tr.sem, 1)
            for j in range(2):
                t = 2 * i + j
                pe.wait_ge(c_tev.sem, c_tev.at(t + 1))
                pe.wait_ge(tail_used.sem, tail_used.at(NT + t - 1))
                for q in range(H // 2):
                    ins = mm(ps[0:TILE, TAIL[j], 0:D], c_ctxT[:, j, q, :], w3[:, q, :],
                             start=q == 0, stop=q == H // 2 - 1)
                ins.then_inc(tail_rdy.sem, 1)
        norm(2)
        if stages < 3:
            return

        pe.wait_ge(xt_rdy.sem, xt_rdy.at(3 * NT))
        pe.wait_ge(w_ld[2].sem, w_ld[2].at(7 * 16))
        with pe.Fori(0, NCH) as c:
            for b in range(FB):
                q, m = b % 2, (128 if b < 5 else 64)
                pe.wait_ge(f_sl.sem, f_sl.at(FB * c + b - 1))
                pe.wait_ge(f_hr.sem, f_hr.at(FB * c + b - 1))
                if m < 128:
                    take_waits()
                for w, bank in ((f_g, q), (f_u, 2 + q)):
                    for k in range(KD):
                        ins = mm(ps[0:m, bank, 0:CHUNK], w[:, k, 128 * b:128 * b + m],
                                 x_feat[:, k, bass.ds(CHUNK * c, CHUNK)], start=k == 0, stop=k == KD - 1)
                ins.then_inc(f_gu.sem, 1)
            pe.wait_ge(f_hr.sem, f_hr.at(FB * (c + 1)))
            for s in range(TPC):
                pe.wait_ge(tail_used.sem, tail_used.at(2 * NT + TPC * c + s - 1))
                for b in range(FB):
                    m = 128 if b < 5 else 64
                    ins = mm(ps[0:TILE, TAIL[s % 2], 0:D], f_h[0:m, b, TILE * s:TILE * s + TILE], f_d[0:m, b, :],
                             start=b == 0, stop=b == FB - 1)
                ins.then_inc(tail_rdy.sem, 1)
        norm(3)
        if stages < 4:
            return

        def projections(base, t, j, ns):
            pe.wait_ge(n_qe.sem, n_qe.at(base + t))
            for q in range(2 * ns):
                for k in range(KD):
                    w = n_w[:, q // 2, k, :] if ns == 2 else z_wq[:, k, :]
                    ins = mm(ps[:, 0, TILE * q:TILE * q + TILE], w[:, 128 * (q % 2):128 * (q % 2) + 128],
                             x_feat[:, k, bass.ds(TILE * t, TILE)], start=k == 0, stop=k == KD - 1)
            ins.then_inc(n_qp.sem, 1)
            pe.wait_ge(n_ke.sem, n_ke.at(base + t))
            if ns == 2:
                pe.wait_ge(n_le.sem, n_le.at(t))
                for q in range(2):
                    for k in range(KD):
                        mm(ps[:, 1, TILE * q:TILE * q + TILE], n_w[:, 2, k, 128 * q:128 * q + 128],
                           x_feat[:, k, bass.ds(TILE * t, TILE)], start=k == 0, stop=k == KD - 1)
                pe.wait_ge(n_xfr.sem, n_xfr.at(base + t + 1))
                for k in range(KD):
                    ins = mm(ps[0:TILE, 1, 2 * TILE:2 * TILE + H], n_xf[:, j, k, :], n_lam[:, k, :],
                             start=k == 0, stop=k == KD - 1)
            else:
                for q in range(2):
                    ins = mm(ps[:, 1, TILE * q:TILE * q + TILE], z_wkv[:, 128 * q:128 * q + 128],
                             z_ctx[:, bass.ds(TILE * t, TILE)], start=True, stop=True)
            ins.then_inc(n_kp.sem, 1)

        def value_products(base, t, j, ns):
            pe.wait_ge(n_xfr.sem, n_xfr.at(base + t + 1))
            pe.wait_ge(n_ve.sem, n_ve.at(base + t))
            if ns == 1:
                take_waits()
            for e in range(2):
                if ns == 2:
                    for k in range(KD):
                        ins = mm(ps[0:S, 2, D * e:D * e + D], n_xf[:, j, k, S * e:S * e + S], n_w[:, 3, k, :],
                                 start=k == 0, stop=k == KD - 1)
                else:
                    ins = mm(ps[0:S, 2, D * e:D * e + D], n_xf[0:DC, j, 0, S * e:S * e + S], z_wkv[:, D:2 * D],
                             start=True, stop=True)
            ins.then_inc(n_vp.sem, 1)

        def scores(base, t, j, ns):
            pe.wait_ge(n_qe.sem, n_qe.at(base + t + 1))
            pe.wait_ge(n_kmr.sem, n_kmr.at(base + t + 1))
            pe.wait_ge(n_sub.sem, n_sub.at(base + t))
            for q in range(2 * ns):
                o = ps[0:TILE, 3 + q, 0:CHUNK]
                for e in range(2):
                    mm(o, n_qz[:, j, q, e, :], n_km[:, j, 2 * (q // 2 if ns == 2 else q) + e, :, :].rearrange("p h k -> p (h k)"),
                       start=e == 0, stop=False)
                ins = mm(o, ident_bf[:], n_caus_bf[:].rearrange("p h k -> p (h k)"), start=False, stop=True)
            ins.then_inc(n_sc.sem, 1)

        def attend(layer, t, j, ahead):
            base = layer * NT
            sets = 2 - layer
            for g in range(4 * sets):
                if g == 0:
                    pe.wait_ge(n_p.sem, n_p.at(base + t + 1))
                    pe.wait_ge(n_ve.sem, n_ve.at(base + t + 1 + min(ahead, 1)))
                    take_waits()
                if g == 1:
                    pe.wait_ge(n_qe.sem, n_qe.at(base + t + 1 + ahead))
                    take_waits()
                if g >= 2:
                    pe.wait_ge(n_te.sem, n_te.at(turned(layer, t) + g - 1))
                    take_waits()
                for q in range(4):
                    ins = nc.tensor.transpose(ps[0:S, 2 - 2 * (g % 2), TILE * q:TILE * q + TILE],
                                              n_e[:, j, S * (4 * g + q):S * (4 * g + q) + S], ident[0:TILE, 0:TILE])
                ins.then_inc(n_tr.sem, 1)
            pe.wait_ge(n_te.sem, n_te.at(turned(layer, t) + 4 * sets))
            pe.wait_ge(n_ke.sem, n_ke.at(base + t + 1 + ahead))
            if layer == 0:
                pe.wait_ge(n_le.sem, n_le.at(t + 1 + ahead))
            pe.wait_ge(n_ye.sem, n_ye.at(base + t))
            take_waits()
            for slot in range(0, H, 2):
                r, col = 32 * ((slot // 2) % 4), 256 + TILE * (slot // 8)
                for e in range(2):
                    for o in range(2 * sets):
                        at = slot + o % 2 + H * (o // 2)
                        head = 8 * (o // 2) + at % 8 if sets == 2 else at
                        ins = mm(ps[r:r + 32, 1, col + S * e:col + S * e + S], n_v[:, j, e, head, :],
                                 n_pt[:, at // 4, TILE * (at % 4) + S * e:TILE * (at % 4) + S * e + S],
                                 start=o == 0, stop=o == 2 * sets - 1)
            ins.then_inc(n_pvm.sem, 1)
            pe.wait_ge(n_ye.sem, n_ye.at(base + t + 1))
            pe.wait_ge(tail_used.sem, tail_used.at((3 + layer) * NT + t))
            wo = n_wo if layer == 0 else z_wo
            for k in range(KD):
                ins = mm(ps[0:TILE, 7, 0:D], n_yt[:, j, k, :], wo[:, k, :], start=k == 0, stop=k == KD - 1)
            ins.then_inc(tail_rdy.sem, 1)

        pe.wait_ge(w_ld[3].sem, w_ld[3].at(12 * 16))
        pe.wait_ge(n_zero.sem, n_zero.at(3))
        pe.wait_ge(n_cst.sem, n_cst.at(2))
        for layer, ns in ((0, 2), (1, 1)):
            base = layer * NT
            if layer == 1 and stages < 5:
                return
            pe.wait_ge(xt_rdy.sem, xt_rdy.at((4 + layer) * NT))
            projections(base, 0, 0, ns)
            value_products(base, 0, 0, ns)
            projections(base, 1, 1, ns)
            scores(base, 0, 0, ns)
            value_products(base, 1, 1, ns)
            with pe.Fori(0, NT // 2 - 1) as i:
                for j in range(2):
                    t = 2 * i + j
                    scores(base, t + 1, 1 - j, ns)
                    projections(base, t + 2, j, ns)
                    attend(layer, t, j, 2)
                    value_products(base, t + 2, j, ns)
            scores(base, NT - 1, 1, ns)
            attend(layer, NT - 2, 0, 1)
            attend(layer, NT - 1, 1, 0)
            norm(4 + layer)
        if stages < 6:
            return

        pe.wait_ge(w_ld[5].sem, w_ld[5].at(4 * 16))
        with pe.Fori(0, NT // 2) as i:
            for j in range(2):
                t = 2 * i + j
                pe.wait_ge(r_cp.sem, r_cp.at(t + 1))
                for k in range(KD):
                    ins = mm(ps[0:TILE, 0, bass.ds(NE * t, NE)], r_xf[:, j, k, :], r_w[:, k, :],
                             start=k == 0, stop=k == KD - 1)
                ins.then_inc(r_mm.sem, 1)
        pe.wait_ge(r_sel.sem, r_sel.at(1))
        for c in range(NCH):
            for s in range(TPC):
                ins = nc.tensor.transpose(ps[0:NE, c, TILE * s:TILE * s + TILE], r_m2[:, TPC * c + s, :],
                                          ident[0:TILE, 0:TILE])
            ins.then_inc(r_tr.sem, 1)

        pe.wait_ge(r_te.sem, r_te.at(NCH))
        pe.wait_ge(e_zr.sem, e_zr.at(1))
        with pe.Fori(0, NCH) as c:
            def gate_up(e, j):
                u = NEX * c + e
                pe.wait_ge(e_ld[j].sem, e_ld[j].at(8 * (u - j) + 16))
                pe.wait_ge(e_sl.sem, e_sl.at(u - 1))
                pe.wait_ge(e_hr.sem, e_hr.at(u - 1))
                for w in range(2):
                    for k in range(KD):
                        ins = mm(ps[:, 2 * w + j, 0:CHUNK], e_wgu[:, j, D * w + 128 * k:D * w + 128 * k + 128],
                                 x_feat[:, k, bass.ds(CHUNK * c, CHUNK)], start=k == 0, stop=k == KD - 1)
                ins.then_inc(e_gu.sem, 1)

            def down(e, j, last=False):
                pe.wait_ge(e_dld[j].sem, e_dld[j].at(8 * (NEX * c + e - j) + 16))
                pe.wait_ge(e_hr.sem, e_hr.at(NEX * c + e + 1))
                for g in range(2):
                    ins = mm(ps[:, 4 + g, 0:CHUNK], e_wd[:, j, 128 * g:128 * g + 128], e_h[:, j, :],
                             start=False, stop=last, skip_group_check=True)
                ins.then_inc(e_dn.sem, 1)

            pe.wait_ge(e_yev.sem, e_yev.at(2 * c))
            for g in range(2):
                mm(ps[:, 4 + g, 0:CHUNK], e_z[:, 0:128], e_z[:], start=True, stop=False, skip_group_check=True)
            gate_up(0, 0)
            with pe.Fori(0, NEX // 2 - 1) as i:
                gate_up(2 * i + 1, 1)
                down(2 * i, 0)
                gate_up(2 * i + 2, 0)
                down(2 * i + 1, 1)
            gate_up(NEX - 1, 1)
            down(NEX - 2, 0)
            down(NEX - 1, 1, True)
            pe.wait_ge(e_yev.sem, e_yev.at(2 * (c + 1)))
            for s in range(TPC):
                pe.wait_ge(tail_used.sem, tail_used.at(5 * NT + TPC * c + s - 1))
                for g in range(2):
                    ins = nc.tensor.transpose(ps[0:TILE, 6 + s % 2, 128 * g:128 * g + 128],
                                              e_y[:, g, TILE * s:TILE * s + TILE], ident[:])
                ins.then_inc(tail_rdy.sem, 1)
        norm(6)

    stack.close()


def _rope(length, dim):
    inv = (1.0 / np.float32(10000.0) ** (np.arange(0, dim, 2, dtype=np.float32) / np.float32(dim))).astype(np.float32)
    f = np.arange(length, dtype=np.float32)[:, None] * inv[None, :]
    return np.repeat(np.sin(f), 2, axis=-1), np.repeat(np.cos(f), 2, axis=-1)


def _tables():
    sq, cq = _rope(S, DCQ)
    ropeq = np.stack([cq[:, :HALFQ].T, sq[:, :HALFQ].T, cq[:, HALFQ:].T, sq[:, HALFQ:].T], axis=1)
    sk, ck = _rope(LK, DC)
    signed = np.concatenate([-sk[:, :DC // 2], sk[:, DC // 2:]], axis=-1)
    ropek = np.stack([ck.reshape(KP, KC, DC), signed.reshape(KP, KC, DC)], axis=1)
    q = np.arange(TILE)[:, None] % S
    return {"c_ident": np.eye(128, dtype=np.float32),
            "c_ropeq": ropeq, "c_ropek": ropek,
            "c_headmask": (np.arange(128)[:, None] // HD == np.arange(8)[None, :]).astype(np.float32),
            "c_causal": np.where(np.arange(S)[None, :] <= q, 0.0, NEG).astype(np.float32),
            "c_lower": (np.arange(NG)[None, :] < np.arange(NG)[:, None]).astype(np.float32),
            "c_ones": np.ones((NEX - NE, T), np.float32)}


def kernel(**inputs):
    import concourse.bacc as bacc
    from concourse.bass_utils import run_bass_kernel_spmd

    g = {k: np.asarray(v) for k, v in inputs.items()}
    m, z, f = (lambda n: g["L0_attn_" + n]), (lambda n: g["L0_xattn_" + n]), (lambda n: g["L0_ffn_" + n])
    n, y, e = (lambda k: g["L1_attn_" + k]), (lambda k: g["L1_xattn_" + k]), (lambda k: g["L1_ffn_" + k])
    split = lambda w: w.reshape(w.shape[0], KD, 128, -1).transpose(0, 2, 1, 3).reshape(w.shape[0], 128, -1)
    shared = lambda w: w.reshape(D, 2, IE).transpose(1, 0, 2)
    order = np.r_[0:H:2, 1:H:2]
    even_first = lambda w: w.reshape(D, H, HD)[:, order].reshape(D, D)
    blocks = lambda w: np.pad(w, (0, FB * 128 - INTER)).reshape(FB, 128).T
    gates = split(np.concatenate([e("w_gate"), shared(e("sw_gate"))]))
    ups = split(np.concatenate([e("w_up"), shared(e("sw_up"))]))
    downs = np.concatenate([e("w_down"), e("sw_down").reshape(2, IE, D)])
    laid = {
        "x": g["x"].reshape(T, D), "ctx": g["ctx_512"],
        "ctx_head_T": g["ctx_512"][:, :S].transpose(2, 0, 1).reshape(DC, T),
        "ln_w": m("ln_w").reshape(KD, 128).T, "ln_b": m("ln_b").reshape(KD, 128).T,
        "in_proj_T": m("in_proj_W").T, "conv_w": m("conv_w")[:, 0, :], "conv_b": m("conv_b")[:, None],
        "x_proj_T": m("x_proj_W").T, "dt_proj_T": m("dt_proj_W").T, "dt_proj_b": m("dt_proj_b")[:, None],
        "A_log": m("A_log"), "D_param": m("D_param")[:, None], "out_proj_T": m("out_proj_W").T,
        "Wq": z("Wq").reshape(H, 128, D), "w_kc_q": z("w_kc_q"), "W_qr_T": z("W_qr").transpose(0, 2, 1),
        "W_kr_T": z("W_kr").transpose(0, 2, 1), "w_kc_kv": z("w_kc_kv"), "Wo_T": z("Wo").T.reshape(H, 128, D),
        "gate_T": f("gate_w").T, "up_T": f("up_w").T, "down_T": f("down_w").T,
        "gate_s": blocks(f("gate_s")), "up_s": blocks(f("up_s")), "down_s": f("down_s"),
        "N_Wq1": even_first(n("Wq1")), "N_Wq2": even_first(n("Wq2")), "N_Wk": n("Wk"), "N_Wv": n("Wv"),
        "N_Wlam": n("Wlam")[:, order], "N_Wo": even_first(n("Wo").T).T,
        "Z_Wq_T": y("Wq").T, "Z_Wkv_T": y("Wkv_expand").T, "Z_Wout_T": y("Wout").T,
        "router_w": e("router_w"), "router_bias": e("router_bias"),
        "W_exp": np.concatenate([gates, ups, downs], axis=2),
    }
    laid.update(_tables())
    nc = bacc.Bacc("TRN2", target_bir_lowering=False, num_devices=1)
    arrays, aps = {}, {}
    for name, arr in laid.items():
        arr = np.ascontiguousarray(arr)
        arrays["in_" + name] = arr
        aps[name] = nc.dram_tensor("in_" + name, arr.shape, mybir.dt.from_np(arr.dtype), kind="ExternalInput").ap()
    out = nc.dram_tensor("out_x", (T, D), F32, kind="ExternalOutput").ap()
    build(nc, aps, out)
    r = run_bass_kernel_spmd(nc, [arrays], core_ids=[0])
    return r.results[0]["out_x"].reshape(NSEQ, S, D)
```

```python
import numpy as np

import concourse.bass as bass
from concourse import mybir
from concourse.alu_op_type import AluOpType as ALU

F32 = mybir.dt.float32
F32R = mybir.dt.float32r
BF16 = mybir.dt.bfloat16
ACT = mybir.ActivationFunctionType
AX = mybir.AxisListType

NSEQ, S, D = 32, 56, 256
T = NSEQ * S
TILE = 2 * S
NT = T // TILE
CHUNK = 8 * S
NCH = T // CHUNK
TPC = CHUNK // TILE
KD = D // 128
EPS = 1e-5

DI, NS, DTR, KW = 96, 16, 6, 3
H = 16
LK, DC, DCQ = 1500, 64, 192
KP, KC = 125, 12
HALFQ = DCQ // 2
MROW = 96
NQ = H * S
INTER = 704
FB = 6
HD = D // H
NE, NEX, NG, TOPG, TOPK, IE = 32, 34, 8, 4, 8, 128
ROUTED_SCALE = 2.5
NEG = -1e30
ATANH = [2.00000001, 0.66666316, 0.40024854, 0.27961419, 0.28174657]


class Signal:

    def __init__(self, nc, name, credit=0):
        self.sem, self.credit = nc.alloc_semaphore(name), credit

    def at(self, count):
        return count + self.credit


class Chain:

    def __init__(self, nc, name):
        self.sem, self.base, self.n = nc.alloc_semaphore(name), 0, 0

    def one(self):
        self.n += 1
        return 1

    def all(self):
        return self.base + self.n

    def enter(self, i, per):
        self.start = self.base + self.n
        self.base, self.n, self.per = self.start + i * per, 0, per

    def leave(self, times):
        assert self.n == self.per, (self.n, self.per)
        self.base, self.n = self.start + times * self.per, 0


def build(nc, a, out, stages=6):
    cursor = [((nc.sbuf_base + 63) // 64) * 64]

    def sb(name, shape, dt=F32):
        size = int(np.prod(shape[1:])) * (2 if dt == BF16 else 4)
        size = (size + 63) // 64 * 64
        h = nc.alloc_sbuf_tensor_at(name, shape, dt, offset=cursor[0])
        cursor[0] += size
        return h

    def sig(name, credit=0):
        s = Signal(nc, name, credit)
        if credit:
            rings.append(s)
        return s

    rings = []
    ps = nc.alloc_psum_tensor("ps", [128, 8, 512], F32)

    x_tok = sb("x_tok", [TILE, NT, D])
    feat_base = cursor[0]
    x_feat = sb("x_feat", [128, KD, T])
    ident = sb("ident", [128, 128])
    xn_base = cursor[0]
    xn = sb("xn", [TILE, 2, D])
    ln_stats = sb("ln_stats", [TILE, NT, 6])
    ln_a = sb("ln_a", [TILE, NT])
    ln_b = sb("ln_b", [TILE, NT])
    ln_d = sb("ln_d", [TILE, NT])
    ln_sq = sb("ln_sq", [TILE, NT])
    ln_mean = sb("ln_mean", [TILE, NT])
    ln_var = sb("ln_var", [TILE, NT])
    ln_std = sb("ln_std", [TILE, NT])
    ln_rstd = sb("ln_rstd", [TILE, NT])
    phase_base = cursor[0]

    m_lnw = sb("m_lnw", [128, KD])
    m_lnb = sb("m_lnb", [128, KD])
    m_in = sb("m_in", [128, KD, DI])
    m_cw = sb("m_cw", [DI, KW])
    m_cb = sb("m_cb", [DI, 1])
    m_xp = sb("m_xp", [DI, DTR + 2 * NS])
    m_dt = sb("m_dt", [DTR, DI])
    m_dtb = sb("m_dtb", [DI, 1])
    m_al = sb("m_al", [DI, NS])
    m_a = sb("m_a", [DI, NS])
    m_dp = sb("m_dp", [DI, 1])
    m_out = sb("m_out", [DI, D])
    m_pad = sb("m_pad", [DI, NSEQ, S + 2])
    m_c = sb("m_c", [DI, NSEQ, S])
    m_u = sb("m_u", [DI, T])
    m_t1 = sb("m_t1", [DI, T])
    m_t2 = sb("m_t2", [DI, T])
    m_delta = sb("m_delta", [DI, NSEQ, S])
    m_du = sb("m_du", [DI, T])
    m_ud = sb("m_ud", [DI, T])
    m_ud2 = sb("m_ud2", [DI, T])
    m_sq = sb("m_sq", [DI, T])
    m_dbc = sb("m_dbc", [DTR + 2 * NS, T])
    m_da = sb("m_da", [DI, 2, NSEQ, S])
    m_dbu = sb("m_dbu", [DI, 2, T])
    m_bb = sb("m_bb", [DI, 2, T])
    m_cc = sb("m_cc", [DI, 2, T])
    m_h = sb("m_h", [DI, 2, T])
    m_y = sb("m_y", [DI, 2, TILE])
    m_end = cursor[0]

    cursor[0] = phase_base
    q_all = sb("q_all", [128, H, T], F32R)
    w3 = sb("w3", [128, H // 2, D])
    after_q = cursor[0]
    a_whi = sb("a_whi", [128, 2, KD, DCQ], F32R)
    a_wlo = sb("a_wlo", [128, 2, KD, DCQ], F32R)
    a_w2 = sb("a_w2", [HALFQ, 2, 2, 2, DC])
    a_prod = sb("a_prod", [HALFQ, 2, 4, CHUNK])
    a_rot = sb("a_rot", [HALFQ, 2, 2, CHUNK])
    cursor[0] = xn_base
    a_rope = sb("a_rope", [HALFQ, 4, S])
    cursor[0] = m_end
    a_wq = sb("a_wq", [128, 2, D])
    a_wkq = sb("a_wkq", [128, 2, DCQ])
    a_wqr = sb("a_wqr", [64, 2, DCQ])
    a_wkr = sb("a_wkr", [64, 2, DC])
    a_wkv = sb("a_wkv", [128, 2, DC])
    a_wo = sb("a_wo", [128, 2, D])
    a_xhi = sb("a_xhi", [128, KD, T], F32R)
    cursor[0] = feat_base
    a_xlo = sb("a_xlo", [128, KD, T], F32R)
    cursor[0] = after_q
    b_q = sb("b_q", [128, 2, NQ], F32R)
    b_of = sb("b_of", [DC + 1, 2, CHUNK])
    b_klo = sb("b_klo", [128, 2, KC * KP], F32R)
    b_pt = sb("b_pt", [KP, 2, NQ])
    b_ctx = sb("b_ctx", [TILE, 2, H // 2, DC])
    b_kv = sb("b_kv", [KP, 2, KC, DC])
    b_rope = sb("b_rope", [KP, 2, KC, DC])
    b_tmp = sb("b_tmp", [KP, KC, DC])
    b_kvr = sb("b_kvr", [KP, 2, KC, DC + 1])
    cursor[0] = feat_base
    b_khi = sb("b_khi", [128, 2, KC * KP], F32R)
    b_mx3 = sb("b_mx3", [TILE, 2, H // 2, 3])
    b_mx = sb("b_mx", [TILE, 2, H // 2])
    b_rs = sb("b_rs", [TILE, 2, H // 2])
    cursor[0] = after_q
    c_ctx = sb("c_ctx", [TILE, 2, H * DC])
    c_ctxT = sb("c_ctxT", [128, 2, H // 2, TILE])

    f_g = sb("f_g", [128, KD, INTER])
    f_u = sb("f_u", [128, KD, INTER])
    f_d = sb("f_d", [128, FB, D])
    f_gs = sb("f_gs", [128, FB])
    f_us = sb("f_us", [128, FB])
    f_ds = sb("f_ds", [TILE, D])
    f_act = sb("f_act", [128, 2, CHUNK])
    f_h = sb("f_h", [128, FB, CHUNK])
    f_y = sb("f_y", [TILE, 2, D])

    cursor[0] = phase_base
    n_w = sb("n_w", [128, 4, KD, D])
    n_lam = sb("n_lam", [128, KD, H])
    n_wo = sb("n_wo", [128, KD, D])
    z_wq = sb("z_wq", [128, KD, D])
    z_wkv = sb("z_wkv", [DC, 2 * D])
    z_wo = sb("z_wo", [128, KD, D])
    z_ctx = sb("z_ctx", [DC, T])
    n_hm = sb("n_hm", [128, 8])
    n_caus = sb("n_caus", [TILE, S])
    ident_bf = sb("ident_bf", [TILE, TILE], BF16)
    n_caus_bf = sb("n_caus_bf", [TILE, 8, S], BF16)
    n_xf = sb("n_xf", [128, 2, KD, TILE])
    n_kf = sb("n_kf", [128, 2, 2, TILE])
    n_qz = sb("n_qz", [128, 2, 4, 2, TILE])
    n_km = sb("n_km", [128, 2, 4, 8, S])
    n_v = sb("n_v", [S, 2, 2, H, 2 * HD])
    n_e = sb("n_e", [TILE, 2, 4 * CHUNK])
    n_mx = sb("n_mx", [TILE, 2, 32])
    n_sum = sb("n_sum", [TILE, 2, 32])
    n_r = sb("n_r", [TILE, 2, 32])
    n_l = sb("n_l", [TILE, 2, 16])
    n_l2 = sb("n_l2", [TILE, 2, 16])
    n_l3 = sb("n_l3", [TILE, 2, 16])
    n_pt = sb("n_pt", [S, 8, CHUNK])
    n_yt = sb("n_yt", [128, 2, 2, TILE])

    assert cursor[0] <= after_q - 4 * (H // 2) * D, "the last block's output weights lie beyond"

    r_w = sb("r_w", [128, KD, NE])
    r_b = sb("r_b", [TILE, NE])
    r_lt = sb("r_lt", [TILE, NG, NG])
    r_s = sb("r_s", [TILE, NT, NE])
    r_sb = sb("r_sb", [TILE, NT, NE])
    r_hi = sb("r_hi", [TILE, NT, NG, 2])
    r_lo = sb("r_lo", [TILE, NT, NG, 2])
    r_g1 = sb("r_g1", [TILE, NT, NG])
    r_g2 = sb("r_g2", [TILE, NT, NG])
    r_g3 = sb("r_g3", [TILE, NT, NG])
    r_c1 = sb("r_c1", [TILE, NT, NG, NG])
    r_c2 = sb("r_c2", [TILE, NT, NG, NG])
    r_top = sb("r_top", [TILE, NT, 8])
    r_m = sb("r_m", [TILE, NT, NE])
    r_m2 = sb("r_m2", [TILE, NT, NE])
    r_den = sb("r_den", [TILE, NT])
    r_rden = sb("r_rden", [TILE, NT])
    r_wt = sb("r_wt", [NEX, T])
    cursor[0] = phase_base
    e_xhi = sb("e_xhi", [128, KD, T], F32R)
    e_wgu = sb("e_wgu", [128, 2, 2 * D])
    e_wd = sb("e_wd", [128, 2, D])
    e_guhi = sb("e_guhi", [128, 2, 2 * D], F32R)
    e_gulo = sb("e_gulo", [128, 2, 2 * D], F32R)
    e_dhi = sb("e_dhi", [128, 2, D], F32R)
    e_dlo = sb("e_dlo", [128, 2, D], F32R)
    e_tw = sb("e_tw", [128, 2, CHUNK])
    e_act = sb("e_act", [128, 2, CHUNK])
    e_up = sb("e_up", [128, 2, CHUNK])
    e_h = sb("e_h", [128, 2, CHUNK])
    e_hhi = sb("e_hhi", [128, 2, CHUNK], F32R)
    e_hlo = sb("e_hlo", [128, 2, CHUNK], F32R)
    e_y = sb("e_y", [128, 2, CHUNK])
    cursor[0] = feat_base
    e_xlo = sb("e_xlo", [128, KD, T], F32R)

    bc_dram = nc.dram_tensor("bc_rows", (2 * NS, T), F32, kind="Internal").ap()
    ctx_dram = nc.dram_tensor("ctx_rows", (T, H, DC), F32, kind="Internal").ap()
    rw_dram = nc.dram_tensor("route_rows", (NEX, T), F32, kind="Internal").ap()

    x_ld = sig("x_ld")
    tail_rdy = sig("tail_rdy", 2)
    tail_used = sig("tail_used", 2)
    ln_st = sig("ln_st")
    std_req, std_rdy = sig("std_req"), sig("std_rdy")
    xn_rdy = sig("xn_rdy")
    xt_mm = sig("xt_mm")
    xt_rdy = sig("xt_rdy")
    w_ld = [sig(f"w_ld{k}") for k in range(6)]
    c_ld = sig("c_ld")

    m_ev, m_mm = sig("m_ev"), sig("m_mm")
    m_padz, m_convd, m_exp, m_silu, m_abs, m_ln, m_dl = (sig(n) for n in (
        "m_padz", "m_convd", "m_exp", "m_silu", "m_abs", "m_ln", "m_dl"))
    m_dbc_ev, m_bc_st = sig("m_dbc_ev"), sig("m_bc_st")
    m_bld = [sig(f"m_bld{j}") for j in range(2)]
    m_cld = [sig(f"m_cld{j}") for j in range(2)]
    m_dbu_rdy, m_scan, m_hc, m_ymm = sig("m_dbu_rdy", 2), sig("m_scan", 2), sig("m_hc", 2), sig("m_ymm", 2)
    m_da_rdy, m_yev = sig("m_da_rdy"), sig("m_yev")

    a_ld = [sig(f"a_ld{j}") for j in range(2)]
    a_prep, a_prep_ev = sig("a_prep", 2), sig("a_prep_ev", 2)
    a_qb, a_pr, a_rt, a_qq, a_qev = sig("a_qb"), sig("a_pr", 2), sig("a_rt", 2), sig("a_qq", 2), sig("a_qev", 2)
    a_qhi, a_xh, a_xl, a_wl = sig("a_qhi"), sig("a_xh"), sig("a_xl"), sig("a_wl", 1)

    b_ld = [sig(f"b_ld{j}") for j in range(2)]
    b_kvr_rdy, b_q_rdy = sig("b_kvr_rdy", 1), sig("b_q_rdy")
    b_rmm = sig("b_rmm")
    b_ktev, b_klev, b_mxd, b_mxc, b_row = sig("b_ktev"), sig("b_klev"), sig("b_mxd"), sig("b_mxc"), sig("b_row")
    b_st, b_exp, b_pv, b_cev = sig("b_st", 1), sig("b_exp", 3), sig("b_pv", 2), sig("b_cev", 1)
    b_cst = [sig(f"b_cst{j}", 1) for j in range(2)]
    b_one, b_oev, b_otr = sig("b_one"), sig("b_oev", 1), sig("b_otr", 1)
    c_in = [sig(f"c_in{j}") for j in range(2)]
    c_tr, c_tev = sig("c_tr", 2), sig("c_tev", 2)

    f_gu, f_sl, f_hr = sig("f_gu"), sig("f_sl", 2), sig("f_hr", 2)

    n_cst = sig("n_cst")
    n_qp, n_kp, n_vp = sig("n_qp"), sig("n_kp"), sig("n_vp", 2)
    n_zero = sig("n_zero")
    n_xfr, n_qe, n_ke, n_ve, n_kmr = sig("n_xfr"), sig("n_qe"), sig("n_ke"), sig("n_ve"), sig("n_kmr", 2)
    n_sc, n_sub, n_exp, n_rr, n_p = sig("n_sc", 2), sig("n_sub"), sig("n_exp"), sig("n_rr", 2), sig("n_p")
    n_tr, n_te, n_td, n_pvm, n_ye, n_le = sig("n_tr"), sig("n_te"), sig("n_td"), sig("n_pvm", 2), sig("n_ye", 1), sig("n_le")

    r_mm = sig("r_mm")
    r_ex, r_sel, r_tr, r_te, r_st = (sig(n) for n in ("r_ex", "r_sel", "r_tr", "r_te", "r_st"))
    e_ld = [sig(f"e_ld{j}") for j in range(2)]
    e_tld = [sig(f"e_tld{j}") for j in range(2)]
    e_dld = [sig(f"e_dld{j}") for j in range(2)]
    e_xh, e_xl = sig("e_xh"), sig("e_xl")
    e_guh, e_gul, e_dh, e_dl = sig("e_guh"), sig("e_gul", 1), sig("e_dh"), sig("e_dl", 1)
    e_gu, e_sl, e_upr, e_hr, e_dn = sig("e_gu", 2), sig("e_sl", 2), sig("e_upr", 2), sig("e_hr", 2), sig("e_dn", 2)
    e_hh, e_hl = sig("e_hh"), sig("e_hl", 2)
    e_yev = sig("e_yev", 1)
    pe_passed = sig("pe_passed")
    out_st = sig("out_st")

    import contextlib
    stack = contextlib.ExitStack()
    block = stack.enter_context(nc.Block())

    def turned(layer, t):
        return 8 * t if layer == 0 else 8 * NT + 4 * t

    ACT_GROUPS = ((0, 1, 2, 4, 6), (0, 1, 2))
    DVE_GROUPS = ((3, 5, 7), (3,))

    def taken(groups, layer, t, g):
        before = len(groups[0]) * t if layer == 0 else len(groups[0]) * NT + len(groups[1]) * t
        return before + sum(k <= g for k in groups[layer])

    TAIL = [4, 5]
    XT = [6, 7]

    @block.sync
    def _(sp):
        def store_result():
            for c in range(NCH):
                sp.wait_ge(xn_rdy.sem, xn_rdy.at(stages * NT + TPC * (c + 1)))
                sp.dma_start(out.rearrange("(t p) d -> p t d", p=TILE)[:, TPC * c:TPC * c + TPC, :],
                             x_tok[:, TPC * c:TPC * c + TPC, :]).then_inc(out_st.sem, 16)
            sp.wait_ge(out_st.sem, out_st.at(16 * NCH))

        for s in rings:
            sp.sem_inc(s.sem, s.credit)
        sp.dma_start(x_tok[:], a["x"].rearrange("(t p) d -> p t d", p=TILE)).then_inc(x_ld.sem, 16)
        for dst, src in ((ident[:], a["c_ident"]), (m_lnw[:], a["ln_w"]), (m_lnb[:], a["ln_b"])):
            sp.dma_start(dst, src).then_inc(c_ld.sem, 16)
        for dst, src in ((m_in[:], a["in_proj_T"].rearrange("(k p) n -> p k n", p=128)),
                         (m_cw[:], a["conv_w"]), (m_cb[:], a["conv_b"]), (m_xp[:], a["x_proj_T"]),
                         (m_dt[:], a["dt_proj_T"]), (m_dtb[:], a["dt_proj_b"]), (m_al[:], a["A_log"]),
                         (m_dp[:], a["D_param"]), (m_out[:], a["out_proj_T"])):
            sp.dma_start(dst, src).then_inc(w_ld[0].sem, 16)

        sp.wait_ge(m_dbc_ev.sem, m_dbc_ev.at(NCH))
        sp.dma_start(bc_dram, m_dbc[DTR:DTR + 2 * NS, :]).then_inc(m_bc_st.sem, 16)
        sp.wait_ge(m_bc_st.sem, m_bc_st.at(16))
        with sp.Fori(0, NS // 2) as i:
            for j in range(2):
                n = 2 * i + j
                sp.wait_ge(m_dbu_rdy.sem, m_dbu_rdy.at(n - 1))
                sp.dma_start(m_bb[:, j, :], bc_dram[n].partition_broadcast(DI)).then_inc(m_bld[j].sem, 16)
                sp.wait_ge(m_hc.sem, m_hc.at(n - 1))
                sp.dma_start(m_cc[:, j, :], bc_dram[n + NS].partition_broadcast(DI)).then_inc(m_cld[j].sem, 16)
        if stages < 2:
            store_result()
            return

        sp.dma_start(a_rope[:], a["c_ropeq"]).then_inc(w_ld[1].sem, 16)
        with sp.Fori(0, H // 2) as i:
            for j in range(2):
                h = 2 * i + j
                sp.wait_ge(a_prep.sem, a_prep.at(2 * i + j - 1))
                for dst, src in ((a_wq[:, j, :], a["Wq"][h]), (a_wkq[:, j, :], a["w_kc_q"][h]),
                                 (a_wqr[:, j, :], a["W_qr_T"][h]), (a_wkr[:, j, :], a["W_kr_T"][h]),
                                 (a_wkv[:, j, :], a["w_kc_kv"][h]), (a_wo[:, j, :], a["Wo_T"][h])):
                    sp.dma_start(dst, src).then_inc(a_ld[j].sem, 16)

        sp.wait_ge(a_qb.sem, a_qb.at(H * NCH))
        sp.dma_start(b_rope[:], a["c_ropek"]).then_inc(w_ld[1].sem, 16)

        def load_kv(b, j):
            sp.dma_start(b_kv[:, j, :, :], a["ctx"][b].rearrange("(p c) d -> p c d", c=KC)).then_inc(b_ld[j].sem, 16)

        def store_ctx(b, j):
            sp.wait_ge(b_cev.sem, b_cev.at(2 * (b + 1)))
            for e in range(2):
                sp.dma_start(ctx_dram.rearrange("(b s) (i e) d -> b e s i d", s=S, e=2)[b, e],
                             b_ctx[S * e:S * e + S, j, :, :]).then_inc(b_cst[j].sem, 16)

        load_kv(0, 0)
        load_kv(1, 1)
        with sp.Fori(0, NSEQ // 2 - 1) as i:
            for j in range(2):
                b = 2 * i + j
                sp.wait_ge(b_kvr_rdy.sem, b_kvr_rdy.at(b + 1))
                load_kv(b + 2, j)
                store_ctx(b, j)
        for j in range(2):
            store_ctx(NSEQ - 2 + j, j)
        sp.wait_ge(b_cst[0].sem, b_cst[0].at(16 * NSEQ))
        sp.wait_ge(b_cst[1].sem, b_cst[1].at(16 * NSEQ))
        sp.wait_ge(b_pv.sem, b_pv.at(NSEQ * KC))
        with sp.Fori(0, NT // 2) as i:
            for j in range(2):
                sp.wait_ge(c_tr.sem, c_tr.at(2 * i + j - 1))
                sp.dma_start(c_ctx[:, j, :], ctx_dram.rearrange("(t p) h d -> t p (h d)", p=TILE)[2 * i + j]
                             ).then_inc(c_in[j].sem, 16)
        if stages < 3:
            store_result()
            return

        for dst, src in ((f_g[:], a["gate_T"].rearrange("(k p) n -> p k n", p=128)),
                         (f_u[:], a["up_T"].rearrange("(k p) n -> p k n", p=128)),
                         (f_d[:, 0:5, :], a["down_T"][0:640].rearrange("(k p) n -> p k n", p=128)),
                         (f_d[0:64, 5, :], a["down_T"][640:704]),
                         (f_gs[:], a["gate_s"]), (f_us[:], a["up_s"]),
                         (f_ds[:], a["down_s"].partition_broadcast(TILE))):
            sp.dma_start(dst, src).then_inc(w_ld[2].sem, 16)
        if stages < 4:
            store_result()
            return

        for k, name in enumerate(("N_Wq1", "N_Wq2", "N_Wk", "N_Wv")):
            sp.dma_start(n_w[:, k, :, :], a[name].rearrange("(k p) n -> p k n", p=128)).then_inc(w_ld[3].sem, 16)
        for dst, src in ((n_lam[:], a["N_Wlam"].rearrange("(k p) n -> p k n", p=128)),
                         (n_wo[:], a["N_Wo"].rearrange("(k p) n -> p k n", p=128)),
                         (z_wq[:], a["Z_Wq_T"].rearrange("(k p) n -> p k n", p=128)),
                         (z_wkv[:], a["Z_Wkv_T"]),
                         (z_wo[:], a["Z_Wout_T"].rearrange("(k p) n -> p k n", p=128)),
                         (z_ctx[:], a["ctx_head_T"]), (n_hm[:], a["c_headmask"]), (n_caus[:], a["c_causal"])):
            sp.dma_start(dst, src).then_inc(w_ld[3].sem, 16)
        if stages < 6:
            store_result()
            return

        sp.wait_ge(xt_rdy.sem, xt_rdy.at(4 * NT))
        for dst, src in ((r_w[:], a["router_w"].rearrange("(k p) n -> p k n", p=128)),
                         (r_b[:], a["router_bias"].partition_broadcast(TILE)),
                         (r_lt[:], a["c_lower"].partition_broadcast(TILE))):
            sp.dma_start(dst, src).then_inc(w_ld[5].sem, 16)
        sp.dma_start(r_wt[NE:NEX, :], a["c_ones"]).then_inc(w_ld[5].sem, 16)

        def load_gate_up(u, e, j):
            if not isinstance(u, int) or u >= 2:
                sp.wait_ge(e_gul.sem, e_gul.at(u - 1))
            sp.dma_start(e_wgu[:, j, :], a["W_exp"][e][:, 0:2 * D]).then_inc(e_ld[j].sem, 16)

        def load_down(u, e, j):
            if not isinstance(u, int) or u >= 2:
                sp.wait_ge(e_dl.sem, e_dl.at(u - 1))
            sp.dma_start(e_wd[:, j, :], a["W_exp"][e][:, 2 * D:3 * D]).then_inc(e_dld[j].sem, 16)

        def load_routing(c, e, j):
            sp.wait_ge(e_upr.sem, e_upr.at(NEX * c + e - 1))
            sp.dma_start(e_tw[:, j, :], rw_dram[e, bass.ds(CHUNK * c, CHUNK)].partition_broadcast(128)
                         ).then_inc(e_tld[j].sem, 16)

        def load_chunk(c, last):
            with sp.Fori(0, NEX // 2 - 1) as i:
                for j in range(2):
                    e = 2 * i + j
                    load_routing(c, e, j)
                    load_gate_up(NEX * c + e + 2, e + 2, j)
                    load_down(NEX * c + e + 1, e + 1, 1 - j)
            for j in range(2):
                e = NEX - 2 + j
                load_routing(c, e, j)
                if not last:
                    load_gate_up(NEX * c + e + 2, j, j)
                if not (last and j == 1):
                    load_down(NEX * c + e + 1, (e + 1) % NEX, 1 - j)

        sp.wait_ge(xt_rdy.sem, xt_rdy.at(6 * NT))
        load_gate_up(0, 0, 0)
        load_gate_up(1, 1, 1)
        load_down(0, 0, 0)
        sp.wait_ge(r_te.sem, r_te.at(NCH))
        sp.dma_start(rw_dram, r_wt[:]).then_inc(r_st.sem, 16)
        sp.wait_ge(r_st.sem, r_st.at(16))
        with sp.Fori(0, NCH - 1) as c:
            load_chunk(c, False)
        load_chunk(NCH - 1, True)
        store_result()

    @block.vector
    def _(dve):
        ch = Chain(nc, "dve_chain")
        v = nc.vector

        def residual(k, t, bank, mul=1.0, col=0):
            dve.wait_ge(tail_rdy.sem, tail_rdy.at((k - 1) * NT + t + 1))
            v.scalar_tensor_tensor(x_tok[:, t, :], x_tok[:, t, :], mul, ps[0:TILE, bank, col:col + D],
                                   ALU.mult, ALU.add).then_inc(tail_used.sem, 1)
            dve.wait_ge(tail_used.sem, tail_used.at((k - 1) * NT + t + 1))
            v.bn_stats(ln_stats[:, t, :], x_tok[:, t, :]).then_inc(ln_st.sem, 1)

        def norm(k):
            dve.wait_ge(ln_st.sem, ln_st.at((k + 1) * NT))
            me, mo, ve, vo = (ln_stats[:, :, q] for q in (1, 4, 2, 5))
            v.tensor_tensor(ln_a[:], me, mo, ALU.add).then_inc(ch.sem, ch.one())
            v.tensor_tensor(ln_d[:], me, mo, ALU.subtract).then_inc(ch.sem, ch.one())
            v.tensor_tensor(ln_b[:], ve, vo, ALU.add).then_inc(ch.sem, ch.one())
            dve.wait_ge(ch.sem, ch.all())
            v.tensor_scalar(ln_mean[:], ln_a[:], 0.5, None, ALU.mult).then_inc(ch.sem, ch.one())
            v.tensor_tensor(ln_sq[:], ln_d[:], ln_d[:], ALU.mult).then_inc(ch.sem, ch.one())
            v.tensor_scalar(ln_b[:], ln_b[:], 1.0 / D, EPS, ALU.mult, ALU.add).then_inc(ch.sem, ch.one())
            dve.wait_ge(ch.sem, ch.all())
            v.scalar_tensor_tensor(ln_var[:], ln_sq[:], 0.25, ln_b[:], ALU.mult, ALU.add).then_inc(std_req.sem, 1)
            dve.wait_ge(std_rdy.sem, std_rdy.at(k + 1))
            v.reciprocal(ln_rstd[:], ln_std[:]).then_inc(ch.sem, ch.one())
            dve.wait_ge(ch.sem, ch.all())
            for t in range(NT):
                if k == 0 and t >= 2:
                    dve.wait_ge(xt_mm.sem, xt_mm.at(t - 1))
                v.tensor_scalar(xn[:, t % 2, :] if k == 0 else x_tok[:, t, :], x_tok[:, t, :],
                                ln_mean[:, t:t + 1], ln_rstd[:, t:t + 1], ALU.subtract, ALU.mult
                                ).then_inc(xn_rdy.sem, 1)

        dve.wait_ge(x_ld.sem, x_ld.at(16))
        with dve.Fori(0, NT) as t:
            v.bn_stats(ln_stats[:, t, :], x_tok[:, t, :]).then_inc(ln_st.sem, 1)
        norm(0)

        dve.wait_ge(w_ld[0].sem, w_ld[0].at(9 * 16))
        dve.wait_ge(m_ev.sem, m_ev.at(NCH))
        dve.wait_ge(m_padz.sem, m_padz.at(2))
        v.tensor_scalar(m_c[:], m_pad[:, :, 0:S], m_cw[:, 0:1], m_cb[:, 0:1], ALU.mult, ALU.add).then_inc(ch.sem, ch.one())
        dve.wait_ge(ch.sem, ch.all())
        v.scalar_tensor_tensor(m_c[:], m_pad[:, :, 1:1 + S], m_cw[:, 1:2], m_c[:], ALU.mult, ALU.add).then_inc(ch.sem, ch.one())
        dve.wait_ge(ch.sem, ch.all())
        v.scalar_tensor_tensor(m_c[:], m_pad[:, :, 2:2 + S], m_cw[:, 2:3], m_c[:], ALU.mult, ALU.add
                               ).then_inc(m_convd.sem, 1)
        dve.wait_ge(m_exp.sem, m_exp.at(1))
        v.tensor_scalar(m_a[:], m_a[:], -1.0, None, ALU.mult).then_inc(ch.sem, ch.one())
        dve.wait_ge(m_silu.sem, m_silu.at(1))
        v.tensor_scalar(m_ud[:], m_u[:], m_dp[:, 0:1], None, ALU.mult).then_inc(m_silu.sem, 1)
        dve.wait_ge(m_mm.sem, m_mm.at(3 * NCH))
        zt = ps[0:DI, 4:8, 0:CHUNK]
        v4 = lambda t: t[:].rearrange("p (c n) -> p c n", c=NCH)
        v.tensor_scalar(v4(m_t1), zt, m_dtb[:, 0:1], 0.0, ALU.add, ALU.min).then_inc(ch.sem, ch.one())
        v.tensor_scalar(v4(m_t2), zt, m_dtb[:, 0:1], 0.0, ALU.add, ALU.max).then_inc(ch.sem, ch.one())
        dve.wait_ge(ch.sem, ch.all())
        v.tensor_tensor(m_t1[:], m_t1[:], m_t2[:], ALU.subtract).then_inc(m_abs.sem, 1)
        dve.wait_ge(m_ln.sem, m_ln.at(1))
        v.tensor_scalar(m_ud2[:], m_t1[:], 2.0, None, ALU.add).then_inc(m_abs.sem, 1)
        dve.wait_ge(m_ln.sem, m_ln.at(3))
        v.tensor_tensor(m_t1[:], m_t1[:], m_sq[:], ALU.mult).then_inc(ch.sem, ch.one())
        dve.wait_ge(ch.sem, ch.all())
        v.tensor_tensor(m_sq[:], m_t1[:], m_t1[:], ALU.mult).then_inc(ch.sem, ch.one())
        dve.wait_ge(ch.sem, ch.all())
        v.tensor_scalar(m_ud2[:], m_sq[:], ATANH[-1], None, ALU.mult).then_inc(ch.sem, ch.one())
        for coef in ATANH[-2:0:-1]:
            dve.wait_ge(ch.sem, ch.all())
            v.scalar_tensor_tensor(m_ud2[:], m_ud2[:], coef, m_sq[:], ALU.add, ALU.mult).then_inc(ch.sem, ch.one())
        dve.wait_ge(ch.sem, ch.all())
        v.scalar_tensor_tensor(m_t1[:], m_ud2[:], ATANH[0], m_t1[:], ALU.add, ALU.mult).then_inc(ch.sem, ch.one())
        dve.wait_ge(ch.sem, ch.all())
        v.tensor_tensor(m_t2[:], m_t2[:], m_t1[:], ALU.add).then_inc(ch.sem, ch.one())
        dve.wait_ge(ch.sem, ch.all())
        flat_delta = m_delta[:].rearrange("p a b -> p (a b)")
        v.tensor_scalar(flat_delta, m_t2[:], 0.001, None, ALU.mult).then_inc(m_dl.sem, 1)
        dve.wait_ge(m_dl.sem, m_dl.at(1))
        v.tensor_tensor(m_du[:], flat_delta, m_u[:], ALU.mult).then_inc(m_dl.sem, 1)
        with dve.Fori(0, NS // 2) as i:
            for j in range(2):
                n = 2 * i + j
                dve.wait_ge(m_da_rdy.sem, m_da_rdy.at(n + 1))
                dve.wait_ge(m_dbu_rdy.sem, m_dbu_rdy.at(n + 1))
                dve.wait_ge(m_ymm.sem, m_ymm.at(n - 1))
                v.tensor_tensor_scan(m_h[:, j, :], m_da[:, j, :, :].rearrange("p a b -> p (a b)"), m_dbu[:, j, :],
                                     0.0, ALU.mult, ALU.add).then_inc(m_scan.sem, 1)
                dve.wait_ge(m_scan.sem, m_scan.at(n + 1))
                dve.wait_ge(m_cld[j].sem, m_cld[j].at(16 * (i + 1)))
                v.tensor_tensor(m_h[:, j, :], m_h[:, j, :], m_cc[:, j, :], ALU.mult).then_inc(m_hc.sem, 1)
        with dve.Fori(0, NT // 2) as i:
            for j in range(2):
                residual(1, 2 * i + j, TAIL[j], 2.0)
        norm(1)
        if stages < 2:
            return

        dve.wait_ge(w_ld[1].sem, w_ld[1].at(16))
        def query_rest(i, v_):
            j, c = v_ // NCH % 2, v_ % NCH
            dve.wait_ge(a_qhi.sem, a_qhi.at(8 * i + v_ + 1))
            rest = q_all[64:128, 2 * i + v_ // NCH, CHUNK * c:CHUNK * c + CHUNK]
            v.tensor_tensor(rest, ps[64:128, 4 + c % 2, 0:CHUNK], rest.bitcast(F32), ALU.subtract
                            ).then_inc(a_qev.sem, 1)

        def weights_rest(h, j):
            dve.wait_ge(a_prep_ev.sem, a_prep_ev.at(h + 1))
            v.tensor_tensor(a_wlo[:, j, :, :], ps[:, 6, 0:KD * DCQ].rearrange("p (k n) -> p k n", k=KD),
                            a_whi[:, j, :, :].bitcast(F32), ALU.subtract).then_inc(a_wl.sem, 1)

        for c in range(NCH):
            dve.wait_ge(a_xh.sem, a_xh.at(c + 1))
            cols = slice(CHUNK * c, CHUNK * c + CHUNK)
            v.tensor_tensor(a_xlo[:, :, cols], x_feat[:, :, cols], a_xhi[:, :, cols].bitcast(F32), ALU.subtract
                            ).then_inc(a_xl.sem, 1)
            if c == 0:
                weights_rest(0, 0)

        def rotate(i, first=False, last=False):
            for j in range(2):
                for c in range(NCH):
                    u = 8 * i + 4 * j + c
                    q = c % 2
                    dve.wait_ge(a_qb.sem, a_qb.at(u + 1))
                    dve.wait_ge(a_rt.sem, a_rt.at(u - 1))
                    for k, (half, tab) in enumerate(((0, 0), (1, 1), (1, 2), (0, 3))):
                        ins = v.tensor_tensor(
                            a_prod[:, q, k, :].rearrange("p (b s) -> p b s", s=S),
                            ps[0:HALFQ, 2 * q + half, 0:CHUNK].rearrange("p (b s) -> p b s", s=S),
                            a_rope[:, tab, :].unsqueeze(1).broadcast_to([HALFQ, 8, S]), ALU.mult)
                    ins.then_inc(a_pr.sem, 1)
                    if j or c > 1 or not first:
                        query_rest(i, 4 * j + c - 2)
                    if c == 1 and not (last and j == 1):
                        weights_rest(2 * i + j + 1, 1 - j)

        rotate(0, first=True)
        with dve.Fori(1, H // 2 - 1) as i:
            rotate(i)
        rotate(H // 2 - 1, last=True)
        query_rest(H // 2 - 1, 6)
        query_rest(H // 2 - 1, 7)

        def maxima(b, j, done=None):
            for r in range(3):
                dve.wait_ge(b_ktev.sem, b_ktev.at(3 * b + r + 1))
                part = slice(4 * KP * r, 4 * KP * r + 4 * KP)
                v.tensor_tensor(b_klo[0:DC, j, part], ps[0:DC, r, 0:4 * KP], b_khi[0:DC, j, part].bitcast(F32),
                                ALU.subtract).then_inc(b_klev.sem, 1)
            for c in range(8):
                if c == 2 and done is not None:
                    outputs(done, j)
                for u in range(3):
                    dve.wait_ge(b_rmm.sem, b_rmm.at(30 * b + 3 + 3 * c + u + 1))
                    v.tensor_reduce(b_mx3[:, j, c, u:u + 1], ps[0:TILE, u, 0:4 * KP], AX.X, ALU.max
                                    ).then_inc(b_mxd.sem, 1)
            dve.wait_ge(b_mxd.sem, b_mxd.at(24 * (b + 1)))
            v.tensor_reduce(b_mx[:, j, :], b_mx3[:, j, :, :], AX.X, ALU.max).then_inc(b_mxc.sem, 1)

        def outputs(b, j):
            dve.wait_ge(b_otr.sem, b_otr.at(b + 1))
            for g in range(2):
                o = ps[0:TILE, g, 0:4 * (DC + 1)].rearrange("p (i d) -> p i d", i=4)
                v.reciprocal(b_rs[:, j, 4 * g:4 * g + 4], o[:, :, DC]).then_inc(ch.sem, ch.one())
            dve.wait_ge(ch.sem, ch.all())
            dve.wait_ge(b_cst[j].sem, b_cst[j].at(16 * (b - j)))
            for g in range(2):
                o = ps[0:TILE, g, 0:4 * (DC + 1)].rearrange("p (i d) -> p i d", i=4)
                v.tensor_tensor(b_ctx[:, j, 4 * g:4 * g + 4, :], o[:, :, 0:DC],
                                b_rs[:, j, 4 * g:4 * g + 4].unsqueeze(2).broadcast_to([TILE, 4, DC]), ALU.mult
                                ).then_inc(b_cev.sem, 1)

        maxima(0, 0)
        dve.wait_ge(xn_rdy.sem, xn_rdy.at(2 * NT))
        maxima(1, 1)
        with dve.Fori(0, NSEQ // 2 - 1) as i:
            ch.enter(i, 4)
            maxima(2 * i + 2, 0, 2 * i)
            maxima(2 * i + 3, 1, 2 * i + 1)
            ch.leave(NSEQ // 2 - 1)
        outputs(NSEQ - 2, 0)
        outputs(NSEQ - 1, 1)
        with dve.Fori(0, NT // 2) as i:
            for j in range(2):
                residual(2, 2 * i + j, TAIL[j])
        norm(2)
        if stages < 3:
            return

        dve.wait_ge(w_ld[2].sem, w_ld[2].at(7 * 16))
        dve.wait_ge(xn_rdy.sem, xn_rdy.at(3 * NT))
        with dve.Fori(0, NCH) as c:
            for b in range(FB):
                q, m = b % 2, (128 if b < 5 else 64)
                dve.wait_ge(f_sl.sem, f_sl.at(FB * c + b + 1))
                if b == 0:
                    dve.wait_ge(tail_rdy.sem, tail_rdy.at(2 * NT + 4 * c))
                v.scalar_tensor_tensor(f_h[0:m, b, :], ps[0:m, 2 + q, 0:CHUNK], f_us[0:m, b:b + 1],
                                       f_act[0:m, q, :], ALU.mult, ALU.mult).then_inc(f_hr.sem, 1)
            ch.enter(c, TPC)
            for s in range(TPC):
                t, j = TPC * c + s, s % 2
                dve.wait_ge(tail_rdy.sem, tail_rdy.at(2 * NT + t + 1))
                v.tensor_tensor(f_y[:, j, :], ps[0:TILE, TAIL[j], 0:D], f_ds[:], ALU.mult).then_inc(ch.sem, ch.one())
                dve.wait_ge(ch.sem, ch.all())
                v.tensor_tensor(x_tok[:, t, :], x_tok[:, t, :], f_y[:, j, :], ALU.add).then_inc(tail_used.sem, 1)
                dve.wait_ge(tail_used.sem, tail_used.at(2 * NT + t + 1))
                v.bn_stats(ln_stats[:, t, :], x_tok[:, t, :]).then_inc(ln_st.sem, 1)
            ch.leave(NCH)
        norm(3)
        if stages < 4:
            return

        dve.wait_ge(w_ld[3].sem, w_ld[3].at(12 * 16))
        v.tensor_copy(n_caus_bf[:], n_caus[:].unsqueeze(1).broadcast_to([TILE, 8, S])).then_inc(n_cst.sem, 1)
        v.tensor_copy(ident_bf[:], ident[0:TILE, 0:TILE]).then_inc(n_cst.sem, 1)

        def turned_out(layer, t):
            dve.wait_ge(n_pvm.sem, n_pvm.at(layer * NT + t))
            for g in DVE_GROUPS[layer]:
                dve.wait_ge(n_tr.sem, n_tr.at(turned(layer, t) + g + 1))
                v.tensor_copy(n_pt[:, g, :], ps[0:S, 0, 0:CHUNK]).then_inc(n_td.sem, 1)

        def softmax(base, t, j, ns, turn=True):
            hh = ns * H
            sc = ps[0:TILE, 3:3 + 2 * ns, 0:CHUNK].rearrange("p q (h k) -> p q h k", k=S)
            dve.wait_ge(n_sc.sem, n_sc.at(base + t + 1))
            v.tensor_reduce(n_mx[:, j, 0:hh].rearrange("p (q h) -> p q h", h=8), sc, AX.X, ALU.max).then_inc(ch.sem, ch.one())
            dve.wait_ge(ch.sem, ch.all())
            for q in range(2 * ns):
                ins = v.tensor_tensor(n_e[:, j, CHUNK * q:CHUNK * q + CHUNK].rearrange("p (h k) -> p h k", k=S),
                                      sc[:, q, :, :],
                                      n_mx[:, j, 8 * q:8 * q + 8].unsqueeze(2).broadcast_to([TILE, 8, S]),
                                      ALU.subtract)
            ins.then_inc(n_sub.sem, 1)
            if turn:
                turned_out(2 - ns, t - 1)
            dve.wait_ge(n_exp.sem, n_exp.at(base + t + 1))
            v.tensor_reduce(n_sum[:, j, 0:hh], n_e[:, j, 0:hh * S].rearrange("p (h k) -> p h k", k=S),
                               AX.X, ALU.add).then_inc(ch.sem, ch.one())
            dve.wait_ge(ch.sem, ch.all())
            if ns == 1:
                v.reciprocal(n_r[:, j, 0:H], n_sum[:, j, 0:H]).then_inc(n_rr.sem, 1)
            else:
                v.reciprocal(n_r[:, j, :], n_sum[:, j, :]).then_inc(ch.sem, ch.one())
                dve.wait_ge(n_le.sem, n_le.at(t + 1))
                v.tensor_scalar(n_l2[:, j, :], n_l[:, j, :], 1.0, None, ALU.add).then_inc(ch.sem, ch.one())
                dve.wait_ge(ch.sem, ch.all())
                v.reciprocal(n_l3[:, j, :], n_l2[:, j, :]).then_inc(ch.sem, ch.one())
                dve.wait_ge(ch.sem, ch.all())
                v.scalar_tensor_tensor(n_r[:, j, H:2 * H], n_r[:, j, H:2 * H], -1.0, n_l3[:, j, :],
                                       ALU.mult, ALU.mult).then_inc(n_rr.sem, 1)

        for layer, ns in ((0, 2), (1, 1)):
            per = 2 if ns == 1 else 5
            base = layer * NT
            if layer == 1 and stages < 5:
                return
            softmax(base, 0, 0, ns, False)
            dve.wait_ge(xn_rdy.sem, xn_rdy.at((4 + layer) * NT))
            with dve.Fori(0, NT // 2 - 1) as i:
                ch.enter(i, 2 * per)
                for j in range(2):
                    softmax(base, 2 * i + j + 1, 1 - j, ns)
                    residual(4 + layer, 2 * i + j, 7)
                ch.leave(NT // 2 - 1)
            softmax(base, NT - 1, 1, ns)
            residual(4 + layer, NT - 2, 7)
            turned_out(layer, NT - 1)
            residual(4 + layer, NT - 1, 7)
            norm(4 + layer)
        if stages < 6:
            return

        dve.wait_ge(w_ld[5].sem, w_ld[5].at(4 * 16))
        dve.wait_ge(r_ex.sem, r_ex.at(1))
        flat = lambda t: t[:].rearrange("p a b -> p (a b)")

        def step(ins):
            ins.then_inc(ch.sem, ch.one())
            dve.wait_ge(ch.sem, ch.all())

        step(v.tensor_scalar(flat(r_s), flat(r_m), 1.0, None, ALU.add))
        step(v.reciprocal(flat(r_s), flat(r_s)))
        step(v.tensor_tensor(r_sb[:], r_s[:], r_b[:].unsqueeze(1).broadcast_to([TILE, NT, NE]), ALU.add))
        quad = r_sb[:].rearrange("p t (g e) -> p (t g) e", e=4)
        f3 = lambda t: t[:].rearrange("p t g e -> p (t g) e")
        f2 = lambda t: t[:].rearrange("p t g -> p (t g)")
        v.tensor_tensor(f3(r_hi), quad[:, :, 0:2], quad[:, :, 2:4], ALU.max).then_inc(ch.sem, ch.one())
        step(v.tensor_tensor(f3(r_lo), quad[:, :, 0:2], quad[:, :, 2:4], ALU.min))
        v.tensor_tensor(f2(r_g1), f3(r_hi)[:, :, 0], f3(r_hi)[:, :, 1], ALU.max).then_inc(ch.sem, ch.one())
        v.tensor_tensor(f2(r_g2), f3(r_hi)[:, :, 0], f3(r_hi)[:, :, 1], ALU.min).then_inc(ch.sem, ch.one())
        step(v.tensor_tensor(f2(r_g3), f3(r_lo)[:, :, 0], f3(r_lo)[:, :, 1], ALU.max))
        step(v.tensor_tensor(r_g2[:], r_g2[:], r_g3[:], ALU.max))
        step(v.tensor_tensor(r_g1[:], r_g1[:], r_g2[:], ALU.add))
        other = r_g1[:].unsqueeze(2).broadcast_to([TILE, NT, NG, NG])
        own = r_g1[:].unsqueeze(3).broadcast_to([TILE, NT, NG, NG])
        for t in range(NT):
            v.tensor_tensor(r_c1[:, t, :, :], other[:, t, :, :], own[:, t, :, :], ALU.is_gt).then_inc(ch.sem, ch.one())
            v.tensor_tensor(r_c2[:, t, :, :], other[:, t, :, :], own[:, t, :, :], ALU.is_equal).then_inc(ch.sem, ch.one())
        dve.wait_ge(ch.sem, ch.all())
        c3 = lambda t: t[:].rearrange("p t g e -> p t (g e)")
        step(v.tensor_tensor(c3(r_c2), c3(r_c2), r_lt[:].rearrange("p g e -> p (g e)").unsqueeze(1).broadcast_to(
            [TILE, NT, NG * NG]), ALU.mult))
        step(v.tensor_tensor(f3(r_c1), f3(r_c1), f3(r_c2), ALU.add))
        step(v.tensor_reduce(f2(r_g2), f3(r_c1), AX.X, ALU.add))
        step(v.tensor_scalar(r_g3[:], r_g2[:], TOPG - 0.5, None, ALU.is_lt))
        step(v.tensor_tensor(r_m[:].rearrange("p t (g e) -> p (t g) e", e=4), quad,
                             f2(r_g3).unsqueeze(2).broadcast_to([TILE, NT * NG, 4]), ALU.mult))
        for t in range(NT):
            v.max(r_top[:, t, :], r_m[:, t, :]).then_inc(ch.sem, ch.one())
        dve.wait_ge(ch.sem, ch.all())
        for t in range(NT):
            v.match_replace(r_m2[:, t, :], r_top[:, t, :], r_m[:, t, :], NEG).then_inc(ch.sem, ch.one())
        dve.wait_ge(ch.sem, ch.all())
        step(v.tensor_scalar(r_m2[:], r_m2[:], NEG / 2, None, ALU.is_lt))
        step(v.tensor_tensor(r_m[:], r_m2[:], r_s[:], ALU.mult))
        step(v.tensor_reduce(r_den[:], r_m[:], AX.X, ALU.add))
        step(v.reciprocal(r_rden[:], r_den[:]))
        step(v.tensor_scalar(r_rden[:], r_rden[:], ROUTED_SCALE, None, ALU.mult))
        v.tensor_tensor(r_m2[:], r_m[:], r_rden[:].unsqueeze(2).broadcast_to([TILE, NT, NE]), ALU.mult
                        ).then_inc(r_sel.sem, 1)

        dve.wait_ge(xn_rdy.sem, xn_rdy.at(6 * NT))
        def expert(u, j):
            dve.wait_ge(e_gu.sem, e_gu.at(u + 1))
            dve.wait_ge(e_tld[j].sem, e_tld[j].at(8 * (u - j) + 16))
            dve.wait_ge(e_hr.sem, e_hr.at(u - 1))
            v.tensor_tensor(e_up[:, j, :], ps[:, 2 + j, 0:CHUNK], e_tw[:, j, :], ALU.mult).then_inc(e_upr.sem, 1)
            dve.wait_ge(e_sl.sem, e_sl.at(u + 1))
            dve.wait_ge(e_upr.sem, e_upr.at(u + 1))
            dve.wait_ge(e_hl.sem, e_hl.at(u - 1))
            v.tensor_tensor(e_h[:, j, :], e_up[:, j, :], e_act[:, j, :], ALU.mult).then_inc(e_hr.sem, 1)
            dve.wait_ge(e_hh.sem, e_hh.at(u + 1))
            v.tensor_tensor(e_hlo[:, j, :], e_h[:, j, :], e_hhi[:, j, :].bitcast(F32), ALU.subtract
                            ).then_inc(e_hl.sem, 1)

        def chunk(c, last):
            expert(NEX * c + 1, 1)
            with dve.Fori(1, NEX // 2) as i:
                for j in range(2):
                    expert(NEX * c + 2 * i + j, j)
            if not last:
                expert(NEX * c + NEX, 0)
            for s in range(TPC):
                residual(6, TPC * c + s, 6 + s // 2, col=D * (s % 2))

        expert(0, 0)
        with dve.Fori(0, NCH - 1) as c:
            chunk(c, False)
        chunk(NCH - 1, True)
        norm(6)


    @block.scalar
    def _(act):
        copy = lambda dst, src, **kw: nc.scalar.activation(dst, src, ACT.Copy, **kw)
        ch = Chain(nc, "act_chain")

        def norm(k):
            act.wait_ge(std_req.sem, std_req.at(k + 1))
            nc.scalar.activation(ln_std[:], ln_var[:], ACT.Sqrt).then_inc(std_rdy.sem, 1)
            if k == stages:
                return
            for p in range(NT // 2):
                act.wait_ge(xt_mm.sem, xt_mm.at(k * NT + 2 * p + 2))
                src = ps[:, XT[p % 2], 0:KD * 2 * TILE].rearrange("p (k n) -> p k n", k=KD)
                cols = slice(2 * TILE * p, 2 * TILE * p + 2 * TILE)
                if k == 0:
                    nc.scalar.activation(x_feat[:, 0, cols], src[:, 0, :], ACT.Identity,
                                         scale=m_lnw[:, 0:1], bias=m_lnb[:, 0:1])
                    nc.scalar.activation(x_feat[:, 1, cols], src[:, 1, :], ACT.Identity,
                                         scale=m_lnw[:, 1:2], bias=m_lnb[:, 1:2]).then_inc(xt_rdy.sem, 2)
                else:
                    copy(x_feat[:, :, cols], src).then_inc(xt_rdy.sem, 2)

        act.wait_ge(c_ld.sem, c_ld.at(48))
        norm(0)

        act.wait_ge(m_padz.sem, m_padz.at(2))
        for c in range(NCH):
            act.wait_ge(m_mm.sem, m_mm.at(c + 1))
            copy(m_pad[:, 8 * c:8 * c + 8, 1:1 + S],
                 ps[0:DI, c, 0:CHUNK].rearrange("p (b s) -> p b s", s=S)).then_inc(m_ev.sem, 1)
        act.wait_ge(w_ld[0].sem, w_ld[0].at(9 * 16))
        nc.scalar.activation(m_a[:], m_al[:], ACT.Exp).then_inc(m_exp.sem, 1)
        act.wait_ge(m_convd.sem, m_convd.at(1))
        nc.scalar.activation(m_u[:], m_c[:].rearrange("p a b -> p (a b)"), ACT.Silu).then_inc(m_silu.sem, 1)
        for c in range(NCH):
            act.wait_ge(m_mm.sem, m_mm.at(NCH + c + 1))
            copy(m_dbc[:, CHUNK * c:CHUNK * c + CHUNK], ps[0:DTR + 2 * NS, c, 0:CHUNK]).then_inc(m_dbc_ev.sem, 1)
        act.wait_ge(m_abs.sem, m_abs.at(1))
        nc.scalar.activation(m_t1[:], m_t1[:], ACT.Exp).then_inc(m_ln.sem, 1)
        act.wait_ge(m_abs.sem, m_abs.at(2))
        nc.scalar.activation(m_sq[:], m_ud2[:], ACT.Ln).then_inc(m_ln.sem, 1)
        act.wait_ge(m_ln.sem, m_ln.at(2))
        nc.scalar.activation(m_sq[:], m_sq[:], ACT.Exp, scale=-1.0).then_inc(m_ln.sem, 1)
        act.wait_ge(m_dl.sem, m_dl.at(1))
        act.wait_ge(m_padz.sem, m_padz.at(3))
        with act.Fori(0, NS // 2) as i:
            for j in range(2):
                n = 2 * i + j
                act.wait_ge(m_scan.sem, m_scan.at(n - 1))
                nc.scalar.activation(m_da[:, j, :, 1:S], m_delta[:, :, 1:S], ACT.Exp, scale=m_a[:, bass.ds(n, 1)]
                                     ).then_inc(m_da_rdy.sem, 1)
        act.wait_ge(m_ymm.sem, m_ymm.at(NS))
        with act.Fori(0, NCH) as c:
            for s in range(TPC):
                t, j = TPC * c + s, s % 2
                act.wait_ge(tail_rdy.sem, tail_rdy.at(t - 1))
                copy(m_y[:, j, :], ps[0:DI, c, TILE * s:TILE * s + TILE]).then_inc(m_yev.sem, 1)
        norm(1)
        if stages < 2:
            return

        def weights_out(pair, j):
            act.wait_ge(a_prep.sem, a_prep.at(2 * pair + j + 1))
            copy(a_whi[:, j, :, :], ps[:, 6, 0:KD * DCQ].rearrange("p (k n) -> p k n", k=KD))
            for e in range(2):
                copy(a_w2[:, j, :, e, :], ps[0:HALFQ, 7, 0:2 * DC].rearrange("p (k n) -> p k n", k=2))
            copy(w3[64 * j:64 * j + 64, pair, :], ps[64 * j:64 * j + 64, 7, 256:512]).then_inc(a_prep_ev.sem, 1)

        def queries_out(i, last):
            for j in range(2):
                for c in range(NCH):
                    u = 8 * i + 4 * j + c
                    if c == 0 and not (last and j == 1):
                        weights_out(i + j, 1 - j)
                    act.wait_ge(a_qq.sem, a_qq.at(u + 1))
                    copy(q_all[:, 2 * i + j, CHUNK * c:CHUNK * c + CHUNK], ps[:, 4 + c % 2, 0:CHUNK]
                         ).then_inc(a_qhi.sem, 1)

        act.wait_ge(xt_rdy.sem, xt_rdy.at(2 * NT))
        for c in range(NCH):
            cols = slice(CHUNK * c, CHUNK * c + CHUNK)
            copy(a_xhi[:, :, cols], x_feat[:, :, cols]).then_inc(a_xh.sem, 1)
            if c == 0:
                weights_out(0, 0)
        with act.Fori(0, H // 2 - 1) as i:
            queries_out(i, False)
        queries_out(H // 2 - 1, True)

        def keys_out(nb, nj):
            if not (isinstance(nb, int) and nb == 0):
                act.wait_ge(b_st.sem, b_st.at(2 * KC * (nb - 1)))
            for r in range(3):
                act.wait_ge(b_rmm.sem, b_rmm.at(30 * nb + r + 1))
                for e in range(2):
                    ins = copy(b_khi[64 * e:64 * e + 64, nj, 4 * KP * r:4 * KP * r + 4 * KP],
                               ps[0:DC, r, 0:4 * KP])
                ins.then_inc(b_ktev.sem, 1)

        def rows_out(nb, nj):
            for r, n in enumerate((3, 3, 2)):
                act.wait_ge(b_rmm.sem, b_rmm.at(30 * nb + 27 + r + 1))
                nc.scalar.activation(b_q[MROW:MROW + 1, nj, 3 * TILE * r:3 * TILE * r + n * TILE], ps[0:1, r, 0:n * TILE],
                                     ACT.Copy, scale=-1.0).then_inc(b_row.sem, 1)

        def exps(b, c):
            if c >= 2 or not (isinstance(b, int) and b == 0):
                act.wait_ge(b_pv.sem, b_pv.at(KC * b + c - 2))
            for g in range(2):
                act.wait_ge(b_st.sem, b_st.at(2 * KC * b + 2 * c + g + 1))
                nc.scalar.activation(b_pt[:, c % 2, CHUNK * g:CHUNK * g + CHUNK], ps[0:KP, 3 + (2 * c + g) % 3, 0:CHUNK],
                                     ACT.Exp).then_inc(b_exp.sem, 1)

        def sums_out(b):
            act.wait_ge(b_pv.sem, b_pv.at(KC * (b + 1)))
            if not (isinstance(b, int) and b == 0):
                act.wait_ge(b_otr.sem, b_otr.at(b))
            for g in range(2):
                copy(b_of[:, g, :], ps[0:DC + 1, 6 + g, 0:CHUNK]).then_inc(b_oev.sem, 1)

        def sequence(b, nb, nj):
            for c in range(KC):
                exps(b, c)
                if c == 0 and not (isinstance(b, int) and b == 0):
                    sums_out(b - 1)
                if nb is not None and c == 10:
                    rows_out(nb, nj)
                if nb is not None and c == 1:
                    keys_out(nb, nj)

        act.wait_ge(a_qev.sem, a_qev.at(H * NCH))
        copy(b_klo[64:128, :, :].rearrange("p a b -> p (a b)"),
             ident[64:128, MROW:MROW + 1].broadcast_to([64, 2 * KC * KP]))
        copy(b_q[64:128, :, :].rearrange("p a b -> p (a b)"), ident[64:128, 0:1].broadcast_to([64, 2 * NQ])
             ).then_inc(b_one.sem, 1)
        keys_out(0, 0)
        act.wait_ge(b_one.sem, b_one.at(2))
        rows_out(0, 0)
        sequence(0, 1, 1)
        with act.Fori(0, NSEQ // 2 - 1) as i:
            for j in range(2):
                sequence(2 * i + j + 1, 2 * i + j + 2, j)
        sequence(NSEQ - 1, None, None)
        sums_out(NSEQ - 1)
        with act.Fori(0, NT // 2) as i:
            for j in range(2):
                t = 2 * i + j
                act.wait_ge(c_tr.sem, c_tr.at(t + 1))
                act.wait_ge(tail_rdy.sem, tail_rdy.at(NT + t - 1))
                copy(c_ctxT[:, j, :, :].rearrange("p (q e) n -> p q (e n)", q=2), ps[:, 2 * j:2 * j + 2, 0:CHUNK]
                     ).then_inc(c_tev.sem, 1)
        norm(2)
        if stages < 3:
            return

        act.wait_ge(w_ld[2].sem, w_ld[2].at(7 * 16))
        with act.Fori(0, NCH) as c:
            for b in range(FB):
                q, m = b % 2, (128 if b < 5 else 64)
                act.wait_ge(f_gu.sem, f_gu.at(FB * c + b + 1))
                act.wait_ge(f_hr.sem, f_hr.at(FB * c + b - 1))
                nc.scalar.activation(f_act[0:m, q, :], ps[0:m, q, 0:CHUNK], ACT.Silu, scale=f_gs[0:m, b:b + 1]
                                     ).then_inc(f_sl.sem, 1)
        norm(3)
        if stages < 4:
            return

        def queries_out(base, t, j, ns):
            act.wait_ge(n_qp.sem, n_qp.at(base + t + 1))
            act.wait_ge(n_sc.sem, n_sc.at(base + t - 1))
            src = ps[:, 0, 0:2 * ns * TILE].rearrange("p (q n) -> p q n", n=TILE)
            for e in range(2):
                ins = copy(n_qz[:, j, 0:2 * ns, e, S * e:S * e + S], src[:, :, S * e:S * e + S], scale=HD ** -0.5)
            ins.then_inc(n_qe.sem, 1)

        def keys_lambda_out(base, t, j, ns):
            act.wait_ge(n_kp.sem, n_kp.at(base + t + 1))
            act.wait_ge(n_kmr.sem, n_kmr.at(base + t - 1))
            copy(n_kf[:, j, :, :], ps[:, 1, 0:2 * TILE].rearrange("p (q n) -> p q n", n=TILE)).then_inc(n_ke.sem, 1)
            if ns == 2:
                act.wait_ge(n_rr.sem, n_rr.at(base + t - 1))
                nc.scalar.activation(n_l[:, j, :], ps[0:TILE, 1, 2 * TILE:2 * TILE + H], ACT.Exp, scale=-1.0
                                     ).then_inc(n_le.sem, 1)

        def vals(base, t, j):
            act.wait_ge(n_vp.sem, n_vp.at(base + t + 1))
            act.wait_ge(n_pvm.sem, n_pvm.at(base + t - 1))
            vsrc = ps[0:S, 2, :].rearrange("p (b g e d) -> p b g e d", b=2, g=H // 2, e=2)
            vdst = n_v[:, j, :, :, :].rearrange("p b (g e) d -> p b g e d", e=2)
            for e in range(2):
                ins = copy(vdst[:, :, :, e, HD * e:HD * e + HD], vsrc[:, :, :, e, :])
            ins.then_inc(n_ve.sem, 1)

        def turned_out(layer, t, g):
            act.wait_ge(n_tr.sem, n_tr.at(turned(layer, t) + g + 1))
            copy(n_pt[:, g, :], ps[0:S, 2 - 2 * (g % 2), 0:CHUNK]).then_inc(n_te.sem, 1)

        def exps2(base, t, j, ns):
            act.wait_ge(n_sub.sem, n_sub.at(base + t + 1))
            nc.scalar.activation(n_e[:, j, 0:2 * ns * CHUNK], n_e[:, j, 0:2 * ns * CHUNK], ACT.Exp
                                 ).then_inc(n_exp.sem, 1)

        def finish(layer, t, j, ns, ahead):
            base = layer * NT
            act.wait_ge(n_pvm.sem, n_pvm.at(base + t))
            for g in ACT_GROUPS[layer]:
                turned_out(layer, t, g)
                if g == 2 and ahead == 2:
                    keys_lambda_out(base, t + 2, j, ns)
            if ahead:
                exps2(base, t + 1, 1 - j, ns)
            act.wait_ge(n_pvm.sem, n_pvm.at(base + t + 1))
            act.wait_ge(tail_rdy.sem, tail_rdy.at((3 + layer) * NT + t - 1))
            copy(n_yt[:, j, :, :], ps[:, 1, 256:256 + 2 * TILE].rearrange("p (k n) -> p k n", k=2)).then_inc(n_ye.sem, 1)

        act.wait_ge(n_zero.sem, n_zero.at(3))
        for layer, ns in ((0, 2), (1, 1)):
            base = layer * NT
            if layer == 1 and stages < 5:
                return
            queries_out(base, 0, 0, ns)
            keys_lambda_out(base, 0, 0, ns)
            vals(base, 0, 0)
            queries_out(base, 1, 1, ns)
            keys_lambda_out(base, 1, 1, ns)
            exps2(base, 0, 0, ns)
            vals(base, 1, 1)
            with act.Fori(0, NT // 2 - 1) as i:
                for j in range(2):
                    t = 2 * i + j
                    queries_out(base, t + 2, j, ns)
                    finish(layer, t, j, ns, 2)
                    vals(base, t + 2, j)
            finish(layer, NT - 2, 0, ns, 1)
            finish(layer, NT - 1, 1, ns, 0)
            norm(4 + layer)
        if stages < 6:
            return

        def gate_up_leading(u, j):
            act.wait_ge(e_ld[j].sem, e_ld[j].at(8 * (u - j) + 16))
            act.wait_ge(e_gu.sem, e_gu.at(u - 1))
            copy(e_guhi[:, j, :], e_wgu[:, j, :]).then_inc(e_guh.sem, 1)

        def down_leading(u, j):
            act.wait_ge(e_dld[j].sem, e_dld[j].at(8 * (u - j) + 16))
            act.wait_ge(e_dn.sem, e_dn.at(u - 1))
            copy(e_dhi[:, j, :], e_wd[:, j, :]).then_inc(e_dh.sem, 1)

        def expert(u, j, last=False):
            act.wait_ge(e_gu.sem, e_gu.at(u + 1))
            act.wait_ge(e_hr.sem, e_hr.at(u - 1))
            nc.scalar.activation(e_act[:, j, :], ps[:, j, 0:CHUNK], ACT.Silu).then_inc(e_sl.sem, 1)
            if not last:
                gate_up_leading(u + 2, j)
            act.wait_ge(e_hr.sem, e_hr.at(u + 1))
            act.wait_ge(e_dn.sem, e_dn.at(u - 1))
            copy(e_hhi[:, j, :], e_h[:, j, :]).then_inc(e_hh.sem, 1)
            if not (last and j == 1):
                down_leading(u + 1, 1 - j)

        def outputs_out(c):
            act.wait_ge(e_dn.sem, e_dn.at(NEX * (c + 1)))
            act.wait_ge(tail_rdy.sem, tail_rdy.at(5 * NT + TPC * c))
            for g in range(2):
                copy(e_y[:, g, :], ps[:, 4 + g, 0:CHUNK]).then_inc(e_yev.sem, 1)

        act.wait_ge(xt_rdy.sem, xt_rdy.at(6 * NT))
        for c in range(NCH):
            cols = slice(CHUNK * c, CHUNK * c + CHUNK)
            copy(e_xhi[:, :, cols], x_feat[:, :, cols]).then_inc(e_xh.sem, 1)
        gate_up_leading(0, 0)
        gate_up_leading(1, 1)
        down_leading(0, 0)
        act.wait_ge(r_mm.sem, r_mm.at(1))
        nc.scalar.activation(r_m[:].rearrange("p a b -> p (a b)"), ps[0:TILE, 4, :], ACT.Exp, scale=-1.0
                             ).then_inc(r_ex.sem, 1)
        for c in range(NCH):
            act.wait_ge(r_tr.sem, r_tr.at(c + 1))
            copy(r_wt[0:NE, CHUNK * c:CHUNK * c + CHUNK], ps[0:NE, 4 + c, 0:CHUNK]).then_inc(r_te.sem, 1)
        with act.Fori(0, NCH - 1) as c:
            with act.Fori(0, NEX // 2) as i:
                for j in range(2):
                    expert(NEX * c + 2 * i + j, j)
            outputs_out(c)
        with act.Fori(0, NEX // 2 - 1) as i:
            for j in range(2):
                expert(NEX * (NCH - 1) + 2 * i + j, j)
        for j in range(2):
            expert(NEX * NCH - 2 + j, j, last=True)
        outputs_out(NCH - 1)
        norm(6)

    @block.gpsimd
    def _(pool):
        p = nc.gpsimd
        ch = Chain(nc, "pool_chain")

        p.memset(m_pad[:, :, 0:1], 0.0).then_inc(m_padz.sem, 1)
        p.memset(m_pad[:, :, S + 1:S + 2], 0.0).then_inc(m_padz.sem, 1)
        p.memset(m_da[:, :, :, 0:1], 0.0).then_inc(m_padz.sem, 1)
        pool.wait_ge(m_dl.sem, m_dl.at(2))
        with pool.Fori(0, NS // 2) as i:
            for j in range(2):
                n = 2 * i + j
                pool.wait_ge(m_bld[j].sem, m_bld[j].at(16 * (i + 1)))
                pool.wait_ge(m_scan.sem, m_scan.at(n - 1))
                p.tensor_tensor(m_dbu[:, j, :], m_du[:], m_bb[:, j, :], ALU.mult).then_inc(m_dbu_rdy.sem, 1)
        if stages < 2:
            return

        with pool.Fori(0, H // 2) as i:
            for j in range(2):
                for c in range(NCH):
                    u, q = 8 * i + 4 * j + c, c % 2
                    pool.wait_ge(a_pr.sem, a_pr.at(u + 1))
                    pool.wait_ge(a_qq.sem, a_qq.at(u - 1))
                    p.tensor_tensor(a_rot[:, q, 0, :], a_prod[:, q, 0, :], a_prod[:, q, 1, :], ALU.subtract)
                    p.tensor_tensor(a_rot[:, q, 1, :], a_prod[:, q, 2, :], a_prod[:, q, 3, :], ALU.add
                                    ).then_inc(a_rt.sem, 1)

        def prepare(nb, nj):
            pool.wait_ge(b_ld[nj].sem, b_ld[nj].at(8 * (nb - nj) + 16))
            kv, hd = b_kv[:, nj, :, :], DC // 2
            pool.wait_ge(b_kvr_rdy.sem, b_kvr_rdy.at(nb))
            p.tensor_tensor(b_tmp[:, :, 0:hd], kv[:, :, hd:DC], b_rope[:, 1, :, 0:hd], ALU.mult).then_inc(ch.sem, ch.one())
            p.tensor_tensor(b_tmp[:, :, hd:DC], kv[:, :, 0:hd], b_rope[:, 1, :, hd:DC], ALU.mult).then_inc(ch.sem, ch.one())
            pool.wait_ge(ch.sem, ch.all())
            p.tensor_tensor(kv, kv, b_rope[:, 0, :, :], ALU.mult).then_inc(ch.sem, ch.one())
            pool.wait_ge(ch.sem, ch.all())
            if not (isinstance(nb, int) and nb == 0):
                pool.wait_ge(b_pv.sem, b_pv.at(KC * (nb - 1)))
            p.tensor_tensor(b_kvr[:, nj, :, 0:DC], kv, b_tmp[:], ALU.add).then_inc(b_kvr_rdy.sem, 1)
            p.tensor_copy(b_q[0:DC, nj, :].rearrange("p (h s) -> p h s", s=S), q_all[0:DC, :, bass.ds(S * nb, S)]
                          ).then_inc(b_q_rdy.sem, 1)

        pool.wait_ge(a_qev.sem, a_qev.at(H * NCH))
        pool.wait_ge(w_ld[1].sem, w_ld[1].at(32))
        p.memset(b_kvr[:, :, :, DC:DC + 1], 1.0).then_inc(b_one.sem, 1)
        prepare(0, 0)
        with pool.Fori(0, NSEQ // 2 - 1) as i:
            ch.enter(i, 6)
            for j in range(2):
                prepare(2 * i + j + 1, 1 - j)
            ch.leave(NSEQ // 2 - 1)
        prepare(NSEQ - 1, 1)
        if stages < 3:
            return
        if stages < 4:
            return

        pool.wait_ge(b_pv.sem, b_pv.at(NSEQ * KC))
        p.memset(n_qz[:], 0.0).then_inc(n_zero.sem, 1)
        p.memset(n_v[:], 0.0).then_inc(n_zero.sem, 1)
        pool.wait_ge(w_ld[3].sem, w_ld[3].at(12 * 16))
        pool.sem_inc(n_zero.sem, 1)

        def stationary(base, t, j, ns):
            pool.wait_ge(n_vp.sem, n_vp.at(base + t - 1))
            if ns == 2:
                p.tensor_copy(n_xf[:, j, :, :], x_feat[:, :, bass.ds(TILE * t, TILE)]).then_inc(n_xfr.sem, 1)
            else:
                p.tensor_copy(n_xf[0:DC, j, 0, :], z_ctx[:, bass.ds(TILE * t, TILE)]).then_inc(n_xfr.sem, 1)
            pool.wait_ge(n_ke.sem, n_ke.at(base + t + 1))
            pool.wait_ge(n_sc.sem, n_sc.at(base + t - 1))
            for half in range(2):
                for e in range(2):
                    ins = p.tensor_tensor(n_km[:, j, 2 * half + e, :, :],
                                          n_kf[:, j, half, S * e:S * e + S].unsqueeze(1).broadcast_to([128, 8, S]),
                                          n_hm[:].unsqueeze(2).broadcast_to([128, 8, S]), ALU.mult)
            ins.then_inc(n_kmr.sem, 1)

        def weigh(base, t, j, ns):
            pool.wait_ge(n_rr.sem, n_rr.at(base + t + 1))
            e4 = n_e[:, j, 0:2 * ns * CHUNK].rearrange("p (h k) -> p h k", k=S)
            p.tensor_tensor(e4, e4, n_r[:, j, 0:ns * H].unsqueeze(2).broadcast_to([TILE, ns * H, S]), ALU.mult
                            ).then_inc(n_p.sem, 1)

        for layer, ns in ((0, 2), (1, 1)):
            base = layer * NT
            if layer == 1 and stages < 5:
                return
            if layer == 0:
                pool.wait_ge(xt_rdy.sem, xt_rdy.at(4 * NT))
            else:
                pool.wait_ge(n_vp.sem, n_vp.at(base))
            stationary(base, 0, 0, ns)
            stationary(base, 1, 1, ns)
            weigh(base, 0, 0, ns)
            with pool.Fori(0, NT // 2 - 1) as i:
                for j in range(2):
                    stationary(base, 2 * i + j + 2, j, ns)
                    weigh(base, 2 * i + j + 1, 1 - j, ns)
            weigh(base, NT - 1, 1, ns)
        if stages < 6:
            return

        pool.wait_ge(xt_rdy.sem, xt_rdy.at(6 * NT))
        pool.wait_ge(r_mm.sem, r_mm.at(1))
        for c in range(NCH):
            pool.wait_ge(e_xh.sem, e_xh.at(c + 1))
            cols = slice(CHUNK * c, CHUNK * c + CHUNK)
            p.tensor_tensor(e_xlo[:, :, cols], x_feat[:, :, cols], e_xhi[:, :, cols].bitcast(F32), ALU.subtract
                            ).then_inc(e_xl.sem, 1)

        def gate_up_rest(u, j):
            pool.wait_ge(e_guh.sem, e_guh.at(u + 1))
            p.tensor_tensor(e_gulo[:, j, :], e_wgu[:, j, :], e_guhi[:, j, :].bitcast(F32), ALU.subtract
                            ).then_inc(e_gul.sem, 1)

        def down_rest(u, j):
            pool.wait_ge(e_dh.sem, e_dh.at(u + 1))
            p.tensor_tensor(e_dlo[:, j, :], e_wd[:, j, :], e_dhi[:, j, :].bitcast(F32), ALU.subtract
                            ).then_inc(e_dl.sem, 1)

        gate_up_rest(0, 0)
        gate_up_rest(1, 1)
        down_rest(0, 0)
        with pool.Fori(0, NEX * NCH // 2 - 1) as i:
            for j in range(2):
                gate_up_rest(2 * i + j + 2, j)
                down_rest(2 * i + j + 1, 1 - j)
        down_rest(NEX * NCH - 1, 1)

    @block.tensor
    def _(pe):
        mm = nc.tensor.matmul

        def take_waits():
            pe.sem_inc(pe_passed.sem, 1)

        def norm(k):
            if k == stages:
                return
            for t in range(NT):
                pe.wait_ge(xn_rdy.sem, xn_rdy.at(k * NT + t + 1))
                if t >= 4 or k:
                    pe.wait_ge(xt_rdy.sem, xt_rdy.at(k * NT + t - t % 2 - 2))
                for q in range(KD):
                    src = xn[:, t % 2, 128 * q:128 * q + 128] if k == 0 else x_tok[:, t, 128 * q:128 * q + 128]
                    at = TILE * (2 * q + t % 2)
                    ins = nc.tensor.transpose(ps[:, XT[t // 2 % 2], at:at + TILE], src, ident[0:TILE, 0:TILE])
                ins.then_inc(xt_mm.sem, 1)

        pe.wait_ge(c_ld.sem, c_ld.at(48))
        norm(0)

        pe.wait_ge(w_ld[0].sem, w_ld[0].at(9 * 16))
        for c in range(NCH):
            pe.wait_ge(xt_rdy.sem, xt_rdy.at(TPC * (c + 1)))
            for k in range(KD):
                ins = mm(ps[0:DI, c, 0:CHUNK], m_in[:, k, :], x_feat[:, k, CHUNK * c:CHUNK * c + CHUNK],
                         start=k == 0, stop=k == KD - 1)
            ins.then_inc(m_mm.sem, 1)
        pe.wait_ge(m_silu.sem, m_silu.at(1))
        pe.wait_ge(m_ev.sem, m_ev.at(NCH))
        for c in range(NCH):
            mm(ps[0:DTR + 2 * NS, c, 0:CHUNK], m_xp[:], m_u[:, CHUNK * c:CHUNK * c + CHUNK],
               start=True, stop=True).then_inc(m_mm.sem, 1)
        for c in range(NCH):
            pe.wait_ge(m_dbc_ev.sem, m_dbc_ev.at(c + 1))
            mm(ps[0:DI, 4 + c, 0:CHUNK], m_dt[:], m_dbc[0:DTR, CHUNK * c:CHUNK * c + CHUNK],
               start=True, stop=True).then_inc(m_mm.sem, 1)
        pe.wait_ge(m_silu.sem, m_silu.at(2))
        for c in range(NCH):
            mm(ps[0:DI, c, 0:CHUNK], ident[0:DI, 0:DI], m_ud[:, CHUNK * c:CHUNK * c + CHUNK],
               start=True, stop=False, skip_group_check=True)

        def add_state(n, j, last):
            pe.wait_ge(m_hc.sem, m_hc.at(n + 1))
            for c in range(NCH):
                ins = mm(ps[0:DI, c, 0:CHUNK], ident[0:DI, 0:DI], m_h[:, j, CHUNK * c:CHUNK * c + CHUNK],
                         start=False, stop=last, skip_group_check=True)
            ins.then_inc(m_ymm.sem, 1)

        with pe.Fori(0, NS // 2 - 1) as i:
            for j in range(2):
                add_state(2 * i + j, j, False)
        add_state(NS - 2, 0, False)
        add_state(NS - 1, 1, True)
        pe.wait_ge(m_dl.sem, m_dl.at(2))
        with pe.Fori(0, NT // 2) as i:
            for j in range(2):
                t = 2 * i + j
                pe.wait_ge(m_yev.sem, m_yev.at(t + 1))
                pe.wait_ge(tail_used.sem, tail_used.at(t - 1))
                mm(ps[0:TILE, TAIL[j], 0:D], m_y[:, j, :], m_out[:], start=True, stop=True).then_inc(tail_rdy.sem, 1)
        norm(1)
        if stages < 2:
            return

        pe.wait_ge(xt_rdy.sem, xt_rdy.at(2 * NT))
        def join(pair, j):
            pe.wait_ge(a_ld[j].sem, a_ld[j].at(96 * (pair + 1)))
            pe.wait_ge(a_wl.sem, a_wl.at(2 * pair + j))
            pe.wait_ge(a_prep_ev.sem, a_prep_ev.at(2 * pair + j))
            for k in range(KD):
                mm(ps[:, 6, DCQ * k:DCQ * k + DCQ], a_wq[:, j, 128 * k:128 * k + 128], a_wkq[:, j, :],
                   start=True, stop=True)
            for k in range(2):
                mm(ps[0:HALFQ, 7, DC * k:DC * k + DC], a_wqr[:, j, HALFQ * k:HALFQ * k + HALFQ], a_wkr[:, j, :],
                   start=True, stop=True)
            mm(ps[64 * j:64 * j + 64, 7, 256:512], a_wkv[:, j, :], a_wo[:, j, :], start=True, stop=True
               ).then_inc(a_prep.sem, 1)

        def latent(i, j, c):
            u, q = 8 * i + 4 * j + c, c % 2
            pe.wait_ge(a_wl.sem, a_wl.at(2 * i + j + 1))
            pe.wait_ge(a_xl.sem, a_xl.at(c + 1))
            pe.wait_ge(a_pr.sem, a_pr.at(u - 1))
            cols = slice(CHUNK * c, CHUNK * c + CHUNK)
            for half in range(2):
                rows = slice(HALFQ * half, HALFQ * half + HALFQ)
                parts = [(w[:, j, k, rows], x[:, k, cols]) for k in range(KD)
                         for w, x in ((a_whi, a_xhi), (a_whi, a_xlo), (a_wlo, a_xhi))]
                for n, (w, x) in enumerate(parts):
                    ins = mm(ps[0:HALFQ, 2 * q + half, 0:CHUNK], w, x, start=n == 0, stop=n == len(parts) - 1)
            ins.then_inc(a_qb.sem, 1)

        def query(i, v_):
            u, j, q = 8 * i + v_, v_ // NCH % 2, v_ % 2
            pe.wait_ge(a_rt.sem, a_rt.at(u + 1))
            pe.wait_ge(a_qev.sem, a_qev.at(u - 1))
            for half in range(2):
                ins = mm(ps[:, 4 + q, 0:CHUNK], a_w2[:, j, half, :, :].rearrange("p e d -> p (e d)"),
                         a_rot[:, q, half, :], start=half == 0, stop=half == 1)
            ins.then_inc(a_qq.sem, 1)

        def two_heads(i, first=False, last=False):
            for u in range(2 * NCH):
                latent(i, u // NCH, u % NCH)
                if u >= 2 or not first:
                    query(i, u - 2)
                if u == 1:
                    join(i, 1)
                if u == NCH + 1 and not last:
                    join(i + 1, 0)

        join(0, 0)
        two_heads(0, first=True)
        with pe.Fori(1, H // 2 - 1) as i:
            two_heads(i)
        two_heads(H // 2 - 1, last=True)
        query(H // 2 - 1, 6)
        query(H // 2 - 1, 7)

        def key_transposes(nb, nj):
            pe.wait_ge(b_kvr_rdy.sem, b_kvr_rdy.at(nb + 1))
            if not (isinstance(nb, int) and nb == 0):
                pe.wait_ge(b_row.sem, b_row.at(3 * nb))
            take_waits()
            for r in range(3):
                for q in range(4):
                    ins = nc.tensor.transpose(ps[0:DC, r, KP * q:KP * q + KP], b_kvr[:, nj, 4 * r + q, 0:DC],
                                              ident[0:KP, 0:KP])
                ins.then_inc(b_rmm.sem, 1)

        def row_scores(nb, nj, i, outputs_before, banks=(0, 1, 2)):
            pe.wait_ge(b_q_rdy.sem, b_q_rdy.at(nb + 1))
            for r in banks:
                if i == 0:
                    pe.wait_ge(b_klev.sem, b_klev.at(3 * nb + r + 1))
                elif i == 2 and r < 2 and outputs_before:
                    pe.wait_ge(b_cev.sem, b_cev.at(2 * (nb - 2) + r + 1))
                else:
                    pe.wait_ge(b_mxd.sem, b_mxd.at(24 * nb + 3 * (i - 1) + r + 1))
                mm(ps[0:TILE, r, 0:4 * KP], b_q[0:MROW, nj, TILE * i:TILE * i + TILE],
                   b_khi[0:MROW, nj, 4 * KP * r:4 * KP * r + 4 * KP], start=True, stop=True).then_inc(b_rmm.sem, 1)

        def sums_transposes(b, reduced):
            pe.wait_ge(b_oev.sem, b_oev.at(2 * (b + 1)))
            pe.wait_ge(b_mxd.sem, b_mxd.at(reduced))
            take_waits()
            for i in range(H // 2):
                ins = nc.tensor.transpose(ps[0:TILE, i // 4, (DC + 1) * (i % 4):(DC + 1) * (i % 4) + DC + 1],
                                          b_of[:, i // 4, TILE * (i % 4):TILE * (i % 4) + TILE],
                                          ident[0:DC + 1, 0:DC + 1])
            ins.then_inc(b_otr.sem, 1)

        def maxima_rows(nb, nj):
            pe.wait_ge(b_mxc.sem, b_mxc.at(nb + 1))
            for r, n in enumerate((3, 3, 2)):
                for q in range(n):
                    ins = mm(ps[0:1, r, TILE * q:TILE * q + TILE], b_mx[:, nj, 3 * r + q:3 * r + q + 1],
                             ident[0:TILE, 0:TILE], start=True, stop=True)
                ins.then_inc(b_rmm.sem, 1)

        def key_scores(b, j, c):
            for g in range(2):
                pe.wait_ge(b_exp.sem, b_exp.at(2 * KC * b + 2 * c + g - 2))
                bank = ps[0:KP, 3 + (2 * c + g) % 3, 0:CHUNK]
                mm(bank, b_khi[:, j, KP * c:KP * c + KP],
                   q_all[:, 8 * g:8 * g + 8, bass.ds(S * b, S)], start=True, stop=False)
                mm(bank, b_klo[:, j, KP * c:KP * c + KP],
                   b_q[:, j, CHUNK * g:CHUNK * g + CHUNK], start=False, stop=True).then_inc(b_st.sem, 1)

        def values(b, j, c, halves=(0, 1)):
            pe.wait_ge(b_exp.sem, b_exp.at(2 * KC * b + 2 * c + 2))
            for g in halves:
                if c == 0 and not (isinstance(b, int) and b == 0):
                    pe.wait_ge(b_oev.sem, b_oev.at(2 * b + g - 1))
                ins = mm(ps[0:DC + 1, 6 + g, 0:CHUNK], b_kvr[:, j, c, :], b_pt[:, c % 2, CHUNK * g:CHUNK * g + CHUNK],
                         start=c == 0, stop=c == KC - 1, skip_group_check=True)
            if 1 in halves:
                ins.then_inc(b_pv.sem, 1)

        def sequence(b, j, nb, first=False):
            for c in range(KC):
                if c:
                    key_scores(b, j, c)
                if c == 3 and nb is not None:
                    row_scores(nb, 1 - j, 0, not first, (2,))
                elif c == 5 and nb is not None:
                    row_scores(nb, 1 - j, 2, not first)
                if c == 4 and not first:
                    values(b, j, c - 1, (0,))
                    sums_transposes(b - 1, 24 * NSEQ if nb is None else 24 * nb + 5)
                    values(b, j, c - 1, (1,))
                elif c:
                    values(b, j, c - 1)
                if nb is None:
                    continue
                if c == 1:
                    key_transposes(nb, 1 - j)
                elif c == 2:
                    row_scores(nb, 1 - j, 0, not first, (0, 1))
                elif c == 3 or 5 <= c <= 9:
                    row_scores(nb, 1 - j, c - 2, not first)
                elif c == 10:
                    maxima_rows(nb, 1 - j)
            if nb is not None:
                pe.wait_ge(b_row.sem, b_row.at(3 * (nb + 1)))
                key_scores(nb, 1 - j, 0)
            values(b, j, KC - 1)

        pe.wait_ge(b_one.sem, b_one.at(2))
        key_transposes(0, 0)
        for i in range(8):
            row_scores(0, 0, i, False)
        maxima_rows(0, 0)
        pe.wait_ge(b_row.sem, b_row.at(3))
        key_scores(0, 0, 0)
        sequence(0, 0, 1, True)
        with pe.Fori(0, NSEQ // 2 - 1) as i:
            for j in range(2):
                sequence(2 * i + j + 1, 1 - j, 2 * i + j + 2)
        sequence(NSEQ - 1, 1, None)
        pe.wait_ge(b_cev.sem, b_cev.at(2 * (NSEQ - 1)))
        sums_transposes(NSEQ - 1, 24 * NSEQ)
        def turn_rows(t, j):
            pe.wait_ge(c_in[j].sem, c_in[j].at(8 * (t - j) + 16))
            pe.wait_ge(c_tev.sem, c_tev.at(t - 1))
            for q in range(H // 2):
                ins = nc.tensor.transpose(ps[:, 2 * j + q // 4, TILE * (q % 4):TILE * (q % 4) + TILE],
                                          c_ctx[:, j, 128 * q:128 * q + 128], ident[0:TILE, 0:TILE])
            ins.then_inc(c_tr.sem, 1)

        def project(t, j):
            pe.wait_ge(c_tev.sem, c_tev.at(t + 1))
            pe.wait_ge(tail_used.sem, tail_used.at(NT + t - 1))
            for q in range(H // 2):
                ins = mm(ps[0:TILE, TAIL[j], 0:D], c_ctxT[:, j, q, :], w3[:, q, :],
                         start=q == 0, stop=q == H // 2 - 1)
            ins.then_inc(tail_rdy.sem, 1)

        turn_rows(0, 0)
        with pe.Fori(0, NT // 2 - 1) as i:
            for j in range(2):
                turn_rows(2 * i + j + 1, 1 - j)
                project(2 * i + j, j)
        turn_rows(NT - 1, 1)
        project(NT - 2, 0)
        project(NT - 1, 1)
        norm(2)
        if stages < 3:
            return

        pe.wait_ge(xt_rdy.sem, xt_rdy.at(3 * NT))
        pe.wait_ge(w_ld[2].sem, w_ld[2].at(7 * 16))
        with pe.Fori(0, NCH) as c:
            for b in range(FB):
                q, m = b % 2, (128 if b < 5 else 64)
                pe.wait_ge(f_sl.sem, f_sl.at(FB * c + b - 1))
                pe.wait_ge(f_hr.sem, f_hr.at(FB * c + b - 1))
                if m < 128:
                    take_waits()
                for w, bank in ((f_g, q), (f_u, 2 + q)):
                    for k in range(KD):
                        ins = mm(ps[0:m, bank, 0:CHUNK], w[:, k, 128 * b:128 * b + m],
                                 x_feat[:, k, bass.ds(CHUNK * c, CHUNK)], start=k == 0, stop=k == KD - 1)
                ins.then_inc(f_gu.sem, 1)
            pe.wait_ge(f_hr.sem, f_hr.at(FB * (c + 1)))
            for s in range(TPC):
                pe.wait_ge(tail_used.sem, tail_used.at(2 * NT + TPC * c + s - 1))
                for b in range(FB):
                    m = 128 if b < 5 else 64
                    ins = mm(ps[0:TILE, TAIL[s % 2], 0:D], f_h[0:m, b, TILE * s:TILE * s + TILE], f_d[0:m, b, :],
                             start=b == 0, stop=b == FB - 1)
                ins.then_inc(tail_rdy.sem, 1)
        norm(3)
        if stages < 4:
            return

        def query_products(base, t, ns):
            pe.wait_ge(n_qe.sem, n_qe.at(base + t))
            for q in range(2 * ns):
                for k in range(KD):
                    w = n_w[:, q // 2, k, :] if ns == 2 else z_wq[:, k, :]
                    ins = mm(ps[:, 0, TILE * q:TILE * q + TILE], w[:, 128 * (q % 2):128 * (q % 2) + 128],
                             x_feat[:, k, bass.ds(TILE * t, TILE)], start=k == 0, stop=k == KD - 1)
            ins.then_inc(n_qp.sem, 1)

        def key_products(base, t, j, ns, q):
            if q == 0:
                pe.wait_ge(n_ke.sem, n_ke.at(base + t))
                if ns == 2:
                    pe.wait_ge(n_le.sem, n_le.at(t))
            if ns == 2:
                for k in range(KD):
                    mm(ps[:, 1, TILE * q:TILE * q + TILE], n_w[:, 2, k, 128 * q:128 * q + 128],
                       x_feat[:, k, bass.ds(TILE * t, TILE)], start=k == 0, stop=k == KD - 1)
                if q == 0:
                    return
                pe.wait_ge(n_xfr.sem, n_xfr.at(base + t + 1))
                for k in range(KD):
                    ins = mm(ps[0:TILE, 1, 2 * TILE:2 * TILE + H], n_xf[:, j, k, :], n_lam[:, k, :],
                             start=k == 0, stop=k == KD - 1)
            else:
                ins = mm(ps[:, 1, TILE * q:TILE * q + TILE], z_wkv[:, 128 * q:128 * q + 128],
                         z_ctx[:, bass.ds(TILE * t, TILE)], start=True, stop=True)
            if q == 1:
                ins.then_inc(n_kp.sem, 1)

        def value_products(base, t, j, ns, seqs=(0, 1)):
            pe.wait_ge(n_xfr.sem, n_xfr.at(base + t + 1))
            pe.wait_ge(n_ve.sem, n_ve.at(base + t))
            if ns == 1:
                take_waits()
            for e in seqs:
                if ns == 2:
                    for k in range(KD):
                        ins = mm(ps[0:S, 2, D * e:D * e + D], n_xf[:, j, k, S * e:S * e + S], n_w[:, 3, k, :],
                                 start=k == 0, stop=k == KD - 1)
                else:
                    ins = mm(ps[0:S, 2, D * e:D * e + D], n_xf[0:DC, j, 0, S * e:S * e + S], z_wkv[:, D:2 * D],
                             start=True, stop=True)
            if 1 in seqs:
                ins.then_inc(n_vp.sem, 1)

        def scores(base, t, j, ns):
            pe.wait_ge(n_qe.sem, n_qe.at(base + t + 1))
            pe.wait_ge(n_kmr.sem, n_kmr.at(base + t + 1))
            pe.wait_ge(n_sub.sem, n_sub.at(base + t))
            for q in range(2 * ns):
                o = ps[0:TILE, 3 + q, 0:CHUNK]
                for e in range(2):
                    mm(o, n_qz[:, j, q, e, :], n_km[:, j, 2 * (q // 2 if ns == 2 else q) + e, :, :].rearrange("p h k -> p (h k)"),
                       start=e == 0, stop=False)
                ins = mm(o, ident_bf[:], n_caus_bf[:].rearrange("p h k -> p (h k)"), start=False, stop=True)
            ins.then_inc(n_sc.sem, 1)

        def attend(layer, t, j, ahead):
            base = layer * NT
            sets = 2 - layer
            for g in range(4 * sets):
                if g == 0:
                    pe.wait_ge(n_p.sem, n_p.at(base + t + 1))
                    pe.wait_ge(n_ve.sem, n_ve.at(base + t + 1 + min(ahead, 1)))
                    take_waits()
                if g == 1:
                    pe.wait_ge(n_qe.sem, n_qe.at(base + t + 1 + ahead))
                    take_waits()
                if g >= 2:
                    if g - 2 in ACT_GROUPS[layer]:
                        pe.wait_ge(n_te.sem, n_te.at(taken(ACT_GROUPS, layer, t, g - 2)))
                    else:
                        pe.wait_ge(n_td.sem, n_td.at(taken(DVE_GROUPS, layer, t, g - 2)))
                    take_waits()
                for q in range(4):
                    ins = nc.tensor.transpose(ps[0:S, 2 - 2 * (g % 2), TILE * q:TILE * q + TILE],
                                              n_e[:, j, S * (4 * g + q):S * (4 * g + q) + S], ident[0:TILE, 0:TILE])
                ins.then_inc(n_tr.sem, 1)
                if g == 3 and ahead == 2:
                    key_products(base, t + 2, j, sets, 1)
            pe.wait_ge(n_te.sem, n_te.at(taken(ACT_GROUPS, layer, t, 8)))
            if ahead == 2:
                value_products(base, t + 2, j, sets, (0,))
            pe.wait_ge(n_td.sem, n_td.at(taken(DVE_GROUPS, layer, t, 8)))
            pe.wait_ge(n_ke.sem, n_ke.at(base + t + 1 + ahead))
            if layer == 0:
                pe.wait_ge(n_le.sem, n_le.at(t + 1 + ahead))
            pe.wait_ge(n_ye.sem, n_ye.at(base + t))
            take_waits()
            for slot in range(0, H, 2):
                r, col = 32 * ((slot // 2) % 4), 256 + TILE * (slot // 8)
                for e in range(2):
                    for o in range(2 * sets):
                        at = slot + o % 2 + H * (o // 2)
                        head = 8 * (o // 2) + at % 8 if sets == 2 else at
                        ins = mm(ps[r:r + 32, 1, col + S * e:col + S * e + S], n_v[:, j, e, head, :],
                                 n_pt[:, at // 4, TILE * (at % 4) + S * e:TILE * (at % 4) + S * e + S],
                                 start=o == 0, stop=o == 2 * sets - 1)
            ins.then_inc(n_pvm.sem, 1)
            if ahead == 2:
                value_products(base, t + 2, j, sets, (1,))
            pe.wait_ge(n_ye.sem, n_ye.at(base + t + 1))
            pe.wait_ge(tail_used.sem, tail_used.at((3 + layer) * NT + t))
            wo = n_wo if layer == 0 else z_wo
            for k in range(KD):
                ins = mm(ps[0:TILE, 7, 0:D], n_yt[:, j, k, :], wo[:, k, :], start=k == 0, stop=k == KD - 1)
            ins.then_inc(tail_rdy.sem, 1)

        pe.wait_ge(w_ld[3].sem, w_ld[3].at(12 * 16))
        pe.wait_ge(n_zero.sem, n_zero.at(3))
        pe.wait_ge(n_cst.sem, n_cst.at(2))
        for layer, ns in ((0, 2), (1, 1)):
            base = layer * NT
            if layer == 1 and stages < 5:
                return
            pe.wait_ge(xt_rdy.sem, xt_rdy.at((4 + layer) * NT))
            query_products(base, 0, ns)
            key_products(base, 0, 0, ns, 0)
            key_products(base, 0, 0, ns, 1)
            value_products(base, 0, 0, ns)
            query_products(base, 1, ns)
            key_products(base, 1, 1, ns, 0)
            key_products(base, 1, 1, ns, 1)
            scores(base, 0, 0, ns)
            value_products(base, 1, 1, ns)
            with pe.Fori(0, NT // 2 - 1) as i:
                for j in range(2):
                    t = 2 * i + j
                    scores(base, t + 1, 1 - j, ns)
                    query_products(base, t + 2, ns)
                    key_products(base, t + 2, j, ns, 0)
                    attend(layer, t, j, 2)
            scores(base, NT - 1, 1, ns)
            attend(layer, NT - 2, 0, 1)
            attend(layer, NT - 1, 1, 0)
            norm(4 + layer)
        if stages < 6:
            return

        pe.wait_ge(w_ld[5].sem, w_ld[5].at(4 * 16))
        pe.wait_ge(xt_rdy.sem, xt_rdy.at(6 * NT))
        for t in range(NT):
            for k in range(KD):
                ins = mm(ps[0:TILE, 4, NE * t:NE * t + NE], x_feat[:, k, TILE * t:TILE * t + TILE], r_w[:, k, :],
                         start=k == 0, stop=k == KD - 1)
        ins.then_inc(r_mm.sem, 1)

        def gate_up(c, e, j):
            u = NEX * c + e
            pe.wait_ge(e_gul.sem, e_gul.at(u + 1))
            pe.wait_ge(e_sl.sem, e_sl.at(u - 1))
            pe.wait_ge(e_upr.sem, e_upr.at(u - 1))
            for w in range(2):
                cols = [slice(D * w + 128 * k, D * w + 128 * k + 128) for k in range(KD)]
                parts = [(m[:, j, cols[k]], x[:, k, bass.ds(CHUNK * c, CHUNK)]) for k in range(KD)
                         for m, x in ((e_guhi, e_xhi), (e_guhi, e_xlo), (e_gulo, e_xhi))]
                for n, (m, x) in enumerate(parts):
                    ins = mm(ps[:, 2 * w + j, 0:CHUNK], m, x, start=n == 0, stop=n == len(parts) - 1)
            ins.then_inc(e_gu.sem, 1)

        def down(c, e, j, first=False, last=False):
            pe.wait_ge(e_dl.sem, e_dl.at(NEX * c + e + 1))
            pe.wait_ge(e_hh.sem, e_hh.at(NEX * c + e + 1))
            for n, (m, h) in enumerate(((e_dhi, e_hhi), (e_dlo, e_hhi), (e_dhi, e_hlo))):
                if n == 2:
                    pe.wait_ge(e_hl.sem, e_hl.at(NEX * c + e + 1))
                for g in range(2):
                    ins = mm(ps[:, 4 + g, 0:CHUNK], m[:, j, 128 * g:128 * g + 128], h[:, j, :],
                             start=first and n == 0, stop=last and n == 2, skip_group_check=True)
            ins.then_inc(e_dn.sem, 1)

        def turn_outputs(c):
            pe.wait_ge(tail_used.sem, tail_used.at(5 * NT + TPC * c))
            pe.wait_ge(e_yev.sem, e_yev.at(2 * (c + 1)))
            for s in range(TPC):
                for g in range(2):
                    ins = nc.tensor.transpose(ps[0:TILE, 6 + s // 2, D * (s % 2) + 128 * g:D * (s % 2) + 128 * g + 128],
                                              e_y[:, g, TILE * s:TILE * s + TILE], ident[:])
                if s % 2:
                    ins.then_inc(tail_rdy.sem, 2)

        pe.wait_ge(e_xl.sem, e_xl.at(1))
        gate_up(0, 0, 0)
        gate_up(0, 1, 1)
        pe.wait_ge(r_sel.sem, r_sel.at(1))
        for c in range(NCH):
            for s in range(TPC):
                ins = nc.tensor.transpose(ps[0:NE, 4 + c, TILE * s:TILE * s + TILE], r_m2[:, TPC * c + s, :],
                                          ident[0:TILE, 0:TILE])
            ins.then_inc(r_tr.sem, 1)

        def chunk(c, last):
            down(c, 0, 0, first=True)
            gate_up(c, 2, 0)
            with pe.Fori(0, NEX // 4 - 1) as i:
                for e in range(1, 5):
                    down(c, 4 * i + e, e % 2)
                    gate_up(c, 4 * i + e + 2, e % 2)
            for e in range(NEX - 5, NEX - 1):
                down(c, e, e % 2)
                if e + 2 < NEX:
                    gate_up(c, e + 2, e % 2)
            if not last:
                gate_up(c + 1, 0, 0)
            down(c, NEX - 1, 1, last=True)
            if not last:
                gate_up(c + 1, 1, 1)
            turn_outputs(c)

        pe.wait_ge(r_te.sem, r_te.at(NCH))
        pe.wait_ge(e_xl.sem, e_xl.at(NCH))
        with pe.Fori(0, NCH - 1) as c:
            chunk(c, False)
        chunk(NCH - 1, True)
        norm(6)

    stack.close()


def _rope(length, dim):
    inv = (1.0 / np.float32(10000.0) ** (np.arange(0, dim, 2, dtype=np.float32) / np.float32(dim))).astype(np.float32)
    f = np.arange(length, dtype=np.float32)[:, None] * inv[None, :]
    return np.repeat(np.sin(f), 2, axis=-1), np.repeat(np.cos(f), 2, axis=-1)


def _tables():
    sq, cq = _rope(S, DCQ)
    ropeq = np.stack([cq[:, :HALFQ].T, sq[:, :HALFQ].T, cq[:, HALFQ:].T, sq[:, HALFQ:].T], axis=1)
    sk, ck = _rope(LK, DC)
    signed = np.concatenate([-sk[:, :DC // 2], sk[:, DC // 2:]], axis=-1)
    ropek = np.stack([ck.reshape(KP, KC, DC), signed.reshape(KP, KC, DC)], axis=1)
    q = np.arange(TILE)[:, None] % S
    return {"c_ident": np.eye(128, dtype=np.float32),
            "c_ropeq": ropeq, "c_ropek": ropek,
            "c_headmask": (np.arange(128)[:, None] // HD == np.arange(8)[None, :]).astype(np.float32),
            "c_causal": np.where(np.arange(S)[None, :] <= q, 0.0, NEG).astype(np.float32),
            "c_lower": (np.arange(NG)[None, :] < np.arange(NG)[:, None]).astype(np.float32),
            "c_ones": np.ones((NEX - NE, T), np.float32)}


def kernel(**inputs):
    import concourse.bacc as bacc
    from concourse.bass_utils import run_bass_kernel_spmd

    g = {k: np.asarray(v) for k, v in inputs.items()}
    m, z, f = (lambda n: g["L0_attn_" + n]), (lambda n: g["L0_xattn_" + n]), (lambda n: g["L0_ffn_" + n])
    n, y, e = (lambda k: g["L1_attn_" + k]), (lambda k: g["L1_xattn_" + k]), (lambda k: g["L1_ffn_" + k])
    split = lambda w: w.reshape(w.shape[0], KD, 128, -1).transpose(0, 2, 1, 3).reshape(w.shape[0], 128, -1)
    shared = lambda w: w.reshape(D, 2, IE).transpose(1, 0, 2)
    order = np.r_[0:H:2, 1:H:2]
    even_first = lambda w: w.reshape(D, H, HD)[:, order].reshape(D, D)
    blocks = lambda w: np.pad(w, (0, FB * 128 - INTER)).reshape(FB, 128).T
    gates = split(np.concatenate([e("w_gate"), shared(e("sw_gate"))]))
    ups = split(np.concatenate([e("w_up"), shared(e("sw_up"))]))
    downs = np.concatenate([e("w_down"), e("sw_down").reshape(2, IE, D)])
    laid = {
        "x": g["x"].reshape(T, D), "ctx": g["ctx_512"],
        "ctx_head_T": g["ctx_512"][:, :S].transpose(2, 0, 1).reshape(DC, T),
        "ln_w": m("ln_w").reshape(KD, 128).T, "ln_b": m("ln_b").reshape(KD, 128).T,
        "in_proj_T": m("in_proj_W").T, "conv_w": m("conv_w")[:, 0, :], "conv_b": m("conv_b")[:, None],
        "x_proj_T": m("x_proj_W").T, "dt_proj_T": m("dt_proj_W").T, "dt_proj_b": m("dt_proj_b")[:, None],
        "A_log": m("A_log"), "D_param": m("D_param")[:, None], "out_proj_T": m("out_proj_W").T,
        "Wq": z("Wq").reshape(H, 128, D), "w_kc_q": z("w_kc_q"), "W_qr_T": z("W_qr").transpose(0, 2, 1),
        "W_kr_T": z("W_kr").transpose(0, 2, 1), "w_kc_kv": z("w_kc_kv"), "Wo_T": z("Wo").T.reshape(H, 128, D),
        "gate_T": f("gate_w").T, "up_T": f("up_w").T, "down_T": f("down_w").T,
        "gate_s": blocks(f("gate_s")), "up_s": blocks(f("up_s")), "down_s": f("down_s"),
        "N_Wq1": even_first(n("Wq1")), "N_Wq2": even_first(n("Wq2")), "N_Wk": n("Wk"), "N_Wv": n("Wv"),
        "N_Wlam": n("Wlam")[:, order], "N_Wo": even_first(n("Wo").T).T,
        "Z_Wq_T": y("Wq").T, "Z_Wkv_T": y("Wkv_expand").T, "Z_Wout_T": y("Wout").T,
        "router_w": e("router_w"), "router_bias": e("router_bias"),
        "W_exp": np.concatenate([gates, ups, downs], axis=2),
    }
    laid.update(_tables())
    nc = bacc.Bacc("TRN2", target_bir_lowering=False, num_devices=1)
    arrays, aps = {}, {}
    for name, arr in laid.items():
        arr = np.ascontiguousarray(arr)
        arrays["in_" + name] = arr
        aps[name] = nc.dram_tensor("in_" + name, arr.shape, mybir.dt.from_np(arr.dtype), kind="ExternalInput").ap()
    out = nc.dram_tensor("out_x", (T, D), F32, kind="ExternalOutput").ap()
    build(nc, aps, out)
    r = run_bass_kernel_spmd(nc, [arrays], core_ids=[0])
    return r.results[0]["out_x"].reshape(NSEQ, S, D)
```
